# Optimizing a Trainium2 kernel written in Bass

```python
import numpy as np
import jax
import jax.numpy as jnp

def _softmax(x, axis=-1):
    return jax.nn.softmax(x, axis=axis)

def _gelu(x):
    return jax.nn.gelu(x, approximate=True)

def _silu(x):
    return jax.nn.silu(x)

def _sigmoid(x):
    return jax.nn.sigmoid(x)

def _layernorm(x, axis=-1, eps=1e-05):
    m = jnp.mean(x, axis=axis, keepdims=True)
    v = jnp.var(x, axis=axis, keepdims=True)
    return (x - m) / jnp.sqrt(v + eps)

def _scatter_add(tgt, idx, src, axis=0):
    return tgt.at[idx].add(src)

def _segment_sum(src, seg, n):
    return jax.ops.segment_sum(src, seg, n)
kernel_name = 'mk_gps_d2_gnn_r32_f95854'

def setup_inputs(seed: int=0):
    np.random.seed(seed)
    _w = jnp.asarray

    def _rec_inputs():
        import jax
        import jax.numpy as jnp
        _gk = jax.random.key(seed)
        x = -0.0002117 + 1 * jax.random.normal(jax.random.fold_in(_gk, 1), (3125, 256), jnp.float32)
        src = jax.random.randint(jax.random.fold_in(_gk, 2), (50000,), 0, 3125, jnp.int32)
        dst = jnp.minimum((3125 * jax.random.uniform(jax.random.fold_in(_gk, 3), (50000,)) ** 2.0).astype(jnp.int32), 99999)
        _o = jnp.argsort(dst, stable=True)
        src = src[_o]
        dst = dst[_o]
        edge_attr_64 = 5.96457e-05 + 0.999887 * jax.random.normal(jax.random.fold_in(_gk, 12), (50000, 64), jnp.float32)
        edge_weight = jax.random.uniform(jax.random.fold_in(_gk, 13), (50000,), jnp.float32, 0.0, 1)
        node_vec1 = jax.random.uniform(jax.random.fold_in(_gk, 14), (3125, 1), jnp.float32, 0.0, 0.999943)
        return (x, src, dst, edge_attr_64, edge_weight, node_vec1)
    x, src, dst, edge_attr_64, edge_weight, node_vec1 = _rec_inputs()

    def _L0_gnn_setup():
        import jax, jax.numpy as jnp
        import numpy as np
        N = 3125
        E = 100000
        IN = 256
        OUT = 256
        BN_EPS = 1e-05

        def _hamilton(w):
            r, i, j, k = jnp.split(w, 4, axis=1)
            h0 = jnp.concatenate([r, -i, -j, -k], axis=0)
            h1 = jnp.concatenate([i, r, -k, j], axis=0)
            h2 = jnp.concatenate([j, k, r, -i], axis=0)
            h3 = jnp.concatenate([k, -j, i, r], axis=0)
            return jnp.concatenate([h0, h1, h2, h3], axis=1)
        key = jax.random.key(seed)
        k0, k1, k2, k3, k4 = jax.random.split(key, 5)
        x = jax.random.normal(k0, (N, IN), dtype=jnp.float32)
        edge_row = jax.random.randint(k1, (E,), 0, N)
        edge_col = jax.random.randint(k2, (E,), 0, N)
        edge_weight = jax.random.uniform(k3, (E,), dtype=jnp.float32)
        stdv = float(np.sqrt(6.0 / (IN // 4 + OUT)))
        weight = jax.random.uniform(k4, (IN // 4, OUT), dtype=jnp.float32, minval=-stdv, maxval=stdv)
        gamma = jnp.ones((OUT,), dtype=jnp.float32)
        beta = jnp.zeros((OUT,), dtype=jnp.float32)
        return {'x': x, 'edge_row': edge_row, 'edge_col': edge_col, 'edge_weight': edge_weight, 'weight': weight, 'gamma': gamma, 'beta': beta}
    _L0_gnn_all = _L0_gnn_setup()
    _L0_gnn_in = {k: v for k, v in _L0_gnn_all.items() if k in ('weight', 'gamma', 'beta')}
    del _L0_gnn_all

    def _L0_mix_setup():
        import jax, jax.numpy as jnp
        import numpy as np
        NHEAD = 8
        ATT_EPS = 1e-06
        LN_EPS = 1e-05

        def _layernorm(x, g, b):
            mu = jnp.mean(x, axis=-1, keepdims=True)
            var = jnp.mean(jnp.square(x - mu), axis=-1, keepdims=True)
            return (x - mu) * jax.lax.rsqrt(var + LN_EPS) * g + b
        key = jax.random.key(seed)
        ks = jax.random.split(key, 7)
        N, L, C = (4, 512, 256)
        s = 1.0 / np.sqrt(C)
        return {'x': jax.random.normal(ks[0], (N, L, C), jnp.float32), 'Wq': jax.random.normal(ks[1], (C, C), jnp.float32) * s, 'Wk': jax.random.normal(ks[2], (C, C), jnp.float32) * s, 'Wv': jax.random.normal(ks[3], (C, C), jnp.float32) * s, 'Wm': jax.random.normal(ks[4], (C, C), jnp.float32) * s, 'W1': jax.random.normal(ks[5], (2 * C, 2 * C), jnp.float32) * (1.0 / np.sqrt(2 * C)), 'W2': jax.random.normal(ks[6], (2 * C, C), jnp.float32) * (1.0 / np.sqrt(2 * C)), 'g1': jnp.ones((C,), jnp.float32), 'b1': jnp.zeros((C,), jnp.float32), 'g2': jnp.ones((C,), jnp.float32), 'b2': jnp.zeros((C,), jnp.float32)}
    _L0_mix_all = _L0_mix_setup()
    _L0_mix_in = {k: v for k, v in _L0_mix_all.items() if k in ('Wq', 'Wk', 'Wv', 'Wm', 'W1', 'W2', 'g1', 'b1', 'g2', 'b2')}
    del _L0_mix_all

    def _L0_ffn_setup():
        import math
        import jax, jax.numpy as jnp
        import numpy as np
        CAPACITY_FACTOR = 1.25
        key = jax.random.key(seed)
        ks = jax.random.split(key, 5)
        B, L, D, F, E = (8, 256, 256, 1024, 8)
        h = jax.random.normal(ks[0], (B, L, D), dtype=jnp.float32)
        gate_w = jax.random.normal(ks[1], (D, E), dtype=jnp.float32) * 0.02
        gate_b = jnp.zeros((E,), dtype=jnp.float32)
        w1 = jax.random.normal(ks[2], (E, D, F), dtype=jnp.float32) * (1.0 / math.sqrt(D))
        b1 = jnp.zeros((E, F), dtype=jnp.float32)
        w2 = jax.random.normal(ks[3], (E, F, D), dtype=jnp.float32) * (1.0 / math.sqrt(F))
        b2 = jnp.zeros((E, D), dtype=jnp.float32)
        return {'h': h, 'gate_w': gate_w, 'gate_b': gate_b, 'w1': w1, 'b1': b1, 'w2': w2, 'b2': b2}
    _L0_ffn_all = _L0_ffn_setup()
    _L0_ffn_in = {k: v for k, v in _L0_ffn_all.items() if k in ('gate_w', 'gate_b', 'w1', 'b1', 'w2', 'b2')}
    del _L0_ffn_all

    def _L1_gnn_setup():
        import jax, jax.numpy as jnp
        import numpy as np
        N_NODES = 10000
        N_EDGES = 5000
        IN_FEATS = 256
        E_DIMS = 64
        NEG_SLOPE = 0.01
        key = jax.random.key(seed)
        ks = jax.random.split(key, 8)
        h = jax.random.normal(ks[0], (N_NODES, IN_FEATS), dtype=jnp.float32)
        w = jax.random.normal(ks[1], (N_EDGES, E_DIMS), dtype=jnp.float32)
        snorm_n = jax.random.uniform(ks[2], (N_NODES, 1), dtype=jnp.float32)
        edge_src = jax.random.randint(ks[3], (N_EDGES,), 0, N_NODES, dtype=jnp.int64)
        edge_dst = jax.random.randint(ks[4], (N_EDGES,), 0, N_NODES, dtype=jnp.int64)
        W_self = jax.random.normal(ks[5], (IN_FEATS, IN_FEATS), dtype=jnp.float32) * np.sqrt(2.0 / IN_FEATS)
        W_func = jax.random.normal(ks[6], (IN_FEATS, IN_FEATS), dtype=jnp.float32) * np.sqrt(2.0 / IN_FEATS)
        W_att = jax.random.normal(ks[7], (1, 2 * IN_FEATS + E_DIMS), dtype=jnp.float32) * np.sqrt(2.0 / (2 * IN_FEATS + E_DIMS))
        return {'h': h, 'w': w, 'snorm_n': snorm_n, 'edge_src': edge_src, 'edge_dst': edge_dst, 'W_self': W_self, 'W_func': W_func, 'W_att': W_att}
    _L1_gnn_all = _L1_gnn_setup()
    _L1_gnn_in = {k: v for k, v in _L1_gnn_all.items() if k in ('W_self', 'W_func', 'W_att')}
    del _L1_gnn_all

    def _L1_mix_setup():
        import jax, jax.numpy as jnp
        import numpy as np
        HEADS = 8
        DIM_HEAD = 64
        EPS = 1e-05

        def _inst_norm_lastdim(t):
            mu = jnp.mean(t, axis=-1, keepdims=True)
            var = jnp.mean(jnp.square(t - mu), axis=-1, keepdims=True)
            return (t - mu) * jax.lax.rsqrt(var + EPS)
        key = jax.random.key(seed)
        k1, k2, k3, k4 = jax.random.split(key, 4)
        b, n, dim = (4, 256, 256)
        inner = HEADS * DIM_HEAD
        x = jax.random.normal(k1, (b, n, dim), dtype=jnp.float32)
        Wqkv = jax.random.normal(k2, (3 * inner, dim), dtype=jnp.float32) * (1.0 / np.sqrt(dim))
        Wout = jax.random.normal(k3, (dim, inner), dtype=jnp.float32) * (1.0 / np.sqrt(inner))
        bout = jax.random.normal(k4, (dim,), dtype=jnp.float32) * 0.01
        return {'x': x, 'Wqkv': Wqkv, 'Wout': Wout, 'bout': bout}
    _L1_mix_all = _L1_mix_setup()
    _L1_mix_in = {k: v for k, v in _L1_mix_all.items() if k in ('Wqkv', 'Wout', 'bout')}
    del _L1_mix_all

    def _L1_ffn_setup():
        import jax, jax.numpy as jnp
        import numpy as np
        B, S, H, F, E, K = (8, 128, 256, 512, 16, 2)
        EPS = 1e-05
        key = jax.random.key(seed)
        ks = jax.random.split(key, 9)
        sc = 0.02
        return {'x': jax.random.normal(ks[0], (B, S, H), dtype=jnp.float32), 'gate_w': jax.random.normal(ks[1], (H, E), dtype=jnp.float32) * sc, 'gate_b': jnp.zeros((E,), dtype=jnp.float32), 'w1': jax.random.normal(ks[2], (E, H, F), dtype=jnp.float32) * sc, 'b1': jnp.zeros((E, F), dtype=jnp.float32), 'w2': jax.random.normal(ks[3], (E, F, H), dtype=jnp.float32) * sc, 'b2': jnp.zeros((E, H), dtype=jnp.float32), 'gamma': jnp.ones((H,), dtype=jnp.float32), 'beta': jnp.zeros((H,), dtype=jnp.float32)}
    _L1_ffn_all = _L1_ffn_setup()
    _L1_ffn_in = {k: v for k, v in _L1_ffn_all.items() if k in ('gate_w', 'gate_b', 'w1', 'b1', 'w2', 'b2', 'gamma', 'beta')}
    del _L1_ffn_all
    return {'x': x, 'src': src, 'dst': dst, 'edge_attr_64': edge_attr_64, 'edge_weight': edge_weight, 'node_vec1': node_vec1, 'L0_gnn_weight': _L0_gnn_in['weight'], 'L0_gnn_gamma': _L0_gnn_in['gamma'], 'L0_gnn_beta': _L0_gnn_in['beta'], 'L0_mix_Wq': _L0_mix_in['Wq'], 'L0_mix_Wk': _L0_mix_in['Wk'], 'L0_mix_Wv': _L0_mix_in['Wv'], 'L0_mix_Wm': _L0_mix_in['Wm'], 'L0_mix_W1': _L0_mix_in['W1'], 'L0_mix_W2': _L0_mix_in['W2'], 'L0_mix_g1': _L0_mix_in['g1'], 'L0_mix_b1': _L0_mix_in['b1'], 'L0_mix_g2': _L0_mix_in['g2'], 'L0_mix_b2': _L0_mix_in['b2'], 'L0_ffn_gate_w': _L0_ffn_in['gate_w'], 'L0_ffn_gate_b': _L0_ffn_in['gate_b'], 'L0_ffn_w1': _L0_ffn_in['w1'], 'L0_ffn_b1': _L0_ffn_in['b1'], 'L0_ffn_w2': _L0_ffn_in['w2'], 'L0_ffn_b2': _L0_ffn_in['b2'], 'L1_gnn_W_self': _L1_gnn_in['W_self'], 'L1_gnn_W_func': _L1_gnn_in['W_func'], 'L1_gnn_W_att': _L1_gnn_in['W_att'], 'L1_mix_Wqkv': _L1_mix_in['Wqkv'], 'L1_mix_Wout': _L1_mix_in['Wout'], 'L1_mix_bout': _L1_mix_in['bout'], 'L1_ffn_gate_w': _L1_ffn_in['gate_w'], 'L1_ffn_gate_b': _L1_ffn_in['gate_b'], 'L1_ffn_w1': _L1_ffn_in['w1'], 'L1_ffn_b1': _L1_ffn_in['b1'], 'L1_ffn_w2': _L1_ffn_in['w2'], 'L1_ffn_b2': _L1_ffn_in['b2'], 'L1_ffn_gamma': _L1_ffn_in['gamma'], 'L1_ffn_beta': _L1_ffn_in['beta']}

def reference(x, src, dst, edge_attr_64, edge_weight, node_vec1, L0_gnn_weight, L0_gnn_gamma, L0_gnn_beta, L0_mix_Wq, L0_mix_Wk, L0_mix_Wv, L0_mix_Wm, L0_mix_W1, L0_mix_W2, L0_mix_g1, L0_mix_b1, L0_mix_g2, L0_mix_b2, L0_ffn_gate_w, L0_ffn_gate_b, L0_ffn_w1, L0_ffn_b1, L0_ffn_w2, L0_ffn_b2, L1_gnn_W_self, L1_gnn_W_func, L1_gnn_W_att, L1_mix_Wqkv, L1_mix_Wout, L1_mix_bout, L1_ffn_gate_w, L1_ffn_gate_b, L1_ffn_w1, L1_ffn_b1, L1_ffn_w2, L1_ffn_b2, L1_ffn_gamma, L1_ffn_beta):
    import jax
    import jax.numpy as jnp

    def _L0_gnn_ref(x, edge_row, edge_col, edge_weight, weight, gamma, beta):
        import jax, jax.numpy as jnp
        import numpy as np
        N = 3125
        E = 100000
        IN = 256
        OUT = 256
        BN_EPS = 1e-05

        def _hamilton(w):
            r, i, j, k = jnp.split(w, 4, axis=1)
            h0 = jnp.concatenate([r, -i, -j, -k], axis=0)
            h1 = jnp.concatenate([i, r, -k, j], axis=0)
            h2 = jnp.concatenate([j, k, r, -i], axis=0)
            h3 = jnp.concatenate([k, -j, i, r], axis=0)
            return jnp.concatenate([h0, h1, h2, h3], axis=1)
        n = x.shape[0]
        support = x @ _hamilton(weight)
        msgs = edge_weight[:, None] * support[edge_col]
        agg = jax.ops.segment_sum(msgs, edge_row, num_segments=n)
        mean = jnp.mean(agg, axis=0)
        var = jnp.mean(jnp.square(agg - mean), axis=0)
        y = (agg - mean) * jax.lax.rsqrt(var + BN_EPS) * gamma + beta
        return jnp.tanh(y)

    def _L0_mix_ref(x, Wq, Wk, Wv, Wm, W1, W2, g1, b1, g2, b2):
        import jax, jax.numpy as jnp
        import numpy as np
        NHEAD = 8
        ATT_EPS = 1e-06
        LN_EPS = 1e-05

        def _layernorm(x, g, b):
            mu = jnp.mean(x, axis=-1, keepdims=True)
            var = jnp.mean(jnp.square(x - mu), axis=-1, keepdims=True)
            return (x - mu) * jax.lax.rsqrt(var + LN_EPS) * g + b
        N, L, C = x.shape
        H = NHEAD
        D = C // H
        q = (x @ Wq).reshape(N, L, H, D)
        k = (x @ Wk).reshape(N, L, H, D)
        v = (x @ Wv).reshape(N, L, H, D)
        Q = jax.nn.elu(q) + 1.0
        K = jax.nn.elu(k) + 1.0
        v = v / L
        KV = jnp.einsum('nshd,nshv->nhdv', K, v)
        Z = 1.0 / (jnp.einsum('nlhd,nhd->nlh', Q, K.sum(axis=1)) + ATT_EPS)
        msg = jnp.einsum('nlhd,nhdv,nlh->nlhv', Q, KV, Z) * L
        msg = msg.reshape(N, L, C) @ Wm
        msg = _layernorm(msg, g1, b1)
        h = jnp.concatenate([x, msg], axis=-1) @ W1
        h = jax.nn.relu(h) @ W2
        msg = _layernorm(h, g2, b2)
        return x + msg

    def _L0_ffn_ref(h, gate_w, gate_b, w1, b1, w2, b2):
        import math
        import jax, jax.numpy as jnp
        import numpy as np
        CAPACITY_FACTOR = 1.25
        B, L, D = h.shape
        E = gate_w.shape[1]
        T = B * L
        C = max(1, math.ceil(CAPACITY_FACTOR * T / E))
        x = h.reshape(T, D)
        logits = x @ gate_w + gate_b
        probs = jax.nn.softmax(logits, axis=-1)
        idx = jnp.argmax(probs, axis=-1)
        prb = jnp.take_along_axis(probs, idx[:, None], axis=1)[:, 0]
        one_hot = jax.nn.one_hot(idx, E, dtype=jnp.float32)
        pos = (jnp.cumsum(one_hot, axis=0) * one_hot).sum(-1).astype(jnp.int32) - 1
        kept = pos < C
        pos_safe = jnp.where(kept, pos, C)
        buf = jnp.zeros((E, C, D), dtype=h.dtype).at[idx, pos_safe].set(x, mode='drop')
        hmid = jax.nn.relu(jnp.einsum('ecd,edf->ecf', buf, w1) + b1[:, None, :])
        ybuf = jnp.einsum('ecf,efd->ecd', hmid, w2) + b2[:, None, :]
        pos_g = jnp.minimum(pos, C - 1)
        y_tok = ybuf[idx, pos_g] * (prb * kept)[:, None]
        y = y_tok.reshape(B, L, D)
        y = jnp.nan_to_num(y, nan=0.0, posinf=10000.0, neginf=-10000.0)
        return y

    def _L1_gnn_ref(h, w, snorm_n, edge_src, edge_dst, W_self, W_func, W_att):
        import jax, jax.numpy as jnp
        import numpy as np
        N_NODES = 10000
        N_EDGES = 5000
        IN_FEATS = 256
        E_DIMS = 64
        NEG_SLOPE = 0.01
        N = h.shape[0]
        h_s = h @ W_self.T
        z = h @ W_func.T
        concat_z = jnp.concatenate([z[edge_src], z[edge_dst], w], axis=-1)
        e = jax.nn.leaky_relu(concat_z @ W_att.T, negative_slope=NEG_SLOPE)[:, 0]
        m = jax.ops.segment_max(e, edge_dst, num_segments=N)
        e_exp = jnp.exp(e - m[edge_dst])
        denom = jax.ops.segment_sum(e_exp, edge_dst, num_segments=N)
        alpha = e_exp / denom[edge_dst]
        agg = jax.ops.segment_sum(alpha[:, None] * z[edge_src], edge_dst, num_segments=N)
        h_new = h_s + agg
        deg = jax.ops.segment_sum(jnp.ones_like(e), edge_dst, num_segments=N)
        h_new = jnp.where(deg[:, None] > 0, h_new, h)
        h_new = jax.nn.relu(h_new)
        return h + h_new

    def _L1_mix_ref(x, Wqkv, Wout, bout):
        import jax, jax.numpy as jnp
        import numpy as np
        HEADS = 8
        DIM_HEAD = 64
        EPS = 1e-05

        def _inst_norm_lastdim(t):
            mu = jnp.mean(t, axis=-1, keepdims=True)
            var = jnp.mean(jnp.square(t - mu), axis=-1, keepdims=True)
            return (t - mu) * jax.lax.rsqrt(var + EPS)
        b, n, dim = x.shape
        qkv = jnp.einsum('bnc,fc->bnf', x, Wqkv)
        q, k, v = jnp.split(qkv, 3, axis=-1)

        def to_heads(t):
            return t.reshape(b, n, HEADS, DIM_HEAD).transpose(0, 2, 1, 3)
        q, k, v = (to_heads(q), to_heads(k), to_heads(v))
        k = _inst_norm_lastdim(k)
        v = _inst_norm_lastdim(v)
        dots = jnp.einsum('bhnd,bhne->bhde', k, v)
        out = jnp.einsum('bhnd,bhde->bhne', q, dots) / n
        out = out.transpose(0, 2, 1, 3).reshape(b, n, HEADS * DIM_HEAD)
        return jnp.einsum('bnf,cf->bnc', out, Wout) + bout

    def _L1_ffn_ref(x, gate_w, gate_b, w1, b1, w2, b2, gamma, beta):
        import jax, jax.numpy as jnp
        import numpy as np
        B, S, H, F, E, K = (8, 128, 256, 512, 16, 2)
        EPS = 1e-05
        gate_logits = x @ gate_w + gate_b
        topk_vals, topk_idx = jax.lax.top_k(gate_logits, K)
        topk_w = jax.nn.softmax(topk_vals, axis=-1)
        h = jax.nn.relu(jnp.einsum('bsh,ehf->bsef', x, w1) + b1)
        expert_out = jnp.einsum('bsef,efh->bseh', h, w2) + b2
        sel = jnp.take_along_axis(expert_out, topk_idx[:, :, :, None], axis=2)
        moe = jnp.sum(topk_w[..., None] * sel, axis=2)
        y = x + moe
        mu = jnp.mean(y, axis=-1, keepdims=True)
        var = jnp.var(y, axis=-1, keepdims=True)
        return (y - mu) / jnp.sqrt(var + EPS) * gamma + beta
    xn = _layernorm(x, axis=-1)
    x = x + _L0_gnn_ref(xn, src, dst, edge_weight, L0_gnn_weight, L0_gnn_gamma, L0_gnn_beta) + _L0_mix_ref(xn[None], L0_mix_Wq, L0_mix_Wk, L0_mix_Wv, L0_mix_Wm, L0_mix_W1, L0_mix_W2, L0_mix_g1, L0_mix_b1, L0_mix_g2, L0_mix_b2)[0]
    x = x + _L0_ffn_ref(_layernorm(x, axis=-1)[None], L0_ffn_gate_w, L0_ffn_gate_b, L0_ffn_w1, L0_ffn_b1, L0_ffn_w2, L0_ffn_b2)[0]
    xn = _layernorm(x, axis=-1)
    x = x + _L1_gnn_ref(xn, edge_attr_64, node_vec1, src, dst, L1_gnn_W_self, L1_gnn_W_func, L1_gnn_W_att) + _L1_mix_ref(xn[None], L1_mix_Wqkv, L1_mix_Wout, L1_mix_bout)[0]
    x = x + _L1_ffn_ref(_layernorm(x, axis=-1)[None], L1_ffn_gate_w, L1_ffn_gate_b, L1_ffn_w1, L1_ffn_b1, L1_ffn_w2, L1_ffn_b2, L1_ffn_gamma, L1_ffn_beta)[0]
    return x

_drawn_inputs = setup_inputs


def setup_inputs(seed=0):
    import zlib

    import numpy as np

    out = dict(_drawn_inputs(seed))
    spreads = {'L0_gnn_gamma': (1.0, 0.2),
     'L0_gnn_beta': (0.0, 0.1),
     'L0_mix_g1': (1.0, 0.2),
     'L0_mix_b1': (0.0, 0.1),
     'L0_mix_g2': (1.0, 0.2),
     'L0_mix_b2': (0.0, 0.1),
     'L0_ffn_gate_b': (0.0, 0.1),
     'L0_ffn_b1': (0.0, 0.8),
     'L0_ffn_b2': (0.0, 0.8),
     'L1_ffn_gate_b': (0.0, 0.62),
     'L1_ffn_b1': (0.0, 0.8),
     'L1_ffn_b2': (0.0, 0.515),
     'L1_ffn_gamma': (1.0, 0.2),
     'L1_ffn_beta': (0.0, 0.395)}
    factors = {'L1_mix_bout': 8.0, 'L1_ffn_gate_w': 2.707, 'L1_ffn_w1': 4.295, 'L1_ffn_w2': 3.425}
    for name, (base, spread) in spreads.items():
        noise = np.random.default_rng([zlib.crc32(name.encode()), seed]).standard_normal(out[name].shape)
        drawn = base * np.exp(spread * noise) if base else spread * noise
        out[name] = jnp.asarray(drawn.astype(out[name].dtype))
    for name, factor in factors.items():
        out[name] = (out[name] * factor).astype(out[name].dtype)
    return out
```

```python
from contextlib import ExitStack

import concourse.bass as bass
from concourse import mybir

ALU = mybir.AluOpType
ACT = mybir.ActivationFunctionType
F32 = mybir.dt.float32
BF16 = mybir.dt.bfloat16
I32 = mybir.dt.int32
AX_X = mybir.AxisListType.X
ds = bass.ds

N, D = 3125, 256
NT = 25
R = N // NT
E = 50000
EC = E // R
HID = 512
EDIM = 64
U5 = 5
EPS = 1e-5
BIG = 1e30
LOWEST = -1e20
TOKS = ((0, 2), (2, 3))

GT0, GT1 = 1, 2
EU = 8


def slots(count, blocks, gt):
    size = 128 * gt
    return (count + blocks * (size - 1)) // size


G0 = -(-slots(E, NT, GT0) // EU) * EU
G1 = -(-slots(E, NT, GT1) * GT1 // EU) * EU // GT1
T0, T1 = G0 * GT0, G1 * GT1
ROW1 = D + 2

X0, F0, K0 = 8, 1024, 1
X1, F1, K1 = 16, 512, 2
CAP = -(-5 * N // (4 * X0))
M0, M1 = slots(N * K0, X0, 1), slots(N * K1, X1, 1)
MAXG = max(G0, G1, T0, T1, 128)
CE = EC // EU


def even(n):
    return n + n % 2


M0, M1 = even(M0), even(M1)


def done(i, u, per=U5):
    return i * per + (u + 1 + per)


def freed(i, u, bufs, per=U5):
    before = u - bufs if u >= bufs else max(w for w in range(per) if w % bufs == u % bufs) - per
    return i * per + (before + 1 + per)


def landed(turns):
    return 16 * (turns + 1)


def gathered(turns):
    return 16 * turns


def gps_kernel(nc, A, out):
    ctx = ExitStack()
    with ctx:
        def sb(name, shape, dt=F32):
            return ctx.enter_context(nc.sbuf_tensor(name, shape, dt))

        def sem(name):
            return ctx.enter_context(nc.semaphore(name))

        X = sb("X", [R, NT, D])
        AGG = sb("AGG", [R, NT, D])
        XN = sb("XN", [R, NT, D])
        xnT = sb("xnT", [128, 2, N])
        WD = sb("WD", [128, 5636])
        SCR = sb("SCR", [128, 12320])
        iota = sb("iota", [128, MAXG])
        ident = sb("ident", [128, 128])
        identb = sb("identb", [128, 128], BF16)
        ones = sb("ones", [128, 128])
        tri = sb("tri", [128, 128])
        zeros = sb("zeros", [128, 512])
        node = sb("node", [R, NT])
        hm32 = sb("hm32", [128, 128])
        hm64 = sb("hm64", [128, 128])
        eps_t = sb("eps_t", [128, 1])
        srcI = sb("srcI", [R, EC], I32)
        dstI = sb("dstI", [R, EC], I32)
        ew = sb("ew", [R, EC])
        te = sb("te", [R, EC])
        recA = sb("recA", [128, T0])
        recW = sb("recW", [128, T0])
        recB = sb("recB", [128, T1])
        recT = sb("recT", [128, T1])
        gblk0 = sb("gblk0", [128, G0], I32)
        gblk1 = sb("gblk1", [128, G1], I32)
        st6 = sb("st6", [R, U5, 6])
        mv = sb("mv", [R, U5, 2])
        sd = sb("sd", [R, U5])
        rs = sb("rs", [R, U5])
        gwt = sb("gwt", [R, 2, NT])
        slotI = sb("slotI", [R, 2 * NT], I32)
        idxA = sb("idxA", [128, T0], I32)
        idxB = sb("idxB", [128, T1], I32)
        dcol = sb("dcol", [R, NT])

        psum = [ctx.enter_context(nc.psum_tensor(f"bank{b}", [128, 512], F32)) for b in range(8)]

        class Carver:
            def __init__(self, t):
                self.t, self.at = t, 0

            def __call__(self, *shape, rows=128, dt=F32):
                n = 1
                for k in shape:
                    n *= k
                v = self.t[0:rows, self.at:self.at + n]
                self.at += n
                assert self.at <= self.t.shape[1], (self.at, shape)
                if dt is not F32:
                    v = v.bitcast(dt)
                if len(shape) == 2:
                    v = v.rearrange("p (a b) -> p a b", a=shape[0])
                if len(shape) == 3:
                    v = v.rearrange("p (a b c) -> p a b c", a=shape[0], b=shape[1])
                return v

        c = Carver(SCR)
        iotaI = c(MAXG, dt=I32)
        nodeI = c(NT, rows=R, dt=I32)

        dram = lambda name, shape: nc.dram_tensor(name, shape, F32, kind="Internal").ap()
        tab0 = dram("tab0", [N, D])
        tab1 = dram("tab1", [N, ROW1])
        hrow0 = dram("hrow0", [N, D])
        hrow1 = dram("hrow1", [N, D])
        ys0 = dram("ys0", [M0 * 128, D])
        ys1 = dram("ys1", [M1 * 128, D])

        def tiles(t):
            return t.rearrange("(p j) d -> p j d", j=NT)

        c = Carver(WD)
        wkv = c(2, 2 * D)
        ham = c(2, D)
        wq = c(2, D)
        wm = c(2, D)
        w1 = c(4, HID)
        w2 = c(4, D)
        c = Carver(WD)
        wfx = c(2, ROW1)
        wsm = c(2, 2 * D)
        wkv1 = c(2, 2 * HID)
        wout = c(4, D)
        wqo = c(4, D)

        vec = {n: sb(n, [128, w]) for n, w in (
            ("g2b", D), ("b2b", D), ("gammab", D), ("betab", D),
            ("attb", 2 * D + EDIM), ("gb0", X0), ("gb1", X1))}
        gw0 = sb("gw0", [128, 2, X0])
        gw1 = sb("gw1", [128, 2, X1])
        LG = sb("LG", [R, NT, X1])
        Mx = sb("Mx", [R, NT])
        den = sb("den", [R, NT])
        has = sb("has", [R, NT])
        g1c = sb("g1c", [128, 2])
        b1c = sb("b1c", [128, 2])

        bar = sem("all_engines_here")
        consts = sem("constants_ready")
        x_in = sem("x_in")
        edges_in = sem("edges_in")
        w0_raw = sem("L0_dense_weights_in")
        vec_in = sem("L0_vectors_in")
        step = {}

        def S(name):
            if name not in step:
                step[name] = sem(name)
            return step[name]

        block = ctx.enter_context(nc.Block())
        barriers = {}

        def barrier(eng, key):
            barriers[key] = barriers.get(key, 0) + 1
            eng.drain().then_inc(bar, 1)
            eng.wait_ge(bar, 5 * barriers[key])


        def turn(ap):
            return ap.rearrange("p a d -> p (a d)")

        c = Carver(SCR)
        xs = c(U5, D, rows=R)
        xT = c(U5, 2, R)
        norm_end = c.at

        BEFORE = {ph: n * (NT // U5) for n, ph in enumerate(("a0", "g0", "a1", "g1", "fin"))}

        def v_norm(v, b, i, kept):
            for u in range(U5):
                v.bn_stats(st6[:, u, :], turn(X[:, ds(i * U5 + u, 1), :]))
            v.drain()
            for u in range(U5):
                k = v.bn_aggr(mv[:, u, :], st6[:, u, :])
            k.then_inc(S("x_var"), 1)
            v.wait_ge(S("x_sd"), b + i + 1)
            v.reciprocal(rs[:, :], sd[:, :])
            v.drain()
            v.wait_ge(S("x_turned"), freed(b + i, U5 - 1, U5))
            kept()
            for u in range(U5):
                v.tensor_scalar(xs[:, u, :], turn(X[:, ds(i * U5 + u, 1), :]), mv[:, u, 0:1],
                                rs[:, u:u + 1], ALU.subtract, ALU.mult).then_inc(S("x_xs"), 1)

        def a_sqrt(a, b, i):
            a.wait_ge(S("x_var"), b + i + 1)
            a.activation(sd[:, :], mv[:, :, 1], ACT.Sqrt, bias=eps_t[0:R, 0:1]).then_inc(S("x_sd"), 1)

        def half(u):
            return psum[u % 2][:, 0:256].rearrange("p (h r) -> p h r", h=2)

        def t_turn(t, b, i, u):
            t.wait_ge(S("x_xs"), (b + i) * U5 + (u + 1))
            t.wait_ge(S("x_xT"), freed(b + i, u, 2))
            for h in range(2):
                k = t.transpose(half(u)[:, h, 0:R], xs[:, u, h * 128:(h + 1) * 128], ident[0:R, 0:R])
            k.then_inc(S("x_turned"), 1)

        def a_turned(a, b, i, u, users):
            a.wait_ge(S("x_turned"), done(b + i, u))
            users()
            a.copy(xT[:, u, :, :], half(u)[:, :, 0:R]).then_inc(S("x_xT"), 1)

        def seed(eng, *names, n=U5):
            for name in names:
                eng.sem_inc(S(name), n)

        c = Carver(SCR)
        c.at = norm_end
        ek = c(U5, D, rows=R)
        Kt = c(U5, D, rows=R)
        Vt = c(U5, 2, 129, rows=R)
        sup = c(U5, D, rows=R)

        def t_a0(t):
            seed(t, "x_turned", "a0_kv", "a0_sup", "a0_KV")
            t.wait_ge(consts, 3)
            t_bounds(t, 258, True, (4,))
            with t.Fori(0, NT // U5) as i:
                for u in range(U5):
                    t_turn(t, 0, i, u)

                def sums(u):
                    t.wait_ge(S("a0_K"), done(i, u))
                    t.wait_ge(S("a0_V"), done(i, u))
                    for h in range(2):
                        k = t.matmul(psum[4][:, h * 129:(h + 1) * 129], Kt[:, u, h * 128:(h + 1) * 128], Vt[:, u, h, :],
                                     start=False, stop=False, skip_group_check=True)
                    k.then_inc(S("a0_KV"), 1)

                for u in range(U5):
                    t.wait_ge(S("x_xT"), done(i, u))
                    t.wait_ge(S("a0_K"), freed(i, u, 2))
                    for h in range(2):
                        k = t.matmul(psum[2 + u % 2][0:R, :], xT[:, u, h, :], wkv[:, h, :],
                                     start=(h == 0), stop=(h == 1))
                    k.then_inc(S("a0_kv"), 1)
                    t.wait_ge(S("a0_supc"), freed(i, u, 2))
                    for h in range(2):
                        k = t.matmul(psum[5 + u % 2][0:R, 0:D], xT[:, u, h, :], ham[:, h, :],
                                     start=(h == 0), stop=(h == 1))
                    k.then_inc(S("a0_sup"), 1)
                    if u:
                        sums(u - 1)
                sums(U5 - 1)
            t_bounds(t, 258, False, (4,))

        def a_a0(a):
            seed(a, "x_xT", "a0_V", "a0_ek")
            with a.Fori(0, NT // U5) as i:
                a_sqrt(a, 0, i)
                for u in range(U5):
                    def users():
                        a.wait_ge(S("a0_sup"), freed(i, u, U5))
                        a.wait_ge(S("a0_xkeep"), freed(i, u, U5))
                    a_turned(a, 0, i, u, users)
                for u in range(U5):
                    a.wait_ge(S("a0_kv"), done(i, u))
                    a.wait_ge(S("a0_K"), freed(i, u, U5))
                    a.activation(ek[:, u, :], psum[2 + u % 2][0:R, 0:D], ACT.Exp).then_inc(S("a0_ek"), 1)
                    a.wait_ge(S("a0_KV"), freed(i, u, U5))
                    a.copy(Vt[:, u, :, 0:128], psum[2 + u % 2][0:R, D:2 * D].rearrange("p (h f) -> p h f", h=2)
                           ).then_inc(S("a0_V"), 1)

        def p_a0(p):
            seed(p, "a0_xkeep")
            with p.Fori(0, NT // U5) as i:
                for u in range(U5):
                    p.wait_ge(S("x_xT"), done(i, u))
                    p.wait_ge(consts, 1)
                    p.tensor_copy(xnT[:, :, ds((i * U5 + u) * R, R)], xT[:, u, :, :]).then_inc(S("a0_xkeep"), 1)

        def v_a0(v):
            seed(v, "a0_K", "a0_supc")
            v.memset(Vt[:, :, :, 128:129].rearrange("p u h o -> p (u h) o"), 1.0)
            with v.Fori(0, NT // U5) as i:
                v_norm(v, 0, i, lambda: None)
                v.drain()
                x5 = X[:, ds(i * U5, U5), :]
                v.tensor_tensor(x5, x5, xs[:, :, :], ALU.add)
                for u in range(U5):
                    v.wait_ge(S("a0_ek"), done(i, u))
                    v.tensor_scalar(ek[:, u, :], ek[:, u, :], 1.0, None, ALU.min)
                    v.drain()
                    v.wait_ge(S("a0_KV"), freed(i, u, U5))
                    v.wait_ge(S("a0_V"), done(i, u))
                    v.scalar_tensor_tensor(Kt[:, u, :], psum[2 + u % 2][0:R, 0:D], 0.0, ek[:, u, :],
                                           ALU.max, ALU.add).then_inc(S("a0_K"), 1)
                    v.wait_ge(S("a0_sup"), done(i, u))
                    v.wait_ge(S(f"a_out{u}"), landed(i))
                    v.wait_ge(consts, 1)
                    v.tensor_copy(sup[:, u, :], psum[5 + u % 2][0:R, 0:D]).then_inc(S("a0_supc"), 1)

        def s_a0(s):
            seed(s, *(f"a_out{u}" for u in range(U5)), n=16)
            with s.Fori(0, NT // U5) as i:
                for u in range(U5):
                    s.wait_ge(S("a0_supc"), done(i, u))
                    s.dma_start(tiles(tab0)[:, ds(i * U5 + u, 1), :].rearrange("p a d -> p (a d)"), sup[:, u, :]
                                ).then_inc(S(f"a_out{u}"), 16)
            for u in range(U5):
                s.wait_ge(S(f"a_out{u}"), landed(NT // U5))

        c = Carver(SCR)
        kvbd = c(2, 128)
        ksx = c(2, 128)
        WMAX = 3 * R
        eq = c(2, WMAX)
        QT = c(2, WMAX)
        dn = c(WMAX)
        msgT = c(2, WMAX)
        mn = c(3, D, rows=R)
        mT = c(2, WMAX)
        hT = c(4, WMAX)
        yr = c(3, D, rows=R)

        def v_kv(v):
            for h in range(2):
                v.scalar_tensor_tensor(kvbd[:, h, :], psum[4][:, h * 129:h * 129 + 128], 1.0 / N, hm32[:, :], ALU.mult, ALU.mult)
                v.tensor_scalar(ksx[:, h, :], hm32[:, :], psum[4][:, h * 129 + 128:h * 129 + 129], None, ALU.mult)

        def row_ps(k):
            return psum[4 + k // 2][0:R, (k % 2) * 256:(k % 2) * 256 + 256]

        def t_b0(t):
            with t.Fori(0, NT // U5) as i:
                for r, (t0, nt) in enumerate(TOKS):
                    n, w = i * 2 + r, nt * R
                    cols = ds((i * U5 + t0) * R, w)
                    for f in range(2):
                        for h in range(2):
                            k = t.matmul(psum[f][:, 0:w], wq[:, h, f * 128:(f + 1) * 128], xnT[:, h, cols],
                                         start=(h == 0), stop=(h == 1))
                    k.then_inc(S("b0_q"), 1)
                    for h in range(2):
                        t.wait_ge(S("b0_Q"), n + 1)
                        t.wait_ge(S("b0_msg"), n * 2 + (h + 2))
                        t.matmul(psum[2][:, 0:w], kvbd[:, h, :], QT[:, h, 0:w], start=True, stop=True)
                        t.matmul(psum[3][:, 0:w], ksx[:, h, :], QT[:, h, 0:w], start=True, stop=True
                                 ).then_inc(S("b0_nd"), 1)
                    t.wait_ge(S("b0_msg"), n * 2 + 4)
                    t.wait_ge(S("b0_x"), n + 1)
                    for j in range(nt):
                        for h in range(2):
                            k = t.matmul(row_ps(j), msgT[:, h, j * R:(j + 1) * R], wm[:, h, :],
                                         start=(h == 0), stop=(h == 1))
                    k.then_inc(S("b0_m"), 1)
                    t.wait_ge(S("b0_mn"), n + 1)
                    for h in range(2):
                        for j in range(nt):
                            k = t.transpose(psum[h][:, j * R:(j + 1) * R], mn[:, j, h * 128:(h + 1) * 128],
                                            ident[0:R, 0:R])
                    k.then_inc(S("b0_mt"), 1)
                    t.wait_ge(S("b0_mT"), n + 1)
                    for f in range(4):
                        t.wait_ge(S("b0_h"), n * 4 + (f + 2))
                        for h in range(4):
                            src_t = xnT[:, h, cols] if h < 2 else mT[:, h - 2, 0:w]
                            k = t.matmul(psum[6 + f % 2][:, 0:w], w1[:, h, f * 128:(f + 1) * 128], src_t,
                                         start=(h == 0), stop=(h == 3))
                        k.then_inc(S("b0_hp"), 1)
                    t.wait_ge(S("b0_h"), n * 4 + 7)
                    for j in range(nt):
                        for f in range(4):
                            k = t.matmul(row_ps(j), hT[:, f, j * R:(j + 1) * R], w2[:, f, :],
                                         start=(f == 0), stop=(f == 3))
                    k.then_inc(S("b0_y"), 1)

        def a_b0(a):
            a.sem_inc(S("b0_h"), 3)
            with a.Fori(0, NT // U5) as i:
                for r, (t0, nt) in enumerate(TOKS):
                    n, w = i * 2 + r, nt * R
                    a.wait_ge(S("b0_q"), n + 1)
                    for f in range(2):
                        a.activation(eq[:, f, 0:w], psum[f][:, 0:w], ACT.Exp).then_inc(S("b0_eq"), 1)
                    a.wait_ge(S("b0_var1"), n + 1)
                    a.activation(sd[:, 0:nt], mv[:, 0:nt, 1], ACT.Sqrt, bias=eps_t[0:R, 0:1]).then_inc(S("b0_sd1"), 1)
                    a.wait_ge(S("b0_mt"), n + 1)
                    for h in range(2):
                        k = a.activation(mT[:, h, 0:w], psum[h][:, 0:w], ACT.Identity, bias=b1c[:, h:h + 1],
                                         scale=g1c[:, h:h + 1])
                    k.then_inc(S("b0_mT"), 1)
                    for f in range(4):
                        a.wait_ge(S("b0_hp"), n * 4 + (f + 1))
                        a.activation(hT[:, f, 0:w], psum[6 + f % 2][:, 0:w], ACT.Relu).then_inc(S("b0_h"), 1)
                    a.wait_ge(S("b0_var2"), n + 1)
                    a.activation(sd[:, 0:nt], mv[:, 0:nt, 1], ACT.Sqrt, bias=eps_t[0:R, 0:1]).then_inc(S("b0_sd2"), 1)

        def v_rows_norm(v, nt, ps, dst, var, sdn, n, free):
            for j in range(nt):
                v.bn_stats(st6[:, j, :], ps(j))
            v.drain()
            for j in range(nt):
                k = v.bn_aggr(mv[:, j, :], st6[:, j, :])
            k.then_inc(S(var), 1)
            v.wait_ge(S(sdn), n + 1)
            v.reciprocal(rs[:, 0:nt], sd[:, 0:nt])
            v.drain()
            free()
            for j in range(nt):
                k = v.tensor_scalar(dst[:, j, :], ps(j), mv[:, j, 0:1], rs[:, j:j + 1], ALU.subtract, ALU.mult)
            return k

        def v_b0(v):
            seed(v, "b0_x", n=1)
            seed(v, "b0_msg", n=2)
            with v.Fori(0, NT // U5) as i:
                for r, (t0, nt) in enumerate(TOKS):
                    n, w = i * 2 + r, nt * R
                    v.wait_ge(S("b0_eq"), n * 2 + 2)
                    v.tensor_scalar(eq[:, :, 0:w], eq[:, :, 0:w], 1.0, None, ALU.min)
                    v.drain()
                    for f in range(2):
                        k = v.scalar_tensor_tensor(QT[:, f, 0:w], psum[f][:, 0:w], 0.0, eq[:, f, 0:w],
                                                   ALU.max, ALU.add)
                    k.then_inc(S("b0_Q"), 1)
                    for h in range(2):
                        v.wait_ge(S("b0_nd"), n * 2 + (h + 1))
                        v.tensor_scalar(dn[:, 0:w], psum[3][:, 0:w], 1e-6, None, ALU.add)
                        v.drain()
                        v.reciprocal(dn[:, 0:w], dn[:, 0:w])
                        v.drain()
                        v.scalar_tensor_tensor(msgT[:, h, 0:w], psum[2][:, 0:w], float(N), dn[:, 0:w],
                                               ALU.mult, ALU.mult).then_inc(S("b0_msg"), 1)
                    v.wait_ge(S("b0_m"), n + 1)
                    v.wait_ge(consts, 1)
                    v_rows_norm(v, nt, row_ps, mn, "b0_var1", "b0_sd1", n, lambda: None).then_inc(S("b0_mn"), 1)
                    v.wait_ge(S("b0_y"), n + 1)
                    v.wait_ge(consts, 1)
                    v_rows_norm(v, nt, row_ps, yr, "b0_var2", "b0_sd2", n, lambda: None).then_inc(S("b0_x"), 1)
                    v.drain()
                    g = g2b[0:R, :].unsqueeze(1).broadcast_to([R, nt, D])
                    v.tensor_tensor(yr[:, 0:nt, :], yr[:, 0:nt, :], g, ALU.mult)
                    v.drain()
                    xr = X[:, ds(i * U5 + t0, nt), :]
                    v.tensor_tensor(xr, xr, yr[:, 0:nt, :], ALU.add)
                    v.drain()
                    v.tensor_tensor(xr, xr, b2b[0:R, :].unsqueeze(1).broadcast_to([R, nt, D]), ALU.add)

        c = Carver(SCR)
        blkF = c(EC, rows=R)
        loI = c(EC, rows=R, dt=I32)
        inb = c(EC, rows=R)
        run = c(EC, rows=R)
        pos = c(EC, rows=R)
        bsum = c(EC, rows=R)
        posI = c(EC, rows=R, dt=I32)
        tI = loI
        one_row = c(EC, rows=R)
        tF = c(EC, rows=R)
        qF = c(EC, rows=R)
        packed = c(EC, rows=R)
        cnt = c(NT, rows=R)
        ngI = c(NT, dt=I32)
        ngF = c(NT)
        cum = c(NT)
        base = c(NT)
        offs = c(NT, rows=R)
        gbF = c(MAXG)
        sort_end = c.at
        gbI = gbF.bitcast(I32)

        SORT = {"s0": 1, "s1": 2, "r0": 3, "r1": 4}
        MOVED = {"s0": 0, "s1": EC, "r0": 2 * EC, "r1": 2 * EC + K0 * NT}

        def v_keys(v, keyI, idxI):
            v.tensor_scalar(loI[:, :], keyI[:, :], 1311.0, None, ALU.mult)
            v.drain()
            v.tensor_scalar(loI[:, :], loI[:, :], 15, None, ALU.logical_shift_right)
            v.drain()
            v.scalar_tensor_tensor(blkF[:, :], loI[:, :], -float(NT), keyI[:, :], ALU.mult, ALU.add)
            v.scalar_tensor_tensor(packed[:, :], loI[:, :], 4096.0, idxI[:, :], ALU.mult, ALU.add)
            v.drain()
            v.tensor_scalar(packed[:, :], packed[:, :], 4096.0, None, ALU.add)

        def v_count(v, ph, C, K):
            v.memset(cnt[:, :], 0.0)
            v.memset(pos[:, 0:C], 0.0)
            v.memset(bsum[:, 0:C], 0.0)
            v.memset(gbF[:, :], 0.0)
            v.memset(one_row[:, :], 1.0)
            v.drain()
            with v.Fori(0, K) as b:
                v.tensor_scalar(inb[:, 0:C], blkF[:, 0:C], iota[0:R, ds(b, 1)], None, ALU.is_equal)
                v.drain()
                v.tensor_reduce(cnt[:, ds(b, 1)], inb[:, 0:C], AX_X, ALU.add)
                v.drain()
            v.drain().then_inc(S("s_cnt"), 1)

        def t_count(t, ph, K):
            t.wait_ge(S("s_cnt"), SORT[ph])
            t.matmul(psum[0][:, 0:K], ones[0:R, :], cnt[:, 0:K], start=True, stop=True)
            t.matmul(psum[1][0:R, 0:K], tri[0:R, 0:R], cnt[:, 0:K], start=True, stop=True
                     ).then_inc(S("s_tot"), 1)

        def v_place(v, ph, C, K, gt, G, gblk, bases=False):
            shift = (128 * gt).bit_length() - 1
            v.wait_ge(S("s_tot"), SORT[ph])
            v.tensor_scalar(ngI[:, 0:K], psum[0][:, 0:K], float(128 * gt - 1), None, ALU.add)
            v.drain()
            v.tensor_scalar(ngI[:, 0:K], ngI[:, 0:K], shift, None, ALU.logical_shift_right)
            v.drain()
            v.tensor_copy(ngF[:, 0:K], ngI[:, 0:K])
            v.drain()
            v.tensor_tensor_scan(cum[:, 0:K], ones[:, 0:K], ngF[:, 0:K], 0.0, ALU.mult, ALU.add)
            v.drain()
            v.tensor_tensor(base[:, 0:K], cum[:, 0:K], ngF[:, 0:K], ALU.subtract)
            v.drain()
            v.tensor_scalar(base[:, 0:K], base[:, 0:K], float(128 * gt), None, ALU.mult)
            v.drain()
            v.scalar_tensor_tensor(offs[:, 0:K], psum[1][0:R, 0:K], -1.0, base[0:R, 0:K], ALU.add, ALU.add)
            v.drain()
            with v.Fori(0, K) as b:
                v.tensor_scalar(inb[:, 0:C], blkF[:, 0:C], iota[0:R, ds(b, 1)], None, ALU.is_equal)
                v.scalar_tensor_tensor(gbF[:, 0:G], iota[:, 0:G], cum[:, ds(b, 1)], gbF[:, 0:G], ALU.is_ge, ALU.add)
                v.drain()
                v.tensor_tensor_scan(run[:, 0:C], one_row[0:R, 0:C], inb[:, 0:C], offs[:, ds(b, 1)], ALU.mult, ALU.add)
                if bases:
                    v.scalar_tensor_tensor(bsum[:, 0:C], inb[:, 0:C], base[0:R, ds(b, 1)], bsum[:, 0:C],
                                           ALU.mult, ALU.add)
                v.drain()
                v.tensor_tensor(run[:, 0:C], run[:, 0:C], inb[:, 0:C], ALU.mult)
                v.drain()
                v.tensor_tensor(pos[:, 0:C], pos[:, 0:C], run[:, 0:C], ALU.add)
                v.drain()
            v.tensor_scalar(gbF[:, 0:G], gbF[:, 0:G], float(K - 1), None, ALU.min)
            v.tensor_copy(posI[:, 0:C], pos[:, 0:C])
            v.drain()
            v.tensor_copy(gblk[:, 0:G], gbF[:, 0:G])
            v.tensor_scalar(tI[:, 0:C], posI[:, 0:C], 7, None, ALU.logical_shift_right)
            v.tensor_scalar(posI[:, 0:C], posI[:, 0:C], 127, None, ALU.bitwise_and)
            v.drain()
            v.tensor_copy(tF[:, 0:C], tI[:, 0:C])
            v.tensor_copy(qF[:, 0:C], posI[:, 0:C])
            v.drain()

        OB = 4
        c = Carver(SCR)
        c.at = sort_end
        ot = c(OB, MAXG, rows=R)
        oq = c(OB, 2, 128, rows=R)
        move_end = c.at

        def v_onehot(v, ph, i, u, val2, T, per=EU):
            col = i * per + u
            v.wait_ge(S("s_used"), freed(i, u, OB, per) + MOVED[ph] + EU - per)
            v.tensor_scalar(ot[:, u % OB, 0:T], iota[0:R, 0:T], tF[:, ds(col, 1)], None, ALU.is_equal)
            vals = (packed,) if val2 is None else (packed, val2)
            for n, val in enumerate(vals):
                k = v.tensor_scalar(oq[:, u % OB, n, :], iota[0:R, 0:128], qF[:, ds(col, 1)], val[:, ds(col, 1)],
                                    ALU.is_equal, ALU.mult)
            k.then_inc(S("s_onehot"), 1)

        def t_move(t, ph, i, u, T, two=True, per=EU):
            t.wait_ge(S("s_onehot"), i * per + (u + 1 + MOVED[ph]))
            for n in range(1 + two):
                k = t.matmul(psum[6 + n][:, 0:T], oq[:, u % OB, n, :], ot[:, u % OB, 0:T], start=False,
                             stop=False, skip_group_check=True)
            k.then_inc(S("s_used"), 1)

        def t_bounds(t, T, start, banks=(6, 7)):
            for b in banks:
                k = t.matmul(psum[b][:, 0:T], zeros[:, 0:128], zeros[:, 0:T], start=start, stop=not start,
                             skip_group_check=True)
            return k

        def v_records(v, T, rec, idx, val):
            v.tensor_copy(idx[:, 0:T], psum[6][:, 0:T])
            v.tensor_copy(val[:, 0:T], psum[7][:, 0:T])
            v.drain()
            v.tensor_scalar(gbI[:, 0:T], idx[:, 0:T], 12, None, ALU.logical_shift_right)
            v.drain()
            v.tensor_scalar(idx[:, 0:T], idx[:, 0:T], 4095, None, ALU.bitwise_and)
            v.tensor_copy(rec[:, 0:T], gbI[:, 0:T])
            v.drain()

        c = Carver(SCR)
        c.at = move_end
        gi = c(2, EU // 2, dt=I32)
        g0 = c(EU, D)
        s0 = c(EU, R)

        def p_gather(p, ph, b, i, idx, table, dst):
            for h in range(2):
                us = range(h * EU // 2, (h + 1) * EU // 2)
                p.wait_ge(S(ph + "_sum"), freed(i, us[-1], EU, EU))
                p.sem_inc(S("holds_waits"), 1)
                p.tensor_copy(gi[:, h, :], idx[:, ds(i * EU + us[0], EU // 2)])
                p.drain()
                for k, u in enumerate(us):
                    p.indirect_dma_start(dst[:, u, :], None, table,
                                         bass.IndirectOffsetOnAxis(ap=gi[:, h, k:k + 1], axis=0)
                                         ).then_inc(S(f"e_g{u}"), 16)

        def v_sel0(v, i, u):
            t = i * EU + u
            v.wait_ge(S("e0_sum"), freed(i, u, EU, EU))
            v.tensor_scalar(s0[:, u, :], iota[:, 1:R + 1], recA[:, ds(t, 1)], recW[:, ds(t, 1)],
                            ALU.is_equal, ALU.mult).then_inc(S("e0_sel"), 1)

        def t_e0(t, i, u):
            t.wait_ge(S("e0_sel"), i * EU + (u + 1))
            t.wait_ge(S(f"e_g{u}"), gathered(i + 1))
            t.wait_ge(S("e0_acc"), freed(i, u, 4, EU))
            t.matmul(psum[2 + u % 4][0:R, 0:D], s0[:, u, :], g0[:, u, :], start=True, stop=True
                     ).then_inc(S("e0_sum"), 1)

        def v_acc0(v, i, u, blk):
            v.drain()
            v.wait_ge(S("e0_sum"), done(i, u, EU))
            a = turn(AGG[:, ds(blk, 1), :])
            v.tensor_tensor(a, a, psum[2 + u % 4][0:R, 0:D], ALU.add).then_inc(S("e0_acc"), 1)

        bnm = XN
        c = Carver(SCR)
        gm2 = c(D, rows=R)
        mean = c(D, rows=R)
        var = c(D, rows=R)
        rstd = c(D, rows=R)

        def t_bn(t, src_t, bank, wait, name):
            t.wait_ge(S(wait), 1)
            for j in range(NT):
                k = t.matmul(psum[bank][0:R, 0:D], ones[0:R, 0:R], src_t[:, j, :], start=(j == 0), stop=(j == NT - 1))
            k.then_inc(S(name), 1)

        def bc(v2):
            return v2[:, :].unsqueeze(1).broadcast_to([R, NT, D])

        def v_bn(v):
            v.drain().then_inc(S("bn_agg"), 1)
            v.wait_ge(S("bn_sum"), 1)
            v.tensor_scalar(mean[:, :], psum[0][0:R, 0:D], 1.0 / N, None, ALU.mult)
            v.drain()
            v.tensor_tensor(AGG[:, :, :], AGG[:, :, :], bc(mean), ALU.subtract).then_inc(S("bn_centred"), 1)
            v.wait_ge(S("bn_ssq"), 1)
            v.tensor_scalar(var[:, :], psum[1][0:R, 0:D], 1.0 / N, None, ALU.mult).then_inc(S("bn_var"), 1)
            v.wait_ge(S("bn_sd"), 1)
            v.reciprocal(rstd[:, :], rstd[:, :])
            v.drain()
            v.tensor_tensor(rstd[:, :], rstd[:, :], gammab[0:R, :], ALU.mult)
            v.drain()
            v.tensor_tensor(AGG[:, :, :], AGG[:, :, :], bc(rstd), ALU.mult)
            v.drain()
            v.tensor_tensor(AGG[:, :, :], AGG[:, :, :], bc(betab[0:R, :]), ALU.add).then_inc(S("bn_y"), 1)
            v.wait_ge(S("bn_tanh"), 1)
            v.tensor_tensor(X[:, :, :], X[:, :, :], bnm[:, :, :], ALU.add)

        def a_bn(a):
            a.wait_ge(S("bn_centred"), 1)
            a.activation(bnm[:, :, :], AGG[:, :, :], ACT.Square).then_inc(S("bn_sq"), 1)
            a.wait_ge(S("bn_var"), 1)
            a.activation(rstd[:, :], var[:, :], ACT.Sqrt, bias=eps_t[0:R, 0:1]).then_inc(S("bn_sd"), 1)
            a.wait_ge(S("bn_y"), 1)
            a.activation(bnm[:, :, :], AGG[:, :, :], ACT.Tanh).then_inc(S("bn_tanh"), 1)


        ea = XN[:, 0:20, :].rearrange("p a b -> p (a b)").rearrange("p (s c e) -> p s c e", s=2, c=40)

        def s_te(s):
            av = A["edge_attr_64"].rearrange("(p c) e -> p c e", p=R)
            with s.Fori(0, EC // 80) as i:
                for u in range(2):
                    s.wait_ge(S("te_read"), freed(i, u, 2, 2))
                    s.dma_start(ea[:, u], av[:, ds((i * 2 + u) * 40, 40), :]).then_inc(S(f"te_in{u}"), 16)

        def v_te(v):
            seed(v, "te_read", n=2)
            with v.Fori(0, EC // 80) as i:
                for u in range(2):
                    v.wait_ge(S(f"te_in{u}"), 16 * (i + 1))
                    v.tensor_tensor(ea[:, u], ea[:, u], attb[0:R, 2 * D:2 * D + EDIM].unsqueeze(1)
                                    .broadcast_to([R, 40, EDIM]), ALU.mult)
                    v.drain()
                    v.tensor_reduce(te[:, ds((i * 2 + u) * 40, 40)], ea[:, u], AX_X, ALU.add
                                    ).then_inc(S("te_read"), 1)

        GATE = {"g0": 0, "g1": NT // U5}

        def t_gate(t, ph, gw, NX):
            if ph == "g0":
                seed(t, "g_lgp")
            with t.Fori(0, NT // U5) as i:
                for u in range(U5):
                    t_turn(t, BEFORE[ph], i, u)
                t.wait_ge(S("g_lg"), GATE[ph] + i + 1)
                for u in range(U5):
                    t.wait_ge(S("x_xT"), done(BEFORE[ph] + i, u))
                    for h in range(2):
                        k = t.matmul(psum[2][0:R, u * NX:(u + 1) * NX], xT[:, u, h, :], gw[:, h, :],
                                     start=(h == 0), stop=(h == 1))
                    k.then_inc(S("g_lgp"), 1)

        def a_gate(a, ph):
            with a.Fori(0, NT // U5) as i:
                a_sqrt(a, BEFORE[ph], i)
                for u in range(U5):
                    a_turned(a, BEFORE[ph], i, u, lambda: a.wait_ge(S("g_lgp"), freed(GATE[ph] + i, u, U5)))

        def v_gate(v, ph, gb, NX, keep):
            if ph == "g0":
                seed(v, "g_lg", n=1)
            with v.Fori(0, NT // U5) as i:
                def kept():
                    v.wait_ge(S("g_hout"), landed(GATE[ph] + i))
                    if keep:
                        v.wait_ge(S("g_keep"), i + 1)
                v_norm(v, BEFORE[ph], i, kept)
                v.wait_ge(S("g_lgp"), done(GATE[ph] + i, U5 - 1))
                v.tensor_tensor(LG[:, ds(i * U5, U5), 0:NX],
                                psum[2][0:R, 0:U5 * NX].rearrange("p (a b) -> p a b", a=U5),
                                gb[0:R, 0:NX].unsqueeze(1).broadcast_to([R, U5, NX]), ALU.add
                                ).then_inc(S("g_lg"), 1)

        def s_gate(s, ph, hrow):
            if ph == "g0":
                seed(s, "g_hout", n=16)
            with s.Fori(0, NT // U5) as i:
                s.wait_ge(S("x_xs"), (BEFORE[ph] + i) * U5 + U5)
                s.dma_start(tiles(hrow)[:, ds(i * U5, U5), :], xs[:, :, :]).then_inc(S("g_hout"), 16)
            s.wait_ge(S("g_hout"), landed(GATE[ph] + NT // U5))

        def p_keep(p, ph):
            seed(p, "g_keep", n=1)
            with p.Fori(0, NT // U5) as i:
                p.wait_ge(S("x_xs"), (BEFORE[ph] + i) * U5 + U5)
                p.sem_inc(S("holds_waits"), 1)
                p.tensor_copy(XN[:, ds(i * U5, U5), :], xs[:, :, :]).then_inc(S("g_keep"), 1)

        c = Carver(SCR)
        c.at = move_end
        mx = c(2, NT, rows=R)
        low = c(NT, rows=R)
        eqm = c(NT, X1, rows=R)
        eqx = c(NT, X1, rows=R)
        sm = c(NT, rows=R)

        def bx(v2, NX):
            return v2.unsqueeze(2).broadcast_to([R, NT, NX])

        def v_choose(v, ph, NX, K):
            v.wait_ge(S("g_hout"), landed(GATE[ph] + NT // U5))
            if K > 1:
                v.wait_ge(S("g_keep"), NT // U5 + 1)
            sc = LG[:, :, 0:NX]
            ids = iota[0:R, 0:NX].unsqueeze(1).broadcast_to([R, NT, NX])
            for k in range(K):
                v.tensor_reduce(mx[:, k, :], sc, AX_X, ALU.max)
                v.drain()
                v.tensor_tensor(eqm[:, :, 0:NX], sc, bx(mx[:, k, :], NX), ALU.is_equal)
                v.drain()
                v.scalar_tensor_tensor(eqm[:, :, 0:NX], eqm[:, :, 0:NX], -100.0, ids, ALU.mult, ALU.add)
                v.drain()
                v.tensor_reduce(low[:, :], eqm[:, :, 0:NX], AX_X, ALU.min)
                v.drain()
                b = blkF[:, k * NT:(k + 1) * NT]
                v.tensor_scalar(b, low[:, :], 100.0, None, ALU.add)
                v.tensor_copy(packed[:, k * NT:(k + 1) * NT], node[:, :])
                v.drain()
                if K == 1:
                    v.tensor_tensor(eqx[:, :, 0:NX], sc, bx(mx[:, 0, :], NX), ALU.subtract)
                elif k == 0:
                    v.tensor_tensor(eqm[:, :, 0:NX], ids, bx(b, NX), ALU.is_equal)
                    v.drain()
                    v.scalar_tensor_tensor(sc, eqm[:, :, 0:NX], -BIG, sc, ALU.mult, ALU.add)
                    v.drain()
            if K == 1:
                v.drain().then_inc(S("g_x"), 1)
                v.wait_ge(S("g_ex"), K)
                v.tensor_reduce(sm[:, :], eqx[:, :, 0:NX], AX_X, ALU.add)
                v.drain()
                v.reciprocal(gwt[:, 0, :], sm[:, :])
            else:
                v.tensor_tensor(sm[:, :], mx[:, 1, :], mx[:, 0, :], ALU.subtract).then_inc(S("g_x"), 1)
                v.wait_ge(S("g_ex"), K)
                v.tensor_scalar(low[:, :], sm[:, :], 1.0, None, ALU.add)
                v.drain()
                v.reciprocal(gwt[:, 0, :], low[:, :])
                v.drain()
                v.tensor_tensor(gwt[:, 1, :], gwt[:, 0, :], sm[:, :], ALU.mult)
            v.drain()

        def a_choose(a, ph, NX, K):
            a.wait_ge(S("g_x"), K)
            z = eqx[:, :, 0:NX] if K == 1 else sm[:, :]
            a.activation(z, z, ACT.Exp).then_inc(S("g_ex"), 1)

        def v_route(v, ph, K, NX, M):
            C = NT * K
            v_count(v, ph, C, NX)
            v_place(v, ph, C, NX, 1, M, gblk0, bases=(K == 1))
            v.tensor_copy(slotI[:, 0:C], pos[:, 0:C])
            if K == 1:
                v.tensor_tensor(low[:, :], pos[:, 0:C], bsum[:, 0:C], ALU.subtract)
                v.drain()
                v.tensor_scalar(low[:, :], low[:, :], float(CAP), None, ALU.is_lt)
                v.drain()
                v.tensor_tensor(gwt[:, 0, :], gwt[:, 0, :], low[:, :], ALU.mult)
            with v.Fori(0, C // U5) as i:
                for u in range(U5):
                    v_onehot(v, ph, i, u, None, M, U5)
            v.wait_ge(S("s_moved"), SORT[ph])
            v.tensor_copy(idxA[:, 0:M], psum[6][:, 0:M])
            v.drain()

        def t_route(t, ph, K, NX, M):
            t_count(t, ph, NX)
            t_bounds(t, M, True, (6,))
            with t.Fori(0, NT * K // U5) as i:
                for u in range(U5):
                    t_move(t, ph, i, u, M, False, U5)
            t_bounds(t, M, False, (6,)).then_inc(S("s_moved"), 1)

        c = Carver(SCR)
        ew1 = c(2, 2 * F0)
        ew2 = c(2, 2 * F0)
        eb1 = c(2, F0 // 128)
        eb2 = c(2, D, rows=1)
        xg = c(2, D)
        gx = c(2, dt=I32)
        xgT = c(2, 2, 128)
        ht = c(2, F0)
        yo = c(2, D)

        def s_expert(s, b, M, F, w1d, b1d, w2d, b2d):
            FC = F // 128
            with s.Fori(0, M // 2) as i:
                for u in range(2):
                    e = s.value_load(gblk0[0:1, ds(i * 2 + u, 1)], min_val=0, max_val=w1d.shape[0] - 1)
                    s.wait_ge(S("m_yp"), freed(b + i, u, 2, 2))
                    s.dma_start(ew1[:, u, 0:2 * F].rearrange("p (h f) -> p h f", h=2),
                                w1d[ds(e, 1), :, :].rearrange("a (h p) f -> p (a h) f", p=128)
                                ).then_inc(S(f"m_w{u}"), 16)
                    s.dma_start(ew2[:, u, 0:2 * F], w2d[ds(e, 1), :, :].rearrange("a (p c) d -> p (a c d)", p=128)
                                ).then_inc(S(f"m_w{u}"), 16)
                    s.dma_start(eb1[:, u, 0:FC], b1d[ds(e, 1), :].rearrange("a (p c) -> p (a c)", p=128)
                                ).then_inc(S(f"m_w{u}"), 16)
                    s.dma_start(eb2[:, u, :], b2d[ds(e, 1), :]).then_inc(S(f"m_w{u}"), 16)

        def p_expert(p, b, M, hrow):
            with p.Fori(0, M // 2) as i:
                p.wait_ge(S("m_tp"), freed(b + i, 1, 2, 2))
                p.sem_inc(S("holds_waits"), 1)
                p.tensor_copy(gx[:, :], idxA[:, ds(i * 2, 2)])
                p.drain()
                for u in range(2):
                    p.indirect_dma_start(xg[:, u, :], None, hrow,
                                         bass.IndirectOffsetOnAxis(ap=gx[:, u:u + 1], axis=0)
                                         ).then_inc(S(f"m_g{u}"), 16)

        def t_expert(t, b, M, F):
            FC = F // 128
            if b == 0:
                seed(t, "m_yp", "m_tp", "m_hp", n=2)
            with t.Fori(0, M // 2) as i:
                for u in range(2):
                    t.wait_ge(S(f"m_g{u}"), gathered(b + i + 1))
                    t.wait_ge(S("m_xT"), freed(b + i, u, 2, 2))
                    for h in range(2):
                        k = t.transpose(psum[u][:, h * 128:(h + 1) * 128], xg[:, u, h * 128:(h + 1) * 128],
                                        ident[:, :])
                    k.then_inc(S("m_tp"), 1)
                for u in range(2):
                    w = ew1[:, u, 0:2 * F].rearrange("p (h q c) -> p h q c", h=2, c=FC)
                    t.wait_ge(S(f"m_w{u}"), 64 * (b + i + 1))
                    t.wait_ge(S("m_xT"), done(b + i, u, 2))
                    t.wait_ge(S("m_h"), freed(b + i, u, 2, 2))
                    for f in range(FC):
                        for h in range(2):
                            k = t.matmul(psum[2 + 2 * u + f // 4][:, (f % 4) * 128:(f % 4 + 1) * 128],
                                         w[:, h, :, f], xgT[:, u, h, :], start=(h == 0), stop=(h == 1))
                    k.then_inc(S("m_hp"), 1)
                for u in range(2):
                    t.wait_ge(S("m_h"), done(b + i, u, 2))
                    t.wait_ge(S("m_y"), freed(b + i, u, 2, 2))
                    for f in range(FC):
                        t.matmul(psum[6 + u][:, 0:D], ht[:, u, f * 128:(f + 1) * 128],
                                 ew2[:, u, f * D:(f + 1) * D], start=(f == 0), stop=False)
                    t.matmul(psum[6 + u][:, 0:D], ones[0:1, :], eb2[:, u, :], start=False, stop=True
                             ).then_inc(S("m_yp"), 1)

        def a_expert(a, b, M, F, ys):
            FC = F // 128
            if b == 0:
                seed(a, "m_xT", "m_h", n=2)
                seed(a, "m_out0", "m_out1", n=16)
            with a.Fori(0, M // 2) as i:
                for u in range(2):
                    a.wait_ge(S("m_tp"), done(b + i, u, 2))
                    a.wait_ge(S("m_hp"), freed(b + i, u, 2, 2))
                    a.copy(xgT[:, u, :, :], psum[u][:, 0:256].rearrange("p (h r) -> p h r", h=2)
                           ).then_inc(S("m_xT"), 1)
                for u in range(2):
                    a.wait_ge(S("m_hp"), done(b + i, u, 2))
                    a.wait_ge(S("m_yp"), freed(b + i, u, 2, 2))
                    for f in range(FC):
                        k = a.activation(ht[:, u, f * 128:(f + 1) * 128],
                                         psum[2 + 2 * u + f // 4][:, (f % 4) * 128:(f % 4 + 1) * 128],
                                         ACT.Relu, bias=eb1[:, u, f:f + 1])
                    k.then_inc(S("m_h"), 1)
                for u in range(2):
                    a.wait_ge(S("m_y"), done(b + i, u, 2))
                    a.dma_start(ys[ds((i * 2 + u) * 128, 128), :], yo[:, u, :]).then_inc(S(f"m_out{u}"), 16)
            for u in range(2):
                a.wait_ge(S(f"m_out{u}"), landed(b + M // 2))

        def v_expert(v, b, M):
            if b == 0:
                seed(v, "m_y", n=2)
            with v.Fori(0, M // 2) as i:
                for u in range(2):
                    v.wait_ge(S("m_yp"), done(b + i, u, 2))
                    v.wait_ge(S(f"m_out{u}"), landed(b + i))
                    v.wait_ge(consts, 1)
                    v.tensor_scalar(yo[:, u, :], psum[6 + u][:, 0:D], 1.0, None, ALU.mult
                                    ).then_inc(S("m_y"), 1)

        c = Carver(SCR)
        c.at = norm_end
        gc = c(2 * U5, rows=R, dt=I32)
        yg = c(2 * U5, D, rows=R)
        fin = c(U5, D, rows=R, dt=I32)
        nan = c(U5, D, rows=R, dt=I32)

        def back_turns(K, n):
            return NT // U5 if K > K0 and n < K0 * U5 else 0

        def p_back(p, ph, K, ys):
            with p.Fori(0, NT // U5) as i:
                p.wait_ge(S(ph + "_took"), i + 1)
                p.sem_inc(S("holds_waits"), 1)
                for k in range(K):
                    p.tensor_copy(gc[:, k * U5:(k + 1) * U5], slotI[:, ds(i * U5 + k * NT, U5)])
                p.drain()
                for n in range(K * U5):
                    p.indirect_dma_start(yg[:, n, :], None, ys,
                                         bass.IndirectOffsetOnAxis(ap=gc[:, n:n + 1], axis=0)
                                         ).then_inc(S(f"b{n}"), 16)

        def v_back0(v):
            seed(v, "m0_took", n=1)
            with v.Fori(0, NT // U5) as i:
                for u in range(U5):
                    v.wait_ge(S(f"b{u}"), gathered(i + 1))
                    v.tensor_scalar(yg[:, u, :], yg[:, u, :], gwt[:, 0, ds(i * U5 + u, 1)], None, ALU.mult)
                v.drain()
                y5 = yg[:, 0:U5, :]
                y5b = yg[:, U5:2 * U5, :]
                v.tensor_scalar(fin[:, :, :], y5, 0.0, 0.0, ALU.mult, ALU.is_equal)
                v.tensor_tensor(nan[:, :, :], y5, y5, ALU.not_equal)
                v.tensor_scalar(y5b, y5, 1e4, -1e4, ALU.min, ALU.max)
                v.drain()
                v.copy_predicated(y5b, fin[:, :, :], y5)
                v.drain()
                v.copy_predicated(y5b, nan[:, :, :], zero3)
                v.drain()
                x5 = X[:, ds(i * U5, U5), :]
                v.tensor_tensor(x5, x5, y5b, ALU.add).then_inc(S("m0_took"), 1)

        zero3 = zeros[0:R, 0:D].unsqueeze(1).broadcast_to([R, U5, D])

        def v_back1(v):
            seed(v, "m1_took", n=1)
            with v.Fori(0, NT // U5) as i:
                for k in range(2):
                    for u in range(U5):
                        xr = turn(XN[:, ds(i * U5 + u, 1), :])
                        v.wait_ge(S(f"b{k * U5 + u}"), gathered(i + 1 + back_turns(2, k * U5 + u)))
                        v.scalar_tensor_tensor(xr, yg[:, k * U5 + u, :], gwt[:, k, ds(i * U5 + u, 1)], xr,
                                               ALU.mult, ALU.add)
                    v.drain()
                v.drain().then_inc(S("m1_took"), 1)
                for u in range(U5):
                    v.bn_stats(st6[:, u, :], turn(XN[:, ds(i * U5 + u, 1), :]))
                v.drain()
                for u in range(U5):
                    k = v.bn_aggr(mv[:, u, :], st6[:, u, :])
                k.then_inc(S("x_var"), 1)
                v.wait_ge(S("x_sd"), BEFORE["fin"] + i + 1)
                v.reciprocal(rs[:, :], sd[:, :])
                v.drain()
                v.wait_ge(S("fin_out"), landed(i))
                for u in range(U5):
                    v.tensor_scalar(xs[:, u, :], turn(XN[:, ds(i * U5 + u, 1), :]), mv[:, u, 0:1],
                                    rs[:, u:u + 1], ALU.subtract, ALU.mult)
                v.drain()
                v.tensor_tensor(xs[:, :, :], xs[:, :, :], gamma1b[0:R, :].unsqueeze(1).broadcast_to([R, U5, D]), ALU.mult)
                v.drain()
                v.tensor_tensor(xs[:, :, :], xs[:, :, :], beta1b[0:R, :].unsqueeze(1).broadcast_to([R, U5, D]), ALU.add)
                v.drain()
                v.tensor_tensor(xs[:, :, :], xs[:, :, :], X[:, ds(i * U5, U5), :], ALU.add).then_inc(S("fin_y"), 1)

        def s_final(s):
            seed(s, "fin_out", n=16)
            with s.Fori(0, NT // U5) as i:
                s.wait_ge(S("fin_y"), i + 1)
                s.dma_start(tiles(out)[:, ds(i * U5, U5), :], xs[:, :, :]).then_inc(S("fin_out"), 16)
            s.wait_ge(S("fin_out"), landed(NT // U5))

        c = Carver(SCR)
        wtmp = c(2, D)
        wmean = c(2, 16)

        def v_w1(v):
            for n in range(2):
                v.tensor_tensor(wtmp[:, :, :], wfx[:, :, 0:D],
                                attb[:, n * D:(n + 1) * D].unsqueeze(1).broadcast_to([128, 2, D]), ALU.mult)
                v.drain()
                v.tensor_reduce(wfx[:, :, D + n:D + n + 1], wtmp[:, :, :], AX_X, ALU.add)
                v.drain()
            for h in range(2):
                g = wkv1[:, h, :].rearrange("p (g e) -> p g e", e=64)
                v.tensor_reduce(wmean[:, h, :], g, AX_X, ALU.add)
                v.drain()
                v.tensor_scalar(wmean[:, h, :], wmean[:, h, :], 1.0 / 64, None, ALU.mult)
                v.drain()
                v.tensor_tensor(g, g, wmean[:, h, :].unsqueeze(2).broadcast_to([128, 16, 64]), ALU.subtract)
            v.memset(Mx[:, :], LOWEST)
            v.memset(den[:, :], 0.0)
            v.memset(AGG[:, :, :], 0.0)

        c = Carver(SCR)
        c.at = norm_end
        zrow = c(U5, ROW1, rows=R)
        sq = c(2, 2 * HID, rows=R)
        K1t = c(2, HID, rows=R)
        V1t = c(2, HID, rows=R)
        ss = c(2, 16, rows=R)
        rr = c(2, 8, rows=R)
        dts = c(4, 128)
        Bm = c(4, D)

        def t_a1(t):
            seed(t, "a1_z", "a1_kp", "a1_vp", "a1_sum")
            t_bounds(t, 512, True, (5,))
            with t.Fori(0, NT // U5) as i:
                for u in range(U5):
                    t_turn(t, BEFORE["a1"], i, u)

                def sums(u):
                    t.wait_ge(S("a1_V"), done(i, u))
                    for q in range(4):
                        k = t.matmul(psum[5][:, q * 128:(q + 1) * 128], V1t[:, u % 2, q * 128:(q + 1) * 128],
                                     K1t[:, u % 2, q * 128:(q + 1) * 128], start=False, stop=False,
                                     skip_group_check=True)
                    k.then_inc(S("a1_sum"), 1)

                for u in range(U5):
                    t.wait_ge(S("x_xT"), done(BEFORE["a1"] + i, u))
                    t.wait_ge(S("a1_zr"), freed(i, u, 2))
                    for h in range(2):
                        k = t.matmul(psum[2 + 4 * (u % 2)][0:R, 0:ROW1], xT[:, u, h, :], wfx[:, h, :],
                                     start=(h == 0), stop=(h == 1))
                    k.then_inc(S("a1_z"), 1)
                    t.wait_ge(S("a1_kc"), freed(i, u, 2))
                    for h in range(2):
                        k = t.matmul(psum[3 + 4 * (u % 2)][0:R, :], xT[:, u, h, :], wkv1[:, h, 0:HID],
                                     start=(h == 0), stop=(h == 1))
                    k.then_inc(S("a1_kp"), 1)
                    t.wait_ge(S("a1_vc"), freed(i, u, 1))
                    for h in range(2):
                        k = t.matmul(psum[4][0:R, :], xT[:, u, h, :], wkv1[:, h, HID:2 * HID],
                                     start=(h == 0), stop=(h == 1))
                    k.then_inc(S("a1_vp"), 1)
                    if u:
                        sums(u - 1)
                sums(U5 - 1)
            t_bounds(t, 512, False, (5,)).then_inc(S("a1_all"), 1)
            t.wait_ge(S("a1_dts"), 1)
            for q in range(4):
                k = t.matmul(psum[6 + q // 2][:, (q % 2) * 256:(q % 2) * 256 + 256], dts[:, q, :], wout[:, q, :],
                             start=True, stop=True)
            k.then_inc(S("a1_B"), 1)
            t.wait_ge(S("a1_Bm"), 1)
            for h in range(2):
                for q in range(4):
                    k = t.matmul(psum[2][:, h * 256:(h + 1) * 256], wqo[:, q, h * 128:(h + 1) * 128], Bm[:, q, :],
                                 start=(q == 0), stop=(q == 3))
            k.then_inc(S("a1_M"), 1)

        def a_a1(a):
            seed(a, "a1_zr", "a1_kc", "a1_vc")
            with a.Fori(0, NT // U5) as i:
                a_sqrt(a, BEFORE["a1"], i)
                for u in range(U5):
                    def users():
                        a.wait_ge(S("a1_vp"), freed(i, u, U5))
                        a.wait_ge(S("a1_xkeep"), freed(i, u, U5))
                    a_turned(a, BEFORE["a1"], i, u, users)
                for u in range(U5):
                    a.wait_ge(S("a1_z"), done(i, u))
                    a.wait_ge(S(f"a_out{u}"), landed(NT // U5 + i))
                    a.wait_ge(S("a1_dcol"), i + 1)
                    a.copy(zrow[:, u, :], psum[2 + 4 * (u % 2)][0:R, 0:ROW1]).then_inc(S("a1_zr"), 1)
                    a.wait_ge(S("a1_kp"), done(i, u))
                    a.wait_ge(S("a1_ss"), freed(i, u, 2))
                    a.activation(sq[:, u % 2, 0:HID], psum[3 + 4 * (u % 2)][0:R, :], ACT.Square)
                    a.wait_ge(S("a1_sum"), freed(i, u, 2))
                    a.copy(K1t[:, u % 2, :], psum[3 + 4 * (u % 2)][0:R, :]).then_inc(S("a1_kc"), 1)
                    a.wait_ge(S("a1_vp"), done(i, u))
                    a.activation(sq[:, u % 2, HID:2 * HID], psum[4][0:R, :], ACT.Square)
                    a.copy(V1t[:, u % 2, :], psum[4][0:R, :]).then_inc(S("a1_vc"), 1)
                    a.wait_ge(S("a1_ss"), done(i, u))
                    a.activation(ss[:, u % 2, :], ss[:, u % 2, :], ACT.Sqrt, bias=eps_t[0:R, 0:1], scale=1.0 / 64
                                 ).then_inc(S("a1_sq"), 1)

        def v_a1(v):
            seed(v, "a1_ss", "a1_V")
            seed(v, "a1_dcol", n=1)
            with v.Fori(0, NT // U5) as i:
                def kept():
                    v.wait_ge(S("a1_keep"), i + 1)
                v_norm(v, BEFORE["a1"], i, kept)
                for u in range(U5):
                    v.drain()
                    v.wait_ge(S("a1_vc"), done(i, u))
                    v.tensor_reduce(ss[:, u % 2, :], sq[:, u % 2, :].rearrange("p (g e) -> p g e", e=64),
                                    AX_X, ALU.add).then_inc(S("a1_ss"), 1)
                    v.wait_ge(S("a1_sq"), i * U5 + (u + 1))
                    v.reciprocal(ss[:, u % 2, :], ss[:, u % 2, :])
                    v.drain()
                    v.tensor_tensor(rr[:, u % 2, :], ss[:, u % 2, 0:8], ss[:, u % 2, 8:16], ALU.mult)
                    v.drain()
                    v1 = V1t[:, u % 2, :].rearrange("p (g e) -> p g e", e=64)
                    v.tensor_tensor(v1, v1, rr[:, u % 2, :].unsqueeze(2).broadcast_to([R, 8, 64]), ALU.mult
                                    ).then_inc(S("a1_V"), 1)
                v.wait_ge(S("a1_zr"), done(i, U5 - 1))
                v.tensor_scalar(dcol[:, ds(i * U5, U5)], zrow[:, :, D + 1], 1.0, None, ALU.mult
                                ).then_inc(S("a1_dcol"), 1)
            v.wait_ge(S("a1_all"), 1)
            for q in range(4):
                k = v.scalar_tensor_tensor(dts[:, q, :], psum[5][:, q * 128:(q + 1) * 128], 1.0 / N, hm64[:, :],
                                           ALU.mult, ALU.mult)
            k.then_inc(S("a1_dts"), 1)
            v.wait_ge(S("a1_B"), 1)
            v.tensor_copy(Bm[:, 0:2, :], psum[6][:, :].rearrange("p (a b) -> p a b", a=2))
            v.tensor_copy(Bm[:, 2:4, :], psum[7][:, :].rearrange("p (a b) -> p a b", a=2)).then_inc(S("a1_Bm"), 1)
            v.wait_ge(S("a1_M"), 1)
            v.tensor_copy(wsm[:, :, D:2 * D], psum[2][:, :].rearrange("p (a b) -> p a b", a=2))

        def s_a1(s):
            with s.Fori(0, NT // U5) as i:
                for u in range(U5):
                    s.wait_ge(S("a1_zr"), done(i, u))
                    s.dma_start(tiles(tab1)[:, ds(i * U5 + u, 1), :].rearrange("p a d -> p (a d)"), zrow[:, u, :]
                                ).then_inc(S(f"a_out{u}"), 16)
            for u in range(U5):
                s.wait_ge(S(f"a_out{u}"), landed(2 * (NT // U5)))

        def p_a1(p):
            seed(p, "a1_xkeep")
            seed(p, "a1_keep", n=1)
            with p.Fori(0, NT // U5) as i:
                p.wait_ge(S("x_xs"), (BEFORE["a1"] + i) * U5 + U5)
                p.sem_inc(S("holds_waits"), 1)
                p.tensor_copy(XN[:, ds(i * U5, U5), :], xs[:, :, :]).then_inc(S("a1_keep"), 1)
                for u in range(U5):
                    p.wait_ge(S("x_xT"), done(BEFORE["a1"] + i, u))
                    p.wait_ge(consts, 1)
                    p.tensor_copy(xnT[:, :, ds((i * U5 + u) * R, R)], xT[:, u, :, :]).then_inc(S("a1_xkeep"), 1)

        GU = EU // GT1
        c = Carver(SCR)
        c.at = move_end
        c(2, EU // 2)
        g1 = c(EU, ROW1)
        gs = c(GU, 2)
        ohg = c(GU, 2, R)
        c.at += c.at % 2
        unb = c(GU, R)
        c.at = 0
        E1 = c(2, 256, rows=R)
        E2 = c(2, 256, rows=R)
        Pm = c(2, 256, rows=R)
        Ps = c(2, 2, R)
        gmx = c(GU, rows=R)
        t1 = c(GU, rows=R)
        mnew = c(GU, rows=R)
        bs = c(GU, 4, rows=R)
        rsc = c(GU, rows=R)

        def v1_sel(v, i, w):
            m = i * GU + w
            for k in range(2):
                v.wait_ge(S(f"e_g{2 * w + k}"), gathered(T0 // EU + i + 1))
            v.tensor_tensor(gs[:, w, :], g1[:, 2 * w:2 * w + 2, D], recT[:, ds(m * 2, 2)], ALU.add)
            v.drain()
            v.wait_ge(S("e1_dt"), freed(i, w, GU, GU))
            for k in range(2):
                key = recB[:, ds(m * 2 + k, 1)]
                v.tensor_scalar(ohg[:, w, k, :], iota[:, 1:R + 1], key, gs[:, w, k:k + 1], ALU.is_equal, ALU.mult)
                j = v.tensor_scalar(unb[:, w, :].bitcast(BF16).rearrange("p (a b) -> p a b", a=2)[:, k, :],
                                    iota[:, 1:R + 1], key, -BIG, ALU.not_equal, ALU.mult)
            j.then_inc(S("e1_sel"), 1)

        def t1_mask(t, i, w):
            t.wait_ge(S("e1_sel"), i * GU + (w + 1))
            t.wait_ge(S("e1_exp"), freed(i, w, 2, GU))
            un = unb[:, w, :].bitcast(BF16).rearrange("p (a b) -> p a b", a=2)
            for k in range(2):
                o = psum[w % 2][0:R, k * 128:(k + 1) * 128]
                t.matmul(o, ohg[:, w, k, :], ident[:, :], start=True, stop=False)
                j = t.matmul(o, un[:, k, :], identb[:, :], start=False, stop=True)
            j.then_inc(S("e1_dt"), 1)

        def v1_max(v, i, w, blk):
            M_, d_ = Mx[:, ds(blk, 1)], dcol[:, ds(blk, 1)]
            v.wait_ge(S("e1_dt"), done(i, w, GU))
            v.tensor_reduce(gmx[:, w:w + 1], psum[w % 2][0:R, 0:256], AX_X, ALU.max)
            v.drain()
            v.tensor_tensor(t1[:, w:w + 1], gmx[:, w:w + 1], d_, ALU.add)
            v.drain()
            v.scalar_tensor_tensor(t1[:, w:w + 1], t1[:, w:w + 1], 0.01, t1[:, w:w + 1], ALU.mult, ALU.max)
            v.drain()
            v.tensor_tensor(mnew[:, w:w + 1], t1[:, w:w + 1], M_, ALU.max)
            v.drain()
            v.tensor_tensor(bs[:, w, 0:1], d_, mnew[:, w:w + 1], ALU.subtract)
            v.scalar_tensor_tensor(bs[:, w, 1:2], d_, 0.01, mnew[:, w:w + 1], ALU.mult, ALU.subtract)
            v.tensor_tensor(bs[:, w, 2:3], M_, mnew[:, w:w + 1], ALU.subtract).then_inc(S("e1_max"), 1)
            v.drain()
            v.tensor_scalar(M_, mnew[:, w:w + 1], 1.0, None, ALU.mult)

        def a1_exp(a, i, w):
            a.wait_ge(S("e1_max"), i * GU + (w + 1))
            a.wait_ge(S("e1_p"), freed(i, w, 2, GU))
            a.activation(E1[:, w % 2, :], psum[w % 2][0:R, 0:256], ACT.Exp, bias=bs[:, w, 0:1])
            a.activation(E2[:, w % 2, :], psum[w % 2][0:R, 0:256], ACT.Exp, bias=bs[:, w, 1:2], scale=0.01)
            a.activation(rsc[:, w:w + 1], bs[:, w, 2:3], ACT.Exp).then_inc(S("e1_exp"), 1)

        def v1_prob(v, i, w):
            v.wait_ge(S("e1_exp"), done(i, w, GU))
            v.wait_ge(S("e1_pt"), freed(i, w, 2, GU))
            v.scalar_tensor_tensor(Pm[:, w % 2, :], E1[:, w % 2, :], 1.0, E2[:, w % 2, :], ALU.mult, ALU.max,
                                   accum_out=bs[:, w, 3:4]).then_inc(S("e1_p"), 1)

        def t1_turn(t, i, w):
            t.wait_ge(S("e1_p"), done(i, w, GU))
            t.wait_ge(S("e1_ps"), freed(i, w, 2, GU))
            for k in range(2):
                j = t.transpose(psum[2 + w % 2][:, k * 128:k * 128 + R], Pm[:, w % 2, k * 128:(k + 1) * 128],
                                ident[0:R, 0:R])
            j.then_inc(S("e1_pt"), 1)

        def a1_turned(a, i, w):
            a.wait_ge(S("e1_pt"), done(i, w, GU))
            a.wait_ge(S("e1_sum"), (freed(i, w, 2, GU)) * 2)
            a.copy(Ps[:, w % 2, :, :], psum[2 + w % 2][:, 0:256].rearrange("p (k r) -> p k r", k=2)[:, :, 0:R]
                   ).then_inc(S("e1_ps"), 1)

        def t1_sum(t, i, w):
            t.wait_ge(S("e1_ps"), done(i, w, GU))
            t.wait_ge(S("e1_acc"), freed(i, w, 2, GU))
            for k in range(2):
                t.matmul(psum[4 + w % 2][0:R, 0:D], Ps[:, w % 2, k, :], g1[:, 2 * w + k, 0:D],
                         start=(k == 0), stop=(k == 1)).then_inc(S("e1_sum"), 1)

        def v1_acc(v, i, w, blk):
            a, n_ = turn(AGG[:, ds(blk, 1), :]), den[:, ds(blk, 1)]
            v.drain()
            v.wait_ge(S("e1_sum"), done(i, w, GU) * 2)
            v.scalar_tensor_tensor(a, a, rsc[:, w:w + 1], psum[4 + w % 2][0:R, 0:D], ALU.mult, ALU.add
                                   ).then_inc(S("e1_acc"), 1)
            v.scalar_tensor_tensor(n_, n_, rsc[:, w:w + 1], bs[:, w, 3:4], ALU.mult, ALU.add)

        def v_e1(v):
            seed(v, "e1_p", "e1_acc", n=GU)
            with v.Fori(0, G1 // GU) as i:
                blk = [v.value_load(gblk1[0:1, ds(i * GU + w, 1)], min_val=0, max_val=NT - 1) for w in range(GU)]
                for w in range(GU):
                    v1_sel(v, i, w)
                for w in range(GU + 2):
                    if w < GU:
                        v1_max(v, i, w, blk[w])
                    if 1 <= w <= GU:
                        v1_prob(v, i, w - 1)
                    if w >= 2:
                        v1_acc(v, i, w - 2, blk[w - 2])

        def a_e1(a):
            seed(a, "e1_exp", "e1_ps", n=GU)
            with a.Fori(0, G1 // GU) as i:
                for w in range(GU + 1):
                    if w < GU:
                        a1_exp(a, i, w)
                    if w >= 1:
                        a1_turned(a, i, w - 1)

        def t_e1(t):
            seed(t, "e1_dt", "e1_pt", n=GU)
            t.sem_inc(S("e1_sum"), 2 * GU)
            with t.Fori(0, G1 // GU) as i:
                for w in range(2):
                    t1_mask(t, i, w)
                for w in range(GU + 1):
                    if w < GU:
                        t1_turn(t, i, w)
                    if w + 2 < GU:
                        t1_mask(t, i, w + 2)
                    if w >= 1:
                        t1_sum(t, i, w - 1)

        c = Carver(SCR)
        c(U5, D)
        xT1 = c(U5, 2, R)
        hn = c(U5, D, rows=R)
        rden = c(NT, rows=R)
        hasn = c(NT, rows=R)

        def p_c1(p):
            seed(p, "c1_x")
            with p.Fori(0, NT // U5) as i:
                for u in range(U5):
                    p.wait_ge(S("c1_p"), freed(i, u, U5))
                    p.sem_inc(S("holds_waits"), 1)
                    p.tensor_copy(xT1[:, u, :, :], xnT[:, :, ds((i * U5 + u) * R, R)]).then_inc(S("c1_x"), 1)

        def t_c1(t):
            seed(t, "c1_p")
            with t.Fori(0, NT // U5) as i:
                for u in range(U5):
                    t.wait_ge(S("c1_x"), done(i, u))
                    t.wait_ge(S("c1_d"), freed(i, u, 2))
                    for h in range(2):
                        k = t.matmul(psum[2 + u % 2][0:R, :], xT1[:, u, h, :], wsm[:, h, :],
                                     start=(h == 0), stop=(h == 1))
                    k.then_inc(S("c1_p"), 1)

        def v_c1(v):
            seed(v, "c1_d")
            v.tensor_scalar(has[:, :], den[:, :], 0.0, None, ALU.is_gt)
            v.tensor_scalar(rden[:, :], den[:, :], 1e-30, None, ALU.max)
            v.tensor_tensor(X[:, :, :], X[:, :, :], bc(boutb[0:R, :]), ALU.add)
            v.drain()
            v.reciprocal(rden[:, :], rden[:, :])
            v.tensor_scalar(hasn[:, :], has[:, :], -1.0, 1.0, ALU.mult, ALU.add)
            v.drain()
            with v.Fori(0, NT // U5) as i:
                tiles5 = ds(i * U5, U5)
                x5, xn5, agg5 = X[:, tiles5, :], XN[:, tiles5, :], AGG[:, tiles5, :]
                for u in range(U5):
                    n = ds(i * U5 + u, 1)
                    ps = psum[2 + u % 2]
                    v.wait_ge(S("c1_p"), done(i, u))
                    v.scalar_tensor_tensor(hn[:, u, :], turn(AGG[:, n, :]), rden[:, n], ps[0:R, 0:D], ALU.mult, ALU.add)
                    xr = turn(X[:, n, :])
                    v.tensor_tensor(xr, xr, ps[0:R, D:2 * D], ALU.add).then_inc(S("c1_d"), 1)
                v.drain()
                v.tensor_tensor(hn[:, :, :], hn[:, :, :], has[:, tiles5].unsqueeze(2).broadcast_to([R, U5, D]), ALU.mult)
                v.tensor_tensor(agg5, xn5, hasn[:, tiles5].unsqueeze(2).broadcast_to([R, U5, D]), ALU.mult)
                v.drain()
                v.tensor_tensor(hn[:, :, :], hn[:, :, :], agg5, ALU.add)
                v.drain()
                v.scalar_tensor_tensor(hn[:, :, :], hn[:, :, :], 0.0, xn5, ALU.max, ALU.add)
                v.drain()
                v.tensor_tensor(x5, x5, hn[:, :, :], ALU.add)
                v.drain()

        g2b, b2b, gammab, betab = vec["g2b"], vec["b2b"], vec["gammab"], vec["betab"]
        boutb, gamma1b, beta1b, attb = g2b, b2b, gammab, vec["attb"]
        gb0, gb1 = vec["gb0"], vec["gb1"]

        def halves(w):
            return w.rearrange("(h p) n -> p h n", p=128)

        def row(w):
            return w.rearrange("(a n) -> a n", a=1)

        hamilton = (("r", "i", "j", "k"), ("-i", "r", "k", "-j"), ("-j", "-k", "r", "i"), ("-k", "j", "-i", "r"))
        L0_DENSE = [(wkv[:, :, 0:D], halves(A["L0_mix_Wk"])), (wkv[:, :, D:2 * D], halves(A["L0_mix_Wv"])),
                    (wq, halves(A["L0_mix_Wq"])), (wm, halves(A["L0_mix_Wm"])), (w1, halves(A["L0_mix_W1"])),
                    (w2, halves(A["L0_mix_W2"]))]
        for a_ in range(4):
            for b_ in range(4):
                q_ = "rijk".index(hamilton[a_][b_][-1])
                L0_DENSE.append((ham[(a_ % 2) * 64:(a_ % 2) * 64 + 64, a_ // 2, b_ * 64:(b_ + 1) * 64],
                                 A["L0_gnn_weight"][:, q_ * 64:(q_ + 1) * 64]))
        W0 = len(L0_DENSE)
        L1_DENSE = [(wfx[:, :, 0:D], halves(A["L1_gnn_W_func_T"])), (wsm[:, :, 0:D], halves(A["L1_gnn_W_self_T"])),
                    (wkv1, halves(A["L1_mix_Wqkv_T"])[:, :, HID:3 * HID]), (wout, halves(A["L1_mix_Wout_T"])),
                    (wqo, halves(A["L1_mix_Wqkv"][0:HID, :]))]
        VECTORS = [(g2b, "L0_mix_g2"), (b2b, "L0_mix_b2"), (gammab, "L0_gnn_gamma"), (betab, "L0_gnn_beta"),
                   (gb0, "L0_ffn_gate_b"), (gb1, "L1_ffn_gate_b")]
        VECTORS1 = [(boutb, "L1_mix_bout"), (gamma1b, "L1_ffn_gamma"), (beta1b, "L1_ffn_beta")]
        NVEC = len(VECTORS) + 7

        @block.sync
        def _(s):
            s.dma_start(X[:, :, :], tiles(A["x"])).then_inc(x_in, 16)
            for dst, src_ap in L0_DENSE:
                s.dma_start(dst, src_ap).then_inc(w0_raw, 16)
            for dst, name in ((srcI, "src"), (dstI, "dst"), (ew, "edge_weight")):
                s.dma_start(dst[:, :], A[name].rearrange("(p c) -> p c", p=R)).then_inc(edges_in, 16)
            for dst, name in VECTORS:
                s.dma_start(dst[:, :], row(A[name]).broadcast_to([128, dst.shape[1]])).then_inc(vec_in, 16)
            s.dma_start(attb[:, :], A["L1_gnn_W_att"].broadcast_to([128, 2 * D + EDIM])).then_inc(vec_in, 16)
            for dst, name in ((g1c, "L0_mix_g1"), (b1c, "L0_mix_b1")):
                for h in range(2):
                    s.dma_start(dst[:, h:h + 1], A[name][h * 128:(h + 1) * 128].rearrange("(p a) -> p a", a=1)
                                ).then_inc(vec_in, 16)
            s.dma_start(gw0[:, :, :], halves(A["L0_ffn_gate_w"])).then_inc(vec_in, 16)
            s.dma_start(gw1[:, :, :], halves(A["L1_ffn_gate_w"])).then_inc(vec_in, 16)
            s_a0(s)
            barrier(s, "sp")
            barrier(s, "sp")
            for dst, src_ap in L1_DENSE:
                s.dma_start(dst, src_ap).then_inc(S("w1_in"), 16)
            barrier(s, "sp")
            s_te(s)
            barrier(s, "sp")
            barrier(s, "sp")
            for dst, name in VECTORS1:
                s.dma_start(dst[:, :], row(A[name]).broadcast_to([128, dst.shape[1]])).then_inc(S("L1_vectors_in"), 16)
            s_gate(s, "g0", hrow0)
            barrier(s, "sp")
            s_expert(s, 0, M0, F0, A["L0_ffn_w1"], A["L0_ffn_b1"], A["L0_ffn_w2"], A["L0_ffn_b2"])
            barrier(s, "sp")
            barrier(s, "sp")
            s_a1(s)
            barrier(s, "sp")
            barrier(s, "sp")
            barrier(s, "sp")
            s_gate(s, "g1", hrow1)
            barrier(s, "sp")
            s_expert(s, M0 // 2, M1, F1, A["L1_ffn_w1"], A["L1_ffn_b1"], A["L1_ffn_w2"], A["L1_ffn_b2"])
            barrier(s, "sp")
            s_final(s)

        @block.gpsimd
        def _(p):
            p.iota(iotaI[:, :], [[1, MAXG]], base=0, channel_multiplier=0)
            p.iota(nodeI[:, :], [[1, NT]], base=0, channel_multiplier=NT)
            p.memset(ident[:, :], 0.0)
            p.memset(ones[:, :], 1.0)
            p.memset(tri[:, :], 1.0)
            p.memset(zeros[:, :], 0.0)
            p.memset(hm32[:, :], 0.0)
            p.memset(hm64[:, :], 0.0)
            p.memset(eps_t[:, :], EPS)
            p.memset(AGG[:, :, :], 0.0)
            p.drain()
            p.affine_select(out=ident[:, :], in_=ident[:, :], compare_op=ALU.not_equal, fill=1.0, base=0,
                            pattern=[[-1, 128]], channel_multiplier=1)
            p.affine_select(out=tri[:, :], in_=tri[:, :], compare_op=ALU.is_gt, fill=0.0, base=0,
                            pattern=[[1, 128]], channel_multiplier=-1)
            p.drain().then_inc(consts, 1)
            p_a0(p)
            barrier(p, "pool")
            barrier(p, "pool")
            barrier(p, "pool")
            with p.Fori(0, T0 // EU) as i:
                p_gather(p, "e0", 0, i, idxA, tab0, g0)
            barrier(p, "pool")
            barrier(p, "pool")
            barrier(p, "pool")
            p_expert(p, 0, M0, hrow0)
            barrier(p, "pool")
            p_back(p, "m0", 1, ys0)
            barrier(p, "pool")
            p_a1(p)
            barrier(p, "pool")
            with p.Fori(0, T1 // EU) as i:
                p_gather(p, "e1", T0 // EU, i, idxB, tab1, g1)
            barrier(p, "pool")
            p_c1(p)
            barrier(p, "pool")
            p_keep(p, "g1")
            barrier(p, "pool")
            p_expert(p, M0 // 2, M1, hrow1)
            barrier(p, "pool")
            p_back(p, "m1", 2, ys1)

        @block.vector
        def _(v):
            v.wait_ge(consts, 1)
            v.tensor_copy(iota[:, :], iotaI[:, :])
            v.tensor_copy(node[:, :], nodeI[:, :])
            v.tensor_copy(identb[:, :], ident[:, :])
            for k in range(4):
                v.memset(hm32[k * 32:(k + 1) * 32, k * 32:(k + 1) * 32], 1.0)
            for k in range(2):
                v.memset(hm64[k * 64:(k + 1) * 64, k * 64:(k + 1) * 64], 1.0)
            v.wait_ge(w0_raw, 16 * W0)
            for a_ in range(4):
                for b_ in range(4):
                    if hamilton[a_][b_][0] == "-":
                        h_ = ham[(a_ % 2) * 64:(a_ % 2) * 64 + 64, a_ // 2, b_ * 64:(b_ + 1) * 64]
                        v.tensor_scalar(h_, h_, -1.0, None, ALU.mult)
            v.drain().then_inc(consts, 2)
            v.wait_ge(x_in, 16)
            v_a0(v)
            barrier(v, "dve")
            v.wait_ge(vec_in, 16 * NVEC)
            v_kv(v)
            v.drain().then_inc(S("b0_kvbd"), 1)
            v_b0(v)
            barrier(v, "dve")
            v.wait_ge(edges_in, 48)
            v_keys(v, srcI, dstI)
            v_count(v, "s0", EC, NT)
            v_place(v, "s0", EC, NT, GT0, G0, gblk0)
            with v.Fori(0, CE) as i:
                for u in range(EU):
                    v_onehot(v, "s0", i, u, ew, T0)
            v.wait_ge(S("s_moved"), 1)
            v_records(v, T0, recA, idxA, recW)
            barrier(v, "dve")
            v_te(v)
            v.drain()
            v_keys(v, dstI, srcI)
            v_count(v, "s1", EC, NT)
            v_place(v, "s1", EC, NT, GT1, G1, gblk1)
            seed(v, "e0_acc", n=EU)

            def e0_turn(i, sort):
                for u in range(EU):
                    v_sel0(v, i, u)
                    if sort:
                        v_onehot(v, "s1", i, u, te, T1)
                blks = [v.value_load(gblk0[0:1, ds(i * EU + u, 1)], min_val=0, max_val=NT - 1) for u in range(EU)]
                for u in range(EU):
                    v_acc0(v, i, u, blks[u])

            with v.Fori(0, CE) as i:
                e0_turn(i, True)
            with v.Fori(CE, T0 // EU) as i:
                e0_turn(i, False)
            v.wait_ge(S("s_moved"), 2)
            v_records(v, T1, recB, idxB, recT)
            v.drain()
            barrier(v, "dve")
            v_bn(v)
            barrier(v, "dve")
            v_gate(v, "g0", gb0, X0, False)
            v.drain()
            v_choose(v, "g0", X0, K0)
            v_route(v, "r0", K0, X0, M0)
            barrier(v, "dve")
            v_expert(v, 0, M0)
            barrier(v, "dve")
            v_back0(v)
            v.wait_ge(S("w1_in"), 16 * len(L1_DENSE))
            v.wait_ge(S("L1_vectors_in"), 16 * len(VECTORS1))
            v_w1(v)
            barrier(v, "dve")
            v_a1(v)
            barrier(v, "dve")
            v_e1(v)
            barrier(v, "dve")
            v_c1(v)
            barrier(v, "dve")
            v_gate(v, "g1", gb1, X1, True)
            v.drain()
            v_choose(v, "g1", X1, K1)
            v_route(v, "r1", K1, X1, M1)
            barrier(v, "dve")
            v_expert(v, M0 // 2, M1)
            barrier(v, "dve")
            v_back1(v)

        @block.scalar
        def _(a):
            a.wait_ge(consts, 3)
            a_a0(a)
            barrier(a, "act")
            a_b0(a)
            barrier(a, "act")
            barrier(a, "act")
            barrier(a, "act")
            a_bn(a)
            barrier(a, "act")
            a_gate(a, "g0")
            a_choose(a, "g0", X0, K0)
            barrier(a, "act")
            a_expert(a, 0, M0, F0, ys0)
            barrier(a, "act")
            barrier(a, "act")
            a_a1(a)
            barrier(a, "act")
            a_e1(a)
            barrier(a, "act")
            barrier(a, "act")
            a_gate(a, "g1")
            a_choose(a, "g1", X1, K1)
            barrier(a, "act")
            a_expert(a, M0 // 2, M1, F1, ys1)
            barrier(a, "act")
            with a.Fori(0, NT // U5) as i:
                a_sqrt(a, BEFORE["fin"], i)

        @block.tensor
        def _(t):
            t_a0(t)
            barrier(t, "pe")
            t.wait_ge(S("b0_kvbd"), 1)
            t_b0(t)
            barrier(t, "pe")
            t_count(t, "s0", NT)
            seed(t, "s_used", n=EU)
            t_bounds(t, T0, True)
            with t.Fori(0, CE) as i:
                for u in range(EU):
                    t_move(t, "s0", i, u, T0)
            t_bounds(t, T0, False).then_inc(S("s_moved"), 1)
            barrier(t, "pe")
            t_count(t, "s1", NT)
            seed(t, "e0_sum", n=EU)
            t_bounds(t, T1, True)
            with t.Fori(0, CE) as i:
                for u in range(EU):
                    t_e0(t, i, u)
                    t_move(t, "s1", i, u, T1)
            with t.Fori(CE, T0 // EU) as i:
                for u in range(EU):
                    t_e0(t, i, u)
            t_bounds(t, T1, False).then_inc(S("s_moved"), 1)
            barrier(t, "pe")
            t_bn(t, AGG, 0, "bn_agg", "bn_sum")
            t_bn(t, bnm, 1, "bn_sq", "bn_ssq")
            barrier(t, "pe")
            t_gate(t, "g0", gw0, X0)
            t_route(t, "r0", K0, X0, M0)
            barrier(t, "pe")
            t_expert(t, 0, M0, F0)
            barrier(t, "pe")
            barrier(t, "pe")
            t_a1(t)
            barrier(t, "pe")
            t_e1(t)
            barrier(t, "pe")
            t_c1(t)
            barrier(t, "pe")
            t_gate(t, "g1", gw1, X1)
            t_route(t, "r1", K1, X1, M1)
            barrier(t, "pe")
            t_expert(t, M0 // 2, M1, F1)
            barrier(t, "pe")


_INS = ("x", "src", "dst", "edge_attr_64", "edge_weight", "L0_gnn_weight", "L0_gnn_gamma", "L0_gnn_beta",
        "L0_mix_Wq", "L0_mix_Wk", "L0_mix_Wv", "L0_mix_Wm", "L0_mix_W1", "L0_mix_W2", "L0_mix_g1", "L0_mix_b1",
        "L0_mix_g2", "L0_mix_b2", "L0_ffn_gate_w", "L0_ffn_gate_b", "L0_ffn_w1", "L0_ffn_b1", "L0_ffn_w2",
        "L0_ffn_b2", "L1_gnn_W_self", "L1_gnn_W_func", "L1_gnn_W_att", "L1_mix_Wqkv", "L1_mix_Wout",
        "L1_mix_bout", "L1_ffn_gate_w", "L1_ffn_gate_b", "L1_ffn_w1", "L1_ffn_b1", "L1_ffn_w2", "L1_ffn_b2",
        "L1_ffn_gamma", "L1_ffn_beta")
_TURNED = ("L1_gnn_W_func", "L1_gnn_W_self", "L1_mix_Wqkv", "L1_mix_Wout")


def kernel(**inputs):
    import numpy as _np
    import concourse.bacc as _bacc
    from concourse import mybir as _mybir
    from concourse.bass_utils import run_bass_kernel_spmd as _run

    laid = {n: _np.ascontiguousarray(inputs[n]) for n in _INS}
    for n in _TURNED:
        laid[n + "_T"] = _np.ascontiguousarray(_np.transpose(laid[n]))
    for n in ("L1_gnn_W_func", "L1_gnn_W_self", "L1_mix_Wout"):
        del laid[n]
    nc = _bacc.Bacc("TRN2", target_bir_lowering=False, num_devices=1)
    arrays, A = {}, {}
    for n, a in laid.items():
        arrays["in_" + n] = a
        A[n] = nc.dram_tensor("in_" + n, a.shape, _mybir.dt.from_np(a.dtype), kind="ExternalInput").ap()
    out = nc.dram_tensor("out", (N, D), F32, kind="ExternalOutput").ap()
    gps_kernel(nc, A, out)
    r = _run(nc, [arrays], core_ids=[0])
    return r.results[0]["out"]
```

```python
from contextlib import ExitStack

import concourse.bass as bass
from concourse import mybir

ALU = mybir.AluOpType
ACT = mybir.ActivationFunctionType
F32 = mybir.dt.float32
BF16 = mybir.dt.bfloat16
I32 = mybir.dt.int32
AX_X = mybir.AxisListType.X
ds = bass.ds

N, D = 3125, 256
NT = 25
R = N // NT
E = 50000
EC = E // R
HID = 512
EDIM = 64
U5 = 5
EPS = 1e-5
BIG = 1e30
LOWEST = -1e20
TOKS = ((0, 2), (2, 3))

GT0, GT1 = 1, 2
EU = 16


def slots(count, blocks, gt):
    size = 128 * gt
    return (count + blocks * (size - 1)) // size


G0 = -(-slots(E, NT, GT0) // EU) * EU
G1 = -(-slots(E, NT, GT1) * GT1 // EU) * EU // GT1
T0, T1 = G0 * GT0, G1 * GT1
ROW1 = D + 2

X0, F0, K0 = 8, 1024, 1
X1, F1, K1 = 16, 512, 2
CAP = -(-5 * N // (4 * X0))
M0, M1 = slots(N * K0, X0, 1), slots(N * K1, X1, 1)
MAXG = max(G0, G1, T0, T1, 128)
SH = 8
SC = EC // (2 * SH)


def even(n):
    return n + n % 2


M0, M1 = even(M0), even(M1)


def done(i, u, per=U5):
    return i * per + (u + 1 + per)


def freed(i, u, bufs, per=U5):
    before = u - bufs if u >= bufs else max(w for w in range(per) if w % bufs == u % bufs) - per
    return i * per + (before + 1 + per)


def landed(turns):
    return 16 * (turns + 1)


def gathered(turns):
    return 16 * turns


def gps_kernel(nc, A, out):
    ctx = ExitStack()
    with ctx:
        def sb(name, shape, dt=F32):
            return ctx.enter_context(nc.sbuf_tensor(name, shape, dt))

        def sem(name):
            return ctx.enter_context(nc.semaphore(name))

        X = sb("X", [R, NT, D])
        AGG = sb("AGG", [R, NT, D])
        XN = sb("XN", [R, NT, D])
        xnT = sb("xnT", [128, 2, N])
        WD = sb("WD", [128, 5636])
        SCR = sb("SCR", [128, 12320])
        iota = sb("iota", [128, MAXG])
        ident = sb("ident", [128, 128])
        identb = sb("identb", [128, 128], BF16)
        ones = sb("ones", [128, 128])
        tri = sb("tri", [128, 128])
        zeros = sb("zeros", [128, 512])
        node = sb("node", [R, NT])
        hm32 = sb("hm32", [128, 128])
        hm64 = sb("hm64", [128, 128])
        eps_t = sb("eps_t", [128, 1])
        srcI = sb("srcI", [R, EC], I32)
        dstI = sb("dstI", [R, EC], I32)
        rec = sb("rec", [R, EC, 3])
        place = sb("place", [R, EC], I32)
        recS = sb("recS", [R, 2, SH, 3])
        placeS = sb("placeS", [R, 2, SH], I32)
        slots_ = sb("slots", [128, T1, 3])
        gblk0 = sb("gblk0", [128, G0], I32)
        gblk1 = sb("gblk1", [128, G1], I32)
        st6 = sb("st6", [R, U5, 6])
        mv = sb("mv", [R, U5, 2])
        sd = sb("sd", [R, U5])
        rs = sb("rs", [R, U5])
        gwt = sb("gwt", [R, 2, NT])
        slotI = sb("slotI", [R, 2 * NT], I32)
        idxX = sb("idxX", [128, M1], I32)

        psum = [ctx.enter_context(nc.psum_tensor(f"bank{b}", [128, 512], F32)) for b in range(8)]

        class Carver:
            def __init__(self, t):
                self.t, self.at = t, 0

            def __call__(self, *shape, rows=128, dt=F32):
                n = 1
                for k in shape:
                    n *= k
                v = self.t[0:rows, self.at:self.at + n]
                self.at += n
                assert self.at <= self.t.shape[1], (self.at, shape)
                if dt is not F32:
                    v = v.bitcast(dt)
                if len(shape) == 2:
                    v = v.rearrange("p (a b) -> p a b", a=shape[0])
                if len(shape) == 3:
                    v = v.rearrange("p (a b c) -> p a b c", a=shape[0], b=shape[1])
                return v

        c = Carver(SCR)
        iotaI = c(MAXG, dt=I32)
        nodeI = c(NT, rows=R, dt=I32)

        dram = lambda name, shape: nc.dram_tensor(name, shape, F32, kind="Internal").ap()
        tab0 = dram("tab0", [N, D])
        tab1 = dram("tab1", [N, ROW1])
        slot0 = dram("slot0", [128 * T0, 3])
        slot1 = dram("slot1", [128 * T1, 3])
        hrow0 = dram("hrow0", [N, D])
        hrow1 = dram("hrow1", [N, D])
        ys0 = dram("ys0", [M0 * 128, D])
        ys1 = dram("ys1", [M1 * 128, D])

        def tiles(t):
            return t.rearrange("(p j) d -> p j d", j=NT)

        c = Carver(WD)
        wkv = c(2, 2 * D)
        ham = c(2, D)
        wq = c(2, D)
        wm = c(2, D)
        w1 = c(4, HID)
        w2 = c(4, D)
        c = Carver(WD)
        wfx = c(2, ROW1)
        wsm = c(2, 2 * D)
        wkv1 = c(2, 2 * HID)
        wout = c(4, D)
        wqo = c(4, D)

        vec = {n: sb(n, [128, w]) for n, w in (
            ("g2b", D), ("b2b", D), ("gammab", D), ("betab", D),
            ("attb", 2 * D + EDIM), ("gb0", X0), ("gb1", X1))}
        gw0 = sb("gw0", [128, 2, X0])
        gw1 = sb("gw1", [128, 2, X1])
        LG = sb("LG", [R, NT, X1])
        dm = sb("dm", [R, NT, 3])
        den = sb("den", [R, NT])
        has = sb("has", [R, NT])
        g1c = sb("g1c", [128, 2])
        b1c = sb("b1c", [128, 2])

        bar = sem("all_engines_here")
        consts = sem("constants_ready")
        x_in = sem("x_in")
        edges_in = sem("edges_in")
        w0_raw = sem("L0_dense_weights_in")
        vec_in = sem("L0_vectors_in")
        step = {}

        def S(name):
            if name not in step:
                step[name] = sem(name)
            return step[name]

        block = ctx.enter_context(nc.Block())
        barriers = {}

        def barrier(eng, key):
            barriers[key] = barriers.get(key, 0) + 1
            eng.drain().then_inc(bar, 1)
            eng.wait_ge(bar, 5 * barriers[key])


        def turn(ap):
            return ap.rearrange("p a d -> p (a d)")

        c = Carver(SCR)
        xs = c(U5, D, rows=R)
        xT = c(U5, 2, R)
        norm_end = c.at

        BEFORE = {ph: n * (NT // U5) for n, ph in enumerate(("a0", "g0", "a1", "g1", "fin"))}

        def v_norm(v, b, i, kept):
            for u in range(U5):
                v.bn_stats(st6[:, u, :], turn(X[:, ds(i * U5 + u, 1), :]))
            v.drain()
            for u in range(U5):
                k = v.bn_aggr(mv[:, u, :], st6[:, u, :])
            k.then_inc(S("x_var"), 1)
            v.wait_ge(S("x_sd"), b + i + 1)
            v.reciprocal(rs[:, :], sd[:, :])
            v.drain()
            v.wait_ge(S("x_turned"), freed(b + i, U5 - 1, U5))
            kept()
            for u in range(U5):
                v.tensor_scalar(xs[:, u, :], turn(X[:, ds(i * U5 + u, 1), :]), mv[:, u, 0:1],
                                rs[:, u:u + 1], ALU.subtract, ALU.mult).then_inc(S("x_xs"), 1)

        def a_sqrt(a, b, i):
            a.wait_ge(S("x_var"), b + i + 1)
            a.activation(sd[:, :], mv[:, :, 1], ACT.Sqrt, bias=eps_t[0:R, 0:1]).then_inc(S("x_sd"), 1)

        def half(u):
            return psum[u % 2][:, 0:256].rearrange("p (h r) -> p h r", h=2)

        def t_turn(t, b, i, u):
            t.wait_ge(S("x_xs"), (b + i) * U5 + (u + 1))
            t.wait_ge(S("x_xT"), freed(b + i, u, 2))
            for h in range(2):
                k = t.transpose(half(u)[:, h, 0:R], xs[:, u, h * 128:(h + 1) * 128], ident[0:R, 0:R])
            k.then_inc(S("x_turned"), 1)

        def a_turned(a, b, i, u, users):
            a.wait_ge(S("x_turned"), done(b + i, u))
            users()
            a.copy(xT[:, u, :, :], half(u)[:, :, 0:R]).then_inc(S("x_xT"), 1)

        def seed(eng, *names, n=U5):
            for name in names:
                eng.sem_inc(S(name), n)

        c = Carver(SCR)
        c.at = norm_end
        ek = c(U5, D, rows=R)
        Kt = c(U5, D, rows=R)
        Vt = c(U5, 2, 129, rows=R)
        sup = c(U5, D, rows=R)

        def t_a0(t):
            seed(t, "x_turned", "a0_kv", "a0_sup", "a0_KV")
            t.wait_ge(consts, 3)
            t_bounds(t, 258, True, (4,))
            with t.Fori(0, NT // U5) as i:
                for u in range(U5):
                    t_turn(t, 0, i, u)

                def sums(u):
                    t.wait_ge(S("a0_K"), done(i, u))
                    t.wait_ge(S("a0_V"), done(i, u))
                    for h in range(2):
                        k = t.matmul(psum[4][:, h * 129:(h + 1) * 129], Kt[:, u, h * 128:(h + 1) * 128], Vt[:, u, h, :],
                                     start=False, stop=False, skip_group_check=True)
                    k.then_inc(S("a0_KV"), 1)

                for u in range(U5):
                    t.wait_ge(S("x_xT"), done(i, u))
                    t.wait_ge(S("a0_K"), freed(i, u, 2))
                    for h in range(2):
                        k = t.matmul(psum[2 + u % 2][0:R, :], xT[:, u, h, :], wkv[:, h, :],
                                     start=(h == 0), stop=(h == 1))
                    k.then_inc(S("a0_kv"), 1)
                    t.wait_ge(S("a0_supc"), freed(i, u, 2))
                    for h in range(2):
                        k = t.matmul(psum[5 + u % 2][0:R, 0:D], xT[:, u, h, :], ham[:, h, :],
                                     start=(h == 0), stop=(h == 1))
                    k.then_inc(S("a0_sup"), 1)
                    if u:
                        sums(u - 1)
                sums(U5 - 1)
            t_bounds(t, 258, False, (4,))

        def a_a0(a):
            seed(a, "x_xT", "a0_V", "a0_ek")
            with a.Fori(0, NT // U5) as i:
                a_sqrt(a, 0, i)
                for u in range(U5):
                    def users():
                        a.wait_ge(S("a0_sup"), freed(i, u, U5))
                        a.wait_ge(S("a0_xkeep"), freed(i, u, U5))
                    a_turned(a, 0, i, u, users)
                for u in range(U5):
                    a.wait_ge(S("a0_kv"), done(i, u))
                    a.wait_ge(S("a0_K"), freed(i, u, U5))
                    a.activation(ek[:, u, :], psum[2 + u % 2][0:R, 0:D], ACT.Exp).then_inc(S("a0_ek"), 1)
                    a.wait_ge(S("a0_KV"), freed(i, u, U5))
                    a.copy(Vt[:, u, :, 0:128], psum[2 + u % 2][0:R, D:2 * D].rearrange("p (h f) -> p h f", h=2)
                           ).then_inc(S("a0_V"), 1)

        def p_a0(p):
            seed(p, "a0_xkeep")
            with p.Fori(0, NT // U5) as i:
                for u in range(U5):
                    p.wait_ge(S("x_xT"), done(i, u))
                    p.wait_ge(consts, 1)
                    p.tensor_copy(xnT[:, :, ds((i * U5 + u) * R, R)], xT[:, u, :, :]).then_inc(S("a0_xkeep"), 1)

        def v_a0(v):
            seed(v, "a0_K", "a0_supc")
            v.memset(Vt[:, :, :, 128:129].rearrange("p u h o -> p (u h) o"), 1.0)
            with v.Fori(0, NT // U5) as i:
                v_norm(v, 0, i, lambda: None)
                v.drain()
                x5 = X[:, ds(i * U5, U5), :]
                v.tensor_tensor(x5, x5, xs[:, :, :], ALU.add)
                for u in range(U5):
                    v.wait_ge(S("a0_ek"), done(i, u))
                    v.tensor_scalar(ek[:, u, :], ek[:, u, :], 1.0, None, ALU.min)
                    v.drain()
                    v.wait_ge(S("a0_KV"), freed(i, u, U5))
                    v.wait_ge(S("a0_V"), done(i, u))
                    v.scalar_tensor_tensor(Kt[:, u, :], psum[2 + u % 2][0:R, 0:D], 0.0, ek[:, u, :],
                                           ALU.max, ALU.add).then_inc(S("a0_K"), 1)
                    v.wait_ge(S("a0_sup"), done(i, u))
                    v.wait_ge(S(f"a_out{u}"), landed(i))
                    v.wait_ge(consts, 1)
                    v.tensor_copy(sup[:, u, :], psum[5 + u % 2][0:R, 0:D]).then_inc(S("a0_supc"), 1)

        def s_a0(s):
            seed(s, *(f"a_out{u}" for u in range(U5)), n=16)
            with s.Fori(0, NT // U5) as i:
                for u in range(U5):
                    s.wait_ge(S("a0_supc"), done(i, u))
                    s.dma_start(tiles(tab0)[:, ds(i * U5 + u, 1), :].rearrange("p a d -> p (a d)"), sup[:, u, :]
                                ).then_inc(S(f"a_out{u}"), 16)
            for u in range(U5):
                s.wait_ge(S(f"a_out{u}"), landed(NT // U5))

        c = Carver(SCR)
        kvbd = c(2, 128)
        ksx = c(2, 128)
        WMAX = 3 * R
        eq = c(2, WMAX)
        QT = c(2, WMAX)
        dn = c(WMAX)
        msgT = c(2, WMAX)
        mn = c(3, D, rows=R)
        mT = c(2, WMAX)
        hT = c(4, WMAX)
        yr = c(3, D, rows=R)

        def v_kv(v):
            for h in range(2):
                v.scalar_tensor_tensor(kvbd[:, h, :], psum[4][:, h * 129:h * 129 + 128], 1.0 / N, hm32[:, :], ALU.mult, ALU.mult)
                v.tensor_scalar(ksx[:, h, :], hm32[:, :], psum[4][:, h * 129 + 128:h * 129 + 129], None, ALU.mult)

        def row_ps(k):
            return psum[4 + k // 2][0:R, (k % 2) * 256:(k % 2) * 256 + 256]

        def t_b0(t):
            with t.Fori(0, NT // U5) as i:
                for r, (t0, nt) in enumerate(TOKS):
                    n, w = i * 2 + r, nt * R
                    cols = ds((i * U5 + t0) * R, w)
                    for f in range(2):
                        for h in range(2):
                            k = t.matmul(psum[f][:, 0:w], wq[:, h, f * 128:(f + 1) * 128], xnT[:, h, cols],
                                         start=(h == 0), stop=(h == 1))
                    k.then_inc(S("b0_q"), 1)
                    for h in range(2):
                        t.wait_ge(S("b0_Q"), n + 1)
                        t.wait_ge(S("b0_msg"), n * 2 + (h + 2))
                        t.matmul(psum[2][:, 0:w], kvbd[:, h, :], QT[:, h, 0:w], start=True, stop=True)
                        t.matmul(psum[3][:, 0:w], ksx[:, h, :], QT[:, h, 0:w], start=True, stop=True
                                 ).then_inc(S("b0_nd"), 1)
                    t.wait_ge(S("b0_msg"), n * 2 + 4)
                    t.wait_ge(S("b0_x"), n + 1)
                    for j in range(nt):
                        for h in range(2):
                            k = t.matmul(row_ps(j), msgT[:, h, j * R:(j + 1) * R], wm[:, h, :],
                                         start=(h == 0), stop=(h == 1))
                    k.then_inc(S("b0_m"), 1)
                    t.wait_ge(S("b0_mn"), n + 1)
                    for h in range(2):
                        for j in range(nt):
                            k = t.transpose(psum[h][:, j * R:(j + 1) * R], mn[:, j, h * 128:(h + 1) * 128],
                                            ident[0:R, 0:R])
                    k.then_inc(S("b0_mt"), 1)
                    t.wait_ge(S("b0_mT"), n + 1)
                    for f in range(4):
                        t.wait_ge(S("b0_h"), n * 4 + (f + 2))
                        for h in range(4):
                            src_t = xnT[:, h, cols] if h < 2 else mT[:, h - 2, 0:w]
                            k = t.matmul(psum[6 + f % 2][:, 0:w], w1[:, h, f * 128:(f + 1) * 128], src_t,
                                         start=(h == 0), stop=(h == 3))
                        k.then_inc(S("b0_hp"), 1)
                    t.wait_ge(S("b0_h"), n * 4 + 7)
                    for j in range(nt):
                        for f in range(4):
                            k = t.matmul(row_ps(j), hT[:, f, j * R:(j + 1) * R], w2[:, f, :],
                                         start=(f == 0), stop=(f == 3))
                    k.then_inc(S("b0_y"), 1)

        def a_b0(a):
            a.sem_inc(S("b0_h"), 3)
            with a.Fori(0, NT // U5) as i:
                for r, (t0, nt) in enumerate(TOKS):
                    n, w = i * 2 + r, nt * R
                    a.wait_ge(S("b0_q"), n + 1)
                    for f in range(2):
                        a.activation(eq[:, f, 0:w], psum[f][:, 0:w], ACT.Exp).then_inc(S("b0_eq"), 1)
                    a.wait_ge(S("b0_var1"), n + 1)
                    a.activation(sd[:, 0:nt], mv[:, 0:nt, 1], ACT.Sqrt, bias=eps_t[0:R, 0:1]).then_inc(S("b0_sd1"), 1)
                    a.wait_ge(S("b0_mt"), n + 1)
                    for h in range(2):
                        k = a.activation(mT[:, h, 0:w], psum[h][:, 0:w], ACT.Identity, bias=b1c[:, h:h + 1],
                                         scale=g1c[:, h:h + 1])
                    k.then_inc(S("b0_mT"), 1)
                    for f in range(4):
                        a.wait_ge(S("b0_hp"), n * 4 + (f + 1))
                        a.activation(hT[:, f, 0:w], psum[6 + f % 2][:, 0:w], ACT.Relu).then_inc(S("b0_h"), 1)
                    a.wait_ge(S("b0_var2"), n + 1)
                    a.activation(sd[:, 0:nt], mv[:, 0:nt, 1], ACT.Sqrt, bias=eps_t[0:R, 0:1]).then_inc(S("b0_sd2"), 1)

        def v_rows_norm(v, nt, ps, dst, var, sdn, n, free):
            for j in range(nt):
                v.bn_stats(st6[:, j, :], ps(j))
            v.drain()
            for j in range(nt):
                k = v.bn_aggr(mv[:, j, :], st6[:, j, :])
            k.then_inc(S(var), 1)
            v.wait_ge(S(sdn), n + 1)
            v.reciprocal(rs[:, 0:nt], sd[:, 0:nt])
            v.drain()
            free()
            for j in range(nt):
                k = v.tensor_scalar(dst[:, j, :], ps(j), mv[:, j, 0:1], rs[:, j:j + 1], ALU.subtract, ALU.mult)
            return k

        def v_b0(v):
            seed(v, "b0_x", n=1)
            seed(v, "b0_msg", n=2)
            with v.Fori(0, NT // U5) as i:
                for r, (t0, nt) in enumerate(TOKS):
                    n, w = i * 2 + r, nt * R
                    v.wait_ge(S("b0_eq"), n * 2 + 2)
                    v.tensor_scalar(eq[:, :, 0:w], eq[:, :, 0:w], 1.0, None, ALU.min)
                    v.drain()
                    for f in range(2):
                        k = v.scalar_tensor_tensor(QT[:, f, 0:w], psum[f][:, 0:w], 0.0, eq[:, f, 0:w],
                                                   ALU.max, ALU.add)
                    k.then_inc(S("b0_Q"), 1)
                    for h in range(2):
                        v.wait_ge(S("b0_nd"), n * 2 + (h + 1))
                        v.tensor_scalar(dn[:, 0:w], psum[3][:, 0:w], 1e-6, None, ALU.add)
                        v.drain()
                        v.reciprocal(dn[:, 0:w], dn[:, 0:w])
                        v.drain()
                        v.scalar_tensor_tensor(msgT[:, h, 0:w], psum[2][:, 0:w], float(N), dn[:, 0:w],
                                               ALU.mult, ALU.mult).then_inc(S("b0_msg"), 1)
                    v.wait_ge(S("b0_m"), n + 1)
                    v.wait_ge(consts, 1)
                    v_rows_norm(v, nt, row_ps, mn, "b0_var1", "b0_sd1", n, lambda: None).then_inc(S("b0_mn"), 1)
                    v.wait_ge(S("b0_y"), n + 1)
                    v.wait_ge(consts, 1)
                    v_rows_norm(v, nt, row_ps, yr, "b0_var2", "b0_sd2", n, lambda: None).then_inc(S("b0_x"), 1)
                    v.drain()
                    g = g2b[0:R, :].unsqueeze(1).broadcast_to([R, nt, D])
                    v.tensor_tensor(yr[:, 0:nt, :], yr[:, 0:nt, :], g, ALU.mult)
                    v.drain()
                    xr = X[:, ds(i * U5 + t0, nt), :]
                    v.tensor_tensor(xr, xr, yr[:, 0:nt, :], ALU.add)
                    v.drain()
                    v.tensor_tensor(xr, xr, b2b[0:R, :].unsqueeze(1).broadcast_to([R, nt, D]), ALU.add)

        c = Carver(SCR)
        blkF = c(EC, rows=R)
        loI = c(EC, rows=R, dt=I32)
        inb = c(EC, rows=R)
        run = c(EC, rows=R)
        pos = c(EC, rows=R)
        bsum = c(EC, rows=R)
        posI = c(EC, rows=R, dt=I32)
        tI = loI
        one_row = c(EC, rows=R)
        tF = c(EC, rows=R)
        qF = c(EC, rows=R)
        packed = c(2 * NT, rows=R)
        cnt = c(NT, rows=R)
        ngI = c(NT, dt=I32)
        ngF = c(NT)
        cum = c(NT)
        base = c(NT)
        offs = c(NT, rows=R)
        gbF = c(MAXG)
        sort_end = c.at
        SORT = {"s0": 1, "s1": 2, "r0": 3, "r1": 4}
        MOVED = {"r0": 0, "r1": K0 * NT}

        def v_keys(v, keyI, idxI):
            v.tensor_scalar(loI[:, :], keyI[:, :], 1311.0, None, ALU.mult)
            v.drain()
            v.tensor_scalar(loI[:, :], loI[:, :], 15, None, ALU.logical_shift_right)
            v.drain()
            v.scalar_tensor_tensor(blkF[:, :], loI[:, :], -float(NT), keyI[:, :], ALU.mult, ALU.add)
            v.tensor_scalar(rec[:, :, 0], loI[:, :], 1.0, None, ALU.add)
            v.tensor_copy(rec[:, :, :].bitcast(I32)[:, :, 1], idxI[:, :])
            v.drain()

        def v_sort_start(v):
            for t, x in ((pos, 0.0), (bsum, 0.0), (gbF, 0.0), (one_row, 1.0)):
                v.memset(t[:, :], x)
            v.drain()

        def v_count(v, C, b):
            v.tensor_scalar(inb[:, 0:C], blkF[:, 0:C], iota[0:R, ds(b, 1)], 0.0, ALU.is_equal, ALU.add,
                            accum_out=cnt[:, ds(b, 1)])
            v.drain()

        def t_count(t, ph, K):
            t.wait_ge(S("s_cnt"), SORT[ph])
            t.matmul(psum[0][:, 0:K], ones[0:R, :], cnt[:, 0:K], start=True, stop=True)
            t.matmul(psum[1][0:R, 0:K], tri[0:R, 0:R], cnt[:, 0:K], start=True, stop=True
                     ).then_inc(S("s_tot"), 1)

        def v_totals(v, ph, K, gt):
            shift = (128 * gt).bit_length() - 1
            v.drain().then_inc(S("s_cnt"), 1)
            v.wait_ge(S("s_tot"), SORT[ph])
            v.tensor_scalar(ngI[:, 0:K], psum[0][:, 0:K], float(128 * gt - 1), None, ALU.add)
            v.drain()
            v.tensor_scalar(ngI[:, 0:K], ngI[:, 0:K], shift, None, ALU.logical_shift_right)
            v.drain()
            v.tensor_copy(ngF[:, 0:K], ngI[:, 0:K])
            v.drain()
            v.tensor_tensor_scan(cum[:, 0:K], ones[:, 0:K], ngF[:, 0:K], 0.0, ALU.mult, ALU.add)
            v.drain()
            v.tensor_tensor(base[:, 0:K], cum[:, 0:K], ngF[:, 0:K], ALU.subtract)
            v.drain()
            v.tensor_scalar(base[:, 0:K], base[:, 0:K], float(128 * gt), None, ALU.mult)
            v.drain()
            v.scalar_tensor_tensor(offs[:, 0:K], psum[1][0:R, 0:K], -1.0, base[0:R, 0:K], ALU.add, ALU.add)
            v.drain()

        def v_place(v, C, G, b, bases=False):
            v.tensor_scalar(inb[:, 0:C], blkF[:, 0:C], iota[0:R, ds(b, 1)], None, ALU.is_equal)
            v.scalar_tensor_tensor(gbF[:, 0:G], iota[:, 0:G], cum[:, ds(b, 1)], gbF[:, 0:G], ALU.is_ge, ALU.add)
            v.drain()
            v.tensor_tensor_scan(run[:, 0:C], one_row[0:R, 0:C], inb[:, 0:C], offs[:, ds(b, 1)], ALU.mult, ALU.add)
            if bases:
                v.scalar_tensor_tensor(bsum[:, 0:C], inb[:, 0:C], base[0:R, ds(b, 1)], bsum[:, 0:C],
                                       ALU.mult, ALU.add)
            v.drain()
            v.tensor_tensor(run[:, 0:C], run[:, 0:C], inb[:, 0:C], ALU.mult)
            v.drain()
            v.tensor_tensor(pos[:, 0:C], pos[:, 0:C], run[:, 0:C], ALU.add)
            v.drain()

        def v_placed(v, C, K, G, gblk):
            v.tensor_scalar(gbF[:, 0:G], gbF[:, 0:G], float(K - 1), None, ALU.min)
            v.tensor_copy(posI[:, 0:C], pos[:, 0:C])
            v.drain()
            v.tensor_copy(gblk[:, 0:G], gbF[:, 0:G])
            v.tensor_scalar(tI[:, 0:C], posI[:, 0:C], 7, None, ALU.logical_shift_right)
            v.tensor_scalar(posI[:, 0:C], posI[:, 0:C], 127, None, ALU.bitwise_and)
            v.drain()

        def v_edges_placed(v, G, T, gblk):
            v_placed(v, EC, NT, G, gblk)
            v.scalar_tensor_tensor(place[:, :], posI[:, :], float(T), tI[:, :], ALU.mult, ALU.add)
            v.drain()

        def p_scatter(p, h, sent, i, table, first=False):
            if not first:
                p.wait_ge(S(f"sent{h}"), 16 * SH * sent)
            p.sem_inc(S("holds_waits"), 1)
            p.tensor_copy(recS[:, h, :, :], rec[:, ds(i * SH, SH), :])
            p.tensor_copy(placeS[:, h, :], place[:, ds(i * SH, SH)])
            p.drain()
            for k in range(SH):
                p.indirect_dma_start(table, bass.IndirectOffsetOnAxis(ap=placeS[:, h, k:k + 1], axis=0),
                                     recS[:, h, k, :], None).then_inc(S(f"sent{h}"), 16)

        def s_slots(s, sent, table, T, n):
            for h in range(2):
                s.wait_ge(S(f"sent{h}"), 16 * SH * sent[h])
            s.dma_start(slots_[:, 0:T, :], table.rearrange("(p t) r -> p t r", p=128)).then_inc(S("slots_in"), 16)
            s.wait_ge(S("slots_in"), 16 * n)

        OB = 4
        c = Carver(SCR)
        c.at = sort_end
        tF = c(2 * NT, rows=R)
        qF = c(2 * NT, rows=R)
        ot = c(OB, 128, rows=R)
        oq = c(OB, 128, rows=R)
        move_end = c.at

        def v_onehot(v, ph, i, u, T, per):
            col = i * per + u
            v.wait_ge(S("s_used"), freed(i, u, OB, per) + MOVED[ph])
            v.tensor_scalar(ot[:, u % OB, 0:T], iota[0:R, 0:T], tF[:, ds(col, 1)], None, ALU.is_equal)
            v.tensor_scalar(oq[:, u % OB, :], iota[0:R, 0:128], qF[:, ds(col, 1)], packed[:, ds(col, 1)],
                            ALU.is_equal, ALU.mult).then_inc(S("s_onehot"), 1)

        def t_move(t, ph, i, u, T, per):
            t.wait_ge(S("s_onehot"), i * per + (u + 1 + MOVED[ph]))
            t.matmul(psum[6][:, 0:T], oq[:, u % OB, :], ot[:, u % OB, 0:T], start=False, stop=False,
                     skip_group_check=True).then_inc(S("s_used"), 1)

        def t_bounds(t, T, start, banks):
            for b in banks:
                k = t.matmul(psum[b][:, 0:T], zeros[:, 0:128], zeros[:, 0:T], start=start, stop=not start,
                             skip_group_check=True)
            return k

        c = Carver(SCR)
        c.at = sort_end
        gi = c(EU // 4, 4, dt=I32)
        g0 = c(EU, D)
        s0 = c(EU, R)
        edge_end = c.at

        def a_rows(a, ph, i, h):
            a.wait_ge(S(ph + "_sum"), freed(i, h * 4 + 3, EU, EU))
            a.wait_ge(consts, 1)
            a.copy(gi[:, h, :], slots_[:, :, :].bitcast(I32)[:, ds(i * EU + h * 4, 4), 1]).then_inc(S("rows"), 1)

        def p_gather(p, before, i, table, dst):
            for h in range(EU // 4):
                p.wait_ge(S("rows"), (before + i) * (EU // 4) + (h + 1))
                p.sem_inc(S("holds_waits"), 1)
                for k in range(4):
                    p.indirect_dma_start(dst[:, h * 4 + k, :], None, table,
                                         bass.IndirectOffsetOnAxis(ap=gi[:, h, k:k + 1], axis=0)
                                         ).then_inc(S(f"e_g{h * 4 + k}"), 16)

        def v_sel0(v, i, u):
            t = i * EU + u
            v.wait_ge(S("e0_sum"), freed(i, u, EU, EU))
            v.tensor_scalar(s0[:, u, :], iota[:, 1:R + 1], slots_[:, ds(t, 1), 0], slots_[:, ds(t, 1), 2],
                            ALU.is_equal, ALU.mult).then_inc(S("e0_sel"), 1)

        def t_e0(t, i, u):
            t.wait_ge(S("e0_sel"), i * EU + (u + 1))
            t.wait_ge(S(f"e_g{u}"), gathered(i + 1))
            t.wait_ge(S("e0_acc"), freed(i, u, 4, EU))
            t.matmul(psum[2 + u % 4][0:R, 0:D], s0[:, u, :], g0[:, u, :], start=True, stop=True
                     ).then_inc(S("e0_sum"), 1)

        def v_acc0(v, i, u):
            blk = v.value_load(gblk0[0:1, ds(i * EU + u, 1)], min_val=0, max_val=NT - 1)
            v.drain()
            v.wait_ge(S("e0_sum"), done(i, u, EU))
            a = turn(AGG[:, ds(blk, 1), :])
            v.tensor_tensor(a, a, psum[2 + u % 4][0:R, 0:D], ALU.add).then_inc(S("e0_acc"), 1)

        bnm = XN
        c = Carver(SCR)
        gm2 = c(D, rows=R)
        mean = c(D, rows=R)
        var = c(D, rows=R)
        rstd = c(D, rows=R)

        def t_bn(t, src_t, bank, wait, name):
            t.wait_ge(S(wait), 1)
            for j in range(NT):
                k = t.matmul(psum[bank][0:R, 0:D], ones[0:R, 0:R], src_t[:, j, :], start=(j == 0), stop=(j == NT - 1))
            k.then_inc(S(name), 1)

        def bc(v2):
            return v2[:, :].unsqueeze(1).broadcast_to([R, NT, D])

        def v_bn(v):
            v.drain().then_inc(S("bn_agg"), 1)
            v.wait_ge(S("bn_sum"), 1)
            v.tensor_scalar(mean[:, :], psum[0][0:R, 0:D], 1.0 / N, None, ALU.mult)
            v.drain()
            v.tensor_tensor(AGG[:, :, :], AGG[:, :, :], bc(mean), ALU.subtract).then_inc(S("bn_centred"), 1)
            v.wait_ge(S("bn_ssq"), 1)
            v.tensor_scalar(var[:, :], psum[1][0:R, 0:D], 1.0 / N, None, ALU.mult).then_inc(S("bn_var"), 1)
            v.wait_ge(S("bn_sd"), 1)
            v.reciprocal(rstd[:, :], rstd[:, :])
            v.drain()
            v.tensor_tensor(rstd[:, :], rstd[:, :], gammab[0:R, :], ALU.mult)
            v.drain()
            v.tensor_tensor(AGG[:, :, :], AGG[:, :, :], bc(rstd), ALU.mult)
            v.drain()
            v.tensor_tensor(AGG[:, :, :], AGG[:, :, :], bc(betab[0:R, :]), ALU.add).then_inc(S("bn_y"), 1)
            v.wait_ge(S("bn_tanh"), 1)
            v.tensor_tensor(X[:, :, :], X[:, :, :], bnm[:, :, :], ALU.add)

        def a_bn(a):
            a.wait_ge(S("bn_centred"), 1)
            a.activation(bnm[:, :, :], AGG[:, :, :], ACT.Square).then_inc(S("bn_sq"), 1)
            a.wait_ge(S("bn_var"), 1)
            a.activation(rstd[:, :], var[:, :], ACT.Sqrt, bias=eps_t[0:R, 0:1]).then_inc(S("bn_sd"), 1)
            a.wait_ge(S("bn_y"), 1)
            a.activation(bnm[:, :, :], AGG[:, :, :], ACT.Tanh).then_inc(S("bn_tanh"), 1)


        TC = EC // NT // 2
        ea = XN[:, 0:4, :].rearrange("p a b -> p (a b)").rearrange("p (s c e) -> p s c e", s=2, c=TC)

        def s_te(s):
            av = A["edge_attr_64"].rearrange("(p c) e -> p c e", p=R)
            with s.Fori(0, NT) as i:
                for u in range(2):
                    s.wait_ge(S("te_read"), freed(i, u, 2, 2))
                    s.dma_start(ea[:, u], av[:, ds((i * 2 + u) * TC, TC), :]).then_inc(S(f"te_in{u}"), 16)

        def v_te(v, i):
            for u in range(2):
                v.wait_ge(S(f"te_in{u}"), 16 * (i + 1))
                v.tensor_tensor(ea[:, u], ea[:, u], attb[0:R, 2 * D:2 * D + EDIM].unsqueeze(1)
                                .broadcast_to([R, TC, EDIM]), ALU.mult)
            v.drain()
            for u in range(2):
                v.tensor_reduce(rec[:, ds((i * 2 + u) * TC, TC), 2], ea[:, u], AX_X, ALU.add
                                ).then_inc(S("te_read"), 1)

        GATE = {"g0": 0, "g1": NT // U5}

        def t_gate(t, ph, gw, NX):
            if ph == "g0":
                seed(t, "g_lgp")
            with t.Fori(0, NT // U5) as i:
                for u in range(U5):
                    t_turn(t, BEFORE[ph], i, u)
                t.wait_ge(S("g_lg"), GATE[ph] + i + 1)
                for u in range(U5):
                    t.wait_ge(S("x_xT"), done(BEFORE[ph] + i, u))
                    for h in range(2):
                        k = t.matmul(psum[2][0:R, u * NX:(u + 1) * NX], xT[:, u, h, :], gw[:, h, :],
                                     start=(h == 0), stop=(h == 1))
                    k.then_inc(S("g_lgp"), 1)

        def a_gate(a, ph):
            with a.Fori(0, NT // U5) as i:
                a_sqrt(a, BEFORE[ph], i)
                for u in range(U5):
                    a_turned(a, BEFORE[ph], i, u, lambda: a.wait_ge(S("g_lgp"), freed(GATE[ph] + i, u, U5)))

        def v_gate(v, ph, gb, NX, keep):
            if ph == "g0":
                seed(v, "g_lg", n=1)
            with v.Fori(0, NT // U5) as i:
                def kept():
                    v.wait_ge(S("g_hout"), landed(GATE[ph] + i))
                    if keep:
                        v.wait_ge(S("g_keep"), i + 1)
                v_norm(v, BEFORE[ph], i, kept)
                v.wait_ge(S("g_lgp"), done(GATE[ph] + i, U5 - 1))
                v.tensor_tensor(LG[:, ds(i * U5, U5), 0:NX],
                                psum[2][0:R, 0:U5 * NX].rearrange("p (a b) -> p a b", a=U5),
                                gb[0:R, 0:NX].unsqueeze(1).broadcast_to([R, U5, NX]), ALU.add
                                ).then_inc(S("g_lg"), 1)

        def s_gate(s, ph, hrow):
            if ph == "g0":
                seed(s, "g_hout", n=16)
            with s.Fori(0, NT // U5) as i:
                s.wait_ge(S("x_xs"), (BEFORE[ph] + i) * U5 + U5)
                s.dma_start(tiles(hrow)[:, ds(i * U5, U5), :], xs[:, :, :]).then_inc(S("g_hout"), 16)
            s.wait_ge(S("g_hout"), landed(GATE[ph] + NT // U5))

        def p_keep(p, ph):
            seed(p, "g_keep", n=1)
            with p.Fori(0, NT // U5) as i:
                p.wait_ge(S("x_xs"), (BEFORE[ph] + i) * U5 + U5)
                p.sem_inc(S("holds_waits"), 1)
                p.tensor_copy(XN[:, ds(i * U5, U5), :], xs[:, :, :]).then_inc(S("g_keep"), 1)

        c = Carver(SCR)
        c.at = move_end
        mx = c(2, NT, rows=R)
        low = c(NT, rows=R)
        eqm = c(NT, X1, rows=R)
        eqx = c(NT, X1, rows=R)
        sm = c(NT, rows=R)

        def bx(v2, NX):
            return v2.unsqueeze(2).broadcast_to([R, NT, NX])

        def v_choose(v, ph, NX, K):
            v.wait_ge(S("g_hout"), landed(GATE[ph] + NT // U5))
            if K > 1:
                v.wait_ge(S("g_keep"), NT // U5 + 1)
            sc = LG[:, :, 0:NX]
            ids = iota[0:R, 0:NX].unsqueeze(1).broadcast_to([R, NT, NX])
            for k in range(K):
                v.tensor_reduce(mx[:, k, :], sc, AX_X, ALU.max)
                v.drain()
                v.tensor_tensor(eqm[:, :, 0:NX], sc, bx(mx[:, k, :], NX), ALU.is_equal)
                v.drain()
                v.scalar_tensor_tensor(eqm[:, :, 0:NX], eqm[:, :, 0:NX], -100.0, ids, ALU.mult, ALU.add)
                v.drain()
                v.tensor_reduce(low[:, :], eqm[:, :, 0:NX], AX_X, ALU.min)
                v.drain()
                b = blkF[:, k * NT:(k + 1) * NT]
                v.tensor_scalar(b, low[:, :], 100.0, None, ALU.add)
                v.tensor_copy(packed[:, k * NT:(k + 1) * NT], node[:, :])
                v.drain()
                if K == 1:
                    v.tensor_tensor(eqx[:, :, 0:NX], sc, bx(mx[:, 0, :], NX), ALU.subtract)
                elif k == 0:
                    v.tensor_tensor(eqm[:, :, 0:NX], ids, bx(b, NX), ALU.is_equal)
                    v.drain()
                    v.scalar_tensor_tensor(sc, eqm[:, :, 0:NX], -BIG, sc, ALU.mult, ALU.add)
                    v.drain()
            if K == 1:
                v.drain().then_inc(S("g_x"), 1)
                v.wait_ge(S("g_ex"), K)
                v.tensor_reduce(sm[:, :], eqx[:, :, 0:NX], AX_X, ALU.add)
                v.drain()
                v.reciprocal(gwt[:, 0, :], sm[:, :])
            else:
                v.tensor_tensor(sm[:, :], mx[:, 1, :], mx[:, 0, :], ALU.subtract).then_inc(S("g_x"), 1)
                v.wait_ge(S("g_ex"), K)
                v.tensor_scalar(low[:, :], sm[:, :], 1.0, None, ALU.add)
                v.drain()
                v.reciprocal(gwt[:, 0, :], low[:, :])
                v.drain()
                v.tensor_tensor(gwt[:, 1, :], gwt[:, 0, :], sm[:, :], ALU.mult)
            v.drain()

        def a_choose(a, ph, NX, K):
            a.wait_ge(S("g_x"), K)
            z = eqx[:, :, 0:NX] if K == 1 else sm[:, :]
            a.activation(z, z, ACT.Exp).then_inc(S("g_ex"), 1)

        def v_route(v, ph, K, NX, M):
            C = NT * K
            v_sort_start(v)
            with v.Fori(0, NX) as b:
                v_count(v, C, b)
            v_totals(v, ph, NX, 1)
            with v.Fori(0, NX) as b:
                v_place(v, C, M, b, bases=(K == 1))
            v_placed(v, C, NX, M, gblk0)
            v.tensor_copy(tF[:, 0:C], tI[:, 0:C])
            v.tensor_copy(qF[:, 0:C], posI[:, 0:C])
            v.tensor_copy(slotI[:, 0:C], pos[:, 0:C])
            if K == 1:
                v.tensor_tensor(low[:, :], pos[:, 0:C], bsum[:, 0:C], ALU.subtract)
                v.drain()
                v.tensor_scalar(low[:, :], low[:, :], float(CAP), None, ALU.is_lt)
                v.drain()
                v.tensor_tensor(gwt[:, 0, :], gwt[:, 0, :], low[:, :], ALU.mult)
            v.drain()
            with v.Fori(0, C // U5) as i:
                for u in range(U5):
                    v_onehot(v, ph, i, u, M, U5)
            v.wait_ge(S("s_moved"), K)
            v.tensor_copy(idxX[:, 0:M], psum[6][:, 0:M])
            v.drain()

        def t_route(t, ph, K, NX, M):
            t_count(t, ph, NX)
            t_bounds(t, M, True, (6,))
            with t.Fori(0, NT * K // U5) as i:
                for u in range(U5):
                    t_move(t, ph, i, u, M, U5)
            t_bounds(t, M, False, (6,)).then_inc(S("s_moved"), 1)

        c = Carver(SCR)
        ew1 = c(2, 2 * F0)
        ew2 = c(2, 2 * F0)
        eb1 = c(2, F0 // 128)
        eb2 = c(2, D, rows=1)
        xg = c(2, D)
        gx = c(2, dt=I32)
        xgT = c(2, 2, 128)
        ht = c(2, F0)
        yo = c(2, D)

        def s_expert(s, b, M, F, w1d, b1d, w2d, b2d):
            FC = F // 128
            with s.Fori(0, M // 2) as i:
                for u in range(2):
                    e = s.value_load(gblk0[0:1, ds(i * 2 + u, 1)], min_val=0, max_val=w1d.shape[0] - 1)
                    s.wait_ge(S("m_yp"), freed(b + i, u, 2, 2))
                    s.dma_start(ew1[:, u, 0:2 * F].rearrange("p (h f) -> p h f", h=2),
                                w1d[ds(e, 1), :, :].rearrange("a (h p) f -> p (a h) f", p=128)
                                ).then_inc(S(f"m_w{u}"), 16)
                    s.dma_start(ew2[:, u, 0:2 * F], w2d[ds(e, 1), :, :].rearrange("a (p c) d -> p (a c d)", p=128)
                                ).then_inc(S(f"m_w{u}"), 16)
                    s.dma_start(eb1[:, u, 0:FC], b1d[ds(e, 1), :].rearrange("a (p c) -> p (a c)", p=128)
                                ).then_inc(S(f"m_w{u}"), 16)
                    s.dma_start(eb2[:, u, :], b2d[ds(e, 1), :]).then_inc(S(f"m_w{u}"), 16)

        def p_expert(p, b, M, hrow, also=None):
            with p.Fori(0, M // 2) as i:
                p.wait_ge(S("m_tp"), freed(b + i, 1, 2, 2))
                p.sem_inc(S("holds_waits"), 1)
                p.tensor_copy(gx[:, :], idxX[:, ds(i * 2, 2)])
                p.drain()
                for u in range(2):
                    p.indirect_dma_start(xg[:, u, :], None, hrow,
                                         bass.IndirectOffsetOnAxis(ap=gx[:, u:u + 1], axis=0)
                                         ).then_inc(S(f"m_g{u}"), 16)
                if also is not None:
                    also(i)

        def t_expert(t, b, M, F):
            FC = F // 128
            if b == 0:
                seed(t, "m_yp", "m_tp", "m_hp", n=2)
            with t.Fori(0, M // 2) as i:
                for u in range(2):
                    t.wait_ge(S(f"m_g{u}"), gathered(b + i + 1))
                    t.wait_ge(S("m_xT"), freed(b + i, u, 2, 2))
                    for h in range(2):
                        k = t.transpose(psum[u][:, h * 128:(h + 1) * 128], xg[:, u, h * 128:(h + 1) * 128],
                                        ident[:, :])
                    k.then_inc(S("m_tp"), 1)
                for u in range(2):
                    w = ew1[:, u, 0:2 * F].rearrange("p (h q c) -> p h q c", h=2, c=FC)
                    t.wait_ge(S(f"m_w{u}"), 64 * (b + i + 1))
                    t.wait_ge(S("m_xT"), done(b + i, u, 2))
                    t.wait_ge(S("m_h"), freed(b + i, u, 2, 2))
                    for f in range(FC):
                        for h in range(2):
                            k = t.matmul(psum[2 + 2 * u + f // 4][:, (f % 4) * 128:(f % 4 + 1) * 128],
                                         w[:, h, :, f], xgT[:, u, h, :], start=(h == 0), stop=(h == 1))
                    k.then_inc(S("m_hp"), 1)
                for u in range(2):
                    t.wait_ge(S("m_h"), done(b + i, u, 2))
                    t.wait_ge(S("m_y"), freed(b + i, u, 2, 2))
                    for f in range(FC):
                        t.matmul(psum[6 + u][:, 0:D], ht[:, u, f * 128:(f + 1) * 128],
                                 ew2[:, u, f * D:(f + 1) * D], start=(f == 0), stop=False)
                    t.matmul(psum[6 + u][:, 0:D], ones[0:1, :], eb2[:, u, :], start=False, stop=True
                             ).then_inc(S("m_yp"), 1)

        def a_expert(a, b, M, F, ys):
            FC = F // 128
            if b == 0:
                seed(a, "m_xT", "m_h", n=2)
                seed(a, "m_out0", "m_out1", n=16)
            with a.Fori(0, M // 2) as i:
                for u in range(2):
                    a.wait_ge(S("m_tp"), done(b + i, u, 2))
                    a.wait_ge(S("m_hp"), freed(b + i, u, 2, 2))
                    a.copy(xgT[:, u, :, :], psum[u][:, 0:256].rearrange("p (h r) -> p h r", h=2)
                           ).then_inc(S("m_xT"), 1)
                for u in range(2):
                    a.wait_ge(S("m_hp"), done(b + i, u, 2))
                    a.wait_ge(S("m_yp"), freed(b + i, u, 2, 2))
                    for f in range(FC):
                        k = a.activation(ht[:, u, f * 128:(f + 1) * 128],
                                         psum[2 + 2 * u + f // 4][:, (f % 4) * 128:(f % 4 + 1) * 128],
                                         ACT.Relu, bias=eb1[:, u, f:f + 1])
                    k.then_inc(S("m_h"), 1)
                for u in range(2):
                    a.wait_ge(S("m_y"), done(b + i, u, 2))
                    a.dma_start(ys[ds((i * 2 + u) * 128, 128), :], yo[:, u, :]).then_inc(S(f"m_out{u}"), 16)
            for u in range(2):
                a.wait_ge(S(f"m_out{u}"), landed(b + M // 2))

        def v_expert(v, b, M):
            if b == 0:
                seed(v, "m_y", n=2)
            with v.Fori(0, M // 2) as i:
                for u in range(2):
                    v.wait_ge(S("m_yp"), done(b + i, u, 2))
                    v.wait_ge(S(f"m_out{u}"), landed(b + i))
                    v.wait_ge(consts, 1)
                    v.tensor_scalar(yo[:, u, :], psum[6 + u][:, 0:D], 1.0, None, ALU.mult
                                    ).then_inc(S("m_y"), 1)

        c = Carver(SCR)
        c.at = norm_end
        gc = c(2 * U5, rows=R, dt=I32)
        yg = c(2 * U5, D, rows=R)
        fin = c(U5, D, rows=R, dt=I32)
        nan = c(U5, D, rows=R, dt=I32)

        def back_turns(K, n):
            return NT // U5 if K > K0 and n < K0 * U5 else 0

        def p_back(p, ph, K, ys):
            with p.Fori(0, NT // U5) as i:
                p.wait_ge(S(ph + "_took"), i + 1)
                p.sem_inc(S("holds_waits"), 1)
                for k in range(K):
                    p.tensor_copy(gc[:, k * U5:(k + 1) * U5], slotI[:, ds(i * U5 + k * NT, U5)])
                p.drain()
                for n in range(K * U5):
                    p.indirect_dma_start(yg[:, n, :], None, ys,
                                         bass.IndirectOffsetOnAxis(ap=gc[:, n:n + 1], axis=0)
                                         ).then_inc(S(f"b{n}"), 16)

        def v_back0(v):
            seed(v, "m0_took", n=1)
            with v.Fori(0, NT // U5) as i:
                for u in range(U5):
                    v.wait_ge(S(f"b{u}"), gathered(i + 1))
                    v.tensor_scalar(yg[:, u, :], yg[:, u, :], gwt[:, 0, ds(i * U5 + u, 1)], None, ALU.mult)
                v.drain()
                y5 = yg[:, 0:U5, :]
                y5b = yg[:, U5:2 * U5, :]
                v.tensor_scalar(fin[:, :, :], y5, 0.0, 0.0, ALU.mult, ALU.is_equal)
                v.tensor_tensor(nan[:, :, :], y5, y5, ALU.not_equal)
                v.tensor_scalar(y5b, y5, 1e4, -1e4, ALU.min, ALU.max)
                v.drain()
                v.copy_predicated(y5b, fin[:, :, :], y5)
                v.drain()
                v.copy_predicated(y5b, nan[:, :, :], zero3)
                v.drain()
                x5 = X[:, ds(i * U5, U5), :]
                v.tensor_tensor(x5, x5, y5b, ALU.add).then_inc(S("m0_took"), 1)

        zero3 = zeros[0:R, 0:D].unsqueeze(1).broadcast_to([R, U5, D])

        def v_back1(v):
            seed(v, "m1_took", n=1)
            with v.Fori(0, NT // U5) as i:
                for k in range(2):
                    for u in range(U5):
                        xr = turn(XN[:, ds(i * U5 + u, 1), :])
                        v.wait_ge(S(f"b{k * U5 + u}"), gathered(i + 1 + back_turns(2, k * U5 + u)))
                        v.scalar_tensor_tensor(xr, yg[:, k * U5 + u, :], gwt[:, k, ds(i * U5 + u, 1)], xr,
                                               ALU.mult, ALU.add)
                    v.drain()
                v.drain().then_inc(S("m1_took"), 1)
                for u in range(U5):
                    v.bn_stats(st6[:, u, :], turn(XN[:, ds(i * U5 + u, 1), :]))
                v.drain()
                for u in range(U5):
                    k = v.bn_aggr(mv[:, u, :], st6[:, u, :])
                k.then_inc(S("x_var"), 1)
                v.wait_ge(S("x_sd"), BEFORE["fin"] + i + 1)
                v.reciprocal(rs[:, :], sd[:, :])
                v.drain()
                v.wait_ge(S("fin_out"), landed(i))
                for u in range(U5):
                    v.tensor_scalar(xs[:, u, :], turn(XN[:, ds(i * U5 + u, 1), :]), mv[:, u, 0:1],
                                    rs[:, u:u + 1], ALU.subtract, ALU.mult)
                v.drain()
                v.tensor_tensor(xs[:, :, :], xs[:, :, :], gamma1b[0:R, :].unsqueeze(1).broadcast_to([R, U5, D]), ALU.mult)
                v.drain()
                v.tensor_tensor(xs[:, :, :], xs[:, :, :], beta1b[0:R, :].unsqueeze(1).broadcast_to([R, U5, D]), ALU.add)
                v.drain()
                v.tensor_tensor(xs[:, :, :], xs[:, :, :], X[:, ds(i * U5, U5), :], ALU.add).then_inc(S("fin_y"), 1)

        def s_final(s):
            seed(s, "fin_out", n=16)
            with s.Fori(0, NT // U5) as i:
                s.wait_ge(S("fin_y"), i + 1)
                s.dma_start(tiles(out)[:, ds(i * U5, U5), :], xs[:, :, :]).then_inc(S("fin_out"), 16)
            s.wait_ge(S("fin_out"), landed(NT // U5))

        c = Carver(SCR)
        wtmp = c(2, D)
        wmean = c(2, 16)

        def v_w1(v):
            for n in range(2):
                v.tensor_tensor(wtmp[:, :, :], wfx[:, :, 0:D],
                                attb[:, n * D:(n + 1) * D].unsqueeze(1).broadcast_to([128, 2, D]), ALU.mult)
                v.drain()
                v.tensor_reduce(wfx[:, :, D + n:D + n + 1], wtmp[:, :, :], AX_X, ALU.add)
                v.drain()
            for h in range(2):
                g = wkv1[:, h, :].rearrange("p (g e) -> p g e", e=64)
                v.tensor_reduce(wmean[:, h, :], g, AX_X, ALU.add)
                v.drain()
                v.tensor_scalar(wmean[:, h, :], wmean[:, h, :], 1.0 / 64, None, ALU.mult)
                v.drain()
                v.tensor_tensor(g, g, wmean[:, h, :].unsqueeze(2).broadcast_to([128, 16, 64]), ALU.subtract)
            v.memset(den[:, :], 0.0)
            v.memset(AGG[:, :, :], 0.0)

        c = Carver(SCR)
        c.at = norm_end
        zrow = c(U5, ROW1, rows=R)
        sq = c(2, 2 * HID, rows=R)
        K1t = c(2, HID, rows=R)
        V1t = c(2, HID, rows=R)
        ss = c(2, 16, rows=R)
        rr = c(2, 8, rows=R)
        dts = c(4, 128)
        Bm = c(4, D)

        def t_a1(t):
            seed(t, "a1_z", "a1_kp", "a1_vp", "a1_sum")
            t_bounds(t, 512, True, (5,))
            with t.Fori(0, NT // U5) as i:
                for u in range(U5):
                    t_turn(t, BEFORE["a1"], i, u)

                def sums(u):
                    t.wait_ge(S("a1_V"), done(i, u))
                    for q in range(4):
                        k = t.matmul(psum[5][:, q * 128:(q + 1) * 128], V1t[:, u % 2, q * 128:(q + 1) * 128],
                                     K1t[:, u % 2, q * 128:(q + 1) * 128], start=False, stop=False,
                                     skip_group_check=True)
                    k.then_inc(S("a1_sum"), 1)

                for u in range(U5):
                    t.wait_ge(S("x_xT"), done(BEFORE["a1"] + i, u))
                    t.wait_ge(S("a1_zr"), freed(i, u, 2))
                    for h in range(2):
                        k = t.matmul(psum[2 + 4 * (u % 2)][0:R, 0:ROW1], xT[:, u, h, :], wfx[:, h, :],
                                     start=(h == 0), stop=(h == 1))
                    k.then_inc(S("a1_z"), 1)
                    t.wait_ge(S("a1_kc"), freed(i, u, 2))
                    for h in range(2):
                        k = t.matmul(psum[3 + 4 * (u % 2)][0:R, :], xT[:, u, h, :], wkv1[:, h, 0:HID],
                                     start=(h == 0), stop=(h == 1))
                    k.then_inc(S("a1_kp"), 1)
                    t.wait_ge(S("a1_vc"), freed(i, u, 1))
                    for h in range(2):
                        k = t.matmul(psum[4][0:R, :], xT[:, u, h, :], wkv1[:, h, HID:2 * HID],
                                     start=(h == 0), stop=(h == 1))
                    k.then_inc(S("a1_vp"), 1)
                    if u:
                        sums(u - 1)
                sums(U5 - 1)
            t_bounds(t, 512, False, (5,)).then_inc(S("a1_all"), 1)
            t.wait_ge(S("a1_dts"), 1)
            for q in range(4):
                k = t.matmul(psum[6 + q // 2][:, (q % 2) * 256:(q % 2) * 256 + 256], dts[:, q, :], wout[:, q, :],
                             start=True, stop=True)
            k.then_inc(S("a1_B"), 1)
            t.wait_ge(S("a1_Bm"), 1)
            for h in range(2):
                for q in range(4):
                    k = t.matmul(psum[2][:, h * 256:(h + 1) * 256], wqo[:, q, h * 128:(h + 1) * 128], Bm[:, q, :],
                                 start=(q == 0), stop=(q == 3))
            k.then_inc(S("a1_M"), 1)

        def a_a1(a):
            seed(a, "a1_zr", "a1_kc", "a1_vc")
            with a.Fori(0, NT // U5) as i:
                a_sqrt(a, BEFORE["a1"], i)
                for u in range(U5):
                    def users():
                        a.wait_ge(S("a1_vp"), freed(i, u, U5))
                        a.wait_ge(S("a1_xkeep"), freed(i, u, U5))
                    a_turned(a, BEFORE["a1"], i, u, users)
                for u in range(U5):
                    a.wait_ge(S("a1_z"), done(i, u))
                    a.wait_ge(S(f"a_out{u}"), landed(NT // U5 + i))
                    a.wait_ge(S("a1_dcol"), i + 1)
                    a.copy(zrow[:, u, :], psum[2 + 4 * (u % 2)][0:R, 0:ROW1]).then_inc(S("a1_zr"), 1)
                    a.wait_ge(S("a1_kp"), done(i, u))
                    a.wait_ge(S("a1_ss"), freed(i, u, 2))
                    a.activation(sq[:, u % 2, 0:HID], psum[3 + 4 * (u % 2)][0:R, :], ACT.Square)
                    a.wait_ge(S("a1_sum"), freed(i, u, 2))
                    a.copy(K1t[:, u % 2, :], psum[3 + 4 * (u % 2)][0:R, :]).then_inc(S("a1_kc"), 1)
                    a.wait_ge(S("a1_vp"), done(i, u))
                    a.activation(sq[:, u % 2, HID:2 * HID], psum[4][0:R, :], ACT.Square)
                    a.copy(V1t[:, u % 2, :], psum[4][0:R, :]).then_inc(S("a1_vc"), 1)
                    a.wait_ge(S("a1_ss"), done(i, u))
                    a.activation(ss[:, u % 2, :], ss[:, u % 2, :], ACT.Sqrt, bias=eps_t[0:R, 0:1], scale=1.0 / 64
                                 ).then_inc(S("a1_sq"), 1)

        def v_a1(v):
            seed(v, "a1_ss", "a1_V")
            seed(v, "a1_dcol", n=1)
            with v.Fori(0, NT // U5) as i:
                def kept():
                    v.wait_ge(S("a1_keep"), i + 1)
                v_norm(v, BEFORE["a1"], i, kept)
                for u in range(U5):
                    v.drain()
                    v.wait_ge(S("a1_vc"), done(i, u))
                    v.tensor_reduce(ss[:, u % 2, :], sq[:, u % 2, :].rearrange("p (g e) -> p g e", e=64),
                                    AX_X, ALU.add).then_inc(S("a1_ss"), 1)
                    v.wait_ge(S("a1_sq"), i * U5 + (u + 1))
                    v.reciprocal(ss[:, u % 2, :], ss[:, u % 2, :])
                    v.drain()
                    v.tensor_tensor(rr[:, u % 2, :], ss[:, u % 2, 0:8], ss[:, u % 2, 8:16], ALU.mult)
                    v.drain()
                    v1 = V1t[:, u % 2, :].rearrange("p (g e) -> p g e", e=64)
                    v.tensor_tensor(v1, v1, rr[:, u % 2, :].unsqueeze(2).broadcast_to([R, 8, 64]), ALU.mult
                                    ).then_inc(S("a1_V"), 1)
                v.wait_ge(S("a1_zr"), done(i, U5 - 1))
                v.tensor_scalar(dm[:, ds(i * U5, U5), 0], zrow[:, :, D + 1], 1.0, None, ALU.mult
                                ).then_inc(S("a1_dcol"), 1)
            v.drain()
            v.tensor_scalar(dm[:, :, 1], dm[:, :, 0], 0.01, None, ALU.mult)
            v.memset(dm[:, :, 2], LOWEST)
            v.wait_ge(S("a1_all"), 1)
            for q in range(4):
                k = v.scalar_tensor_tensor(dts[:, q, :], psum[5][:, q * 128:(q + 1) * 128], 1.0 / N, hm64[:, :],
                                           ALU.mult, ALU.mult)
            k.then_inc(S("a1_dts"), 1)
            v.wait_ge(S("a1_B"), 1)
            v.tensor_copy(Bm[:, 0:2, :], psum[6][:, :].rearrange("p (a b) -> p a b", a=2))
            v.tensor_copy(Bm[:, 2:4, :], psum[7][:, :].rearrange("p (a b) -> p a b", a=2)).then_inc(S("a1_Bm"), 1)
            v.wait_ge(S("a1_M"), 1)
            v.tensor_copy(wsm[:, :, D:2 * D], psum[2][:, :].rearrange("p (a b) -> p a b", a=2))

        def s_a1(s):
            with s.Fori(0, NT // U5) as i:
                for u in range(U5):
                    s.wait_ge(S("a1_zr"), done(i, u))
                    s.dma_start(tiles(tab1)[:, ds(i * U5 + u, 1), :].rearrange("p a d -> p (a d)"), zrow[:, u, :]
                                ).then_inc(S(f"a_out{u}"), 16)
            for u in range(U5):
                s.wait_ge(S(f"a_out{u}"), landed(2 * (NT // U5)))

        def p_a1(p):
            seed(p, "a1_xkeep")
            seed(p, "a1_keep", n=1)
            with p.Fori(0, NT // U5) as i:
                p.wait_ge(S("x_xs"), (BEFORE["a1"] + i) * U5 + U5)
                p.sem_inc(S("holds_waits"), 1)
                p.tensor_copy(XN[:, ds(i * U5, U5), :], xs[:, :, :]).then_inc(S("a1_keep"), 1)
                for h, before in enumerate((SCB + M0 // 2, SCB)):
                    p_scatter(p, h, SC + before + i, 2 * SCB + M0 // 2 + i * 2 + h, slot1)
                for u in range(U5):
                    p.wait_ge(S("x_xT"), done(BEFORE["a1"] + i, u))
                    p.wait_ge(consts, 1)
                    p.tensor_copy(xnT[:, :, ds((i * U5 + u) * R, R)], xT[:, u, :, :]).then_inc(S("a1_xkeep"), 1)

        GU = EU // GT1
        c = Carver(SCR)
        c.at = sort_end
        c(EU // 4, 4)
        g1 = c(EU, ROW1)
        c.at = 0
        gs = c(GU, 2)
        ohg = c(4, 2, R)
        unb = c(4, 2 * (R + 1) // 2, dt=BF16)
        E1 = c(2, 256, rows=R)
        E2 = c(2, 256, rows=R)
        Pm = c(2, 256, rows=R)
        Ps = c(2, 2, R)
        gmx = c(GU, rows=R)
        t1 = c(GU, 2, rows=R)
        mnew = c(GU, rows=R)
        bs = c(GU, 4, rows=R)
        rsc = c(GU, rows=R)
        assert c.at <= sort_end

        def group_block(v, i, w):
            return v.value_load(gblk1[0:1, ds(i * GU + w, 1)], min_val=0, max_val=NT - 1)

        def v1_sel(v, i, w):
            for k in range(2):
                v.wait_ge(S(f"e_g{2 * w + k}"), gathered(T0 // EU + i + 1))
            v.tensor_tensor(gs[:, w, :], g1[:, 2 * w:2 * w + 2, D], slots_[:, ds((i * GU + w) * 2, 2), 2], ALU.add)
            v.drain()
            v.wait_ge(S("e1_dt"), freed(i, w, 4, GU))
            for k in range(2):
                key = slots_[:, ds((i * GU + w) * 2 + k, 1), 0]
                v.tensor_scalar(ohg[:, w % 4, k, :], iota[:, 1:R + 1], key, gs[:, w, k:k + 1], ALU.is_equal, ALU.mult)
                j = v.tensor_scalar(unb[:, w % 4, k * (R + 1):k * (R + 1) + R], iota[:, 1:R + 1], key, -BIG,
                                    ALU.not_equal, ALU.mult)
            j.then_inc(S("e1_sel"), 1)

        def t1_mask(t, i, w):
            t.wait_ge(S("e1_sel"), i * GU + (w + 1))
            t.wait_ge(S("e1_exp"), freed(i, w, 2, GU))
            for k in range(2):
                o = psum[w % 2][0:R, k * 128:(k + 1) * 128]
                t.matmul(o, ohg[:, w % 4, k, :], ident[:, :], start=True, stop=False)
                j = t.matmul(o, unb[:, w % 4, k * (R + 1):k * (R + 1) + R], identb[:, :], start=False, stop=True)
            j.then_inc(S("e1_dt"), 1)

        def v1_max(v, i, w):
            blk = group_block(v, i, w)
            d_, m_ = dm[:, ds(blk, 1), 0], dm[:, ds(blk, 1), 2]
            v.wait_ge(S("e1_dt"), done(i, w, GU))
            v.tensor_reduce(gmx[:, w:w + 1], psum[w % 2][0:R, 0:256], AX_X, ALU.max)
            v.drain()
            v.tensor_scalar(t1[:, w, 0:1], gmx[:, w:w + 1], d_, m_, ALU.add, ALU.max)
            v.tensor_scalar(t1[:, w, 1:2], gmx[:, w:w + 1], d_, 0.01, ALU.add, ALU.mult)
            v.drain()
            v.tensor_tensor(mnew[:, w:w + 1], t1[:, w, 0:1], t1[:, w, 1:2], ALU.max)
            v.drain()
            v.tensor_scalar(bs[:, w, 0:3], turn(dm[:, ds(blk, 1), :]), mnew[:, w:w + 1], None, ALU.subtract
                            ).then_inc(S("e1_max"), 1)
            v.drain()
            v.tensor_scalar(m_, mnew[:, w:w + 1], 1.0, None, ALU.mult)

        def a1_exp(a, i, w):
            a.wait_ge(S("e1_max"), i * GU + (w + 1))
            a.wait_ge(S("e1_p"), freed(i, w, 2, GU))
            a.activation(E1[:, w % 2, :], psum[w % 2][0:R, 0:256], ACT.Exp, bias=bs[:, w, 0:1])
            a.activation(E2[:, w % 2, :], psum[w % 2][0:R, 0:256], ACT.Exp, bias=bs[:, w, 1:2], scale=0.01)
            a.activation(rsc[:, w:w + 1], bs[:, w, 2:3], ACT.Exp).then_inc(S("e1_exp"), 1)

        def v1_prob(v, i, w):
            v.wait_ge(S("e1_exp"), done(i, w, GU))
            v.wait_ge(S("e1_pt"), freed(i, w, 2, GU))
            v.scalar_tensor_tensor(Pm[:, w % 2, :], E1[:, w % 2, :], 1.0, E2[:, w % 2, :], ALU.mult, ALU.max,
                                   accum_out=bs[:, w, 3:4]).then_inc(S("e1_p"), 1)

        def t1_turn(t, i, w):
            t.wait_ge(S("e1_p"), done(i, w, GU))
            t.wait_ge(S("e1_ps"), freed(i, w, 2, GU))
            for k in range(2):
                j = t.transpose(psum[2 + w % 2][:, k * 128:k * 128 + R], Pm[:, w % 2, k * 128:(k + 1) * 128],
                                ident[0:R, 0:R])
            j.then_inc(S("e1_pt"), 1)

        def a1_turned(a, i, w):
            a.wait_ge(S("e1_pt"), done(i, w, GU))
            a.wait_ge(S("e1_sum"), (freed(i, w, 2, GU)) * 2)
            a.copy(Ps[:, w % 2, :, :], psum[2 + w % 2][:, 0:256].rearrange("p (k r) -> p k r", k=2)[:, :, 0:R]
                   ).then_inc(S("e1_ps"), 1)

        LAST1 = G1 // GU - 1

        def a1_rows(a, i, w):
            if w % 2 and i is not LAST1:
                a_rows(a, "e1", i + 1, w // 2)

        def t1_sum(t, i, w):
            t.wait_ge(S("e1_ps"), done(i, w, GU))
            t.wait_ge(S("e1_acc"), freed(i, w, 2, GU))
            for k in range(2):
                t.matmul(psum[4 + w % 2][0:R, 0:D], Ps[:, w % 2, k, :], g1[:, 2 * w + k, 0:D],
                         start=(k == 0), stop=(k == 1)).then_inc(S("e1_sum"), 1)

        def v1_acc(v, i, w):
            blk = group_block(v, i, w)
            a, n_ = turn(AGG[:, ds(blk, 1), :]), den[:, ds(blk, 1)]
            v.drain()
            v.wait_ge(S("e1_sum"), done(i, w, GU) * 2)
            v.scalar_tensor_tensor(a, a, rsc[:, w:w + 1], psum[4 + w % 2][0:R, 0:D], ALU.mult, ALU.add
                                   ).then_inc(S("e1_acc"), 1)
            v.scalar_tensor_tensor(n_, n_, rsc[:, w:w + 1], bs[:, w, 3:4], ALU.mult, ALU.add)

        def skewed(eng, *stages):
            first, last = min(l for l, _ in stages), max(l for l, _ in stages)
            for k in range(first, GU):
                for lag, stage in stages:
                    if k >= lag:
                        stage(eng, 0 if k - lag < GU else 1, (k - lag) % GU)
            with eng.Fori(1, G1 // GU - 1) as i:
                for k in range(GU):
                    for lag, stage in stages:
                        stage(eng, i + (k - lag) // GU, (k - lag) % GU)
            for k in range(G1 - GU, G1 + last):
                for lag, stage in stages:
                    if k - lag < G1:
                        stage(eng, LAST1 if k - lag >= G1 - GU else LAST1 - 1, (k - lag) % GU)

        def v_e1(v):
            seed(v, "e1_p", "e1_acc", n=GU)
            skewed(v, (-2, v1_sel), (0, v1_max), (1, v1_prob), (3, v1_acc))

        def a_e1(a):
            seed(a, "e1_exp", "e1_ps", n=GU)
            for h in range(EU // 4):
                a_rows(a, "e1", 0, h)
            skewed(a, (0, a1_exp), (1, a1_turned), (3, a1_rows))

        def t_e1(t):
            seed(t, "e1_dt", "e1_pt", n=GU)
            t.sem_inc(S("e1_sum"), 2 * GU)
            skewed(t, (-1, t1_mask), (2, t1_sum), (1, t1_turn))

        c = Carver(SCR)
        c(U5, D)
        xT1 = c(U5, 2, R)
        hn = c(U5, D, rows=R)
        rden = c(NT, rows=R)
        hasn = c(NT, rows=R)

        def p_c1(p):
            seed(p, "c1_x")
            with p.Fori(0, NT // U5) as i:
                for u in range(U5):
                    p.wait_ge(S("c1_p"), freed(i, u, U5))
                    p.sem_inc(S("holds_waits"), 1)
                    p.tensor_copy(xT1[:, u, :, :], xnT[:, :, ds((i * U5 + u) * R, R)]).then_inc(S("c1_x"), 1)

        def t_c1(t):
            seed(t, "c1_p")
            with t.Fori(0, NT // U5) as i:
                for u in range(U5):
                    t.wait_ge(S("c1_x"), done(i, u))
                    t.wait_ge(S("c1_d"), freed(i, u, 2))
                    for h in range(2):
                        k = t.matmul(psum[2 + u % 2][0:R, :], xT1[:, u, h, :], wsm[:, h, :],
                                     start=(h == 0), stop=(h == 1))
                    k.then_inc(S("c1_p"), 1)

        def v_c1(v):
            seed(v, "c1_d")
            v.tensor_scalar(has[:, :], den[:, :], 0.0, None, ALU.is_gt)
            v.tensor_scalar(rden[:, :], den[:, :], 1e-30, None, ALU.max)
            v.tensor_tensor(X[:, :, :], X[:, :, :], bc(boutb[0:R, :]), ALU.add)
            v.drain()
            v.reciprocal(rden[:, :], rden[:, :])
            v.tensor_scalar(hasn[:, :], has[:, :], -1.0, 1.0, ALU.mult, ALU.add)
            v.drain()
            with v.Fori(0, NT // U5) as i:
                tiles5 = ds(i * U5, U5)
                x5, xn5, agg5 = X[:, tiles5, :], XN[:, tiles5, :], AGG[:, tiles5, :]
                for u in range(U5):
                    n = ds(i * U5 + u, 1)
                    ps = psum[2 + u % 2]
                    v.wait_ge(S("c1_p"), done(i, u))
                    v.scalar_tensor_tensor(hn[:, u, :], turn(AGG[:, n, :]), rden[:, n], ps[0:R, 0:D], ALU.mult, ALU.add)
                    xr = turn(X[:, n, :])
                    v.tensor_tensor(xr, xr, ps[0:R, D:2 * D], ALU.add).then_inc(S("c1_d"), 1)
                v.drain()
                v.tensor_tensor(hn[:, :, :], hn[:, :, :], has[:, tiles5].unsqueeze(2).broadcast_to([R, U5, D]), ALU.mult)
                v.tensor_tensor(agg5, xn5, hasn[:, tiles5].unsqueeze(2).broadcast_to([R, U5, D]), ALU.mult)
                v.drain()
                v.tensor_tensor(hn[:, :, :], hn[:, :, :], agg5, ALU.add)
                v.drain()
                v.scalar_tensor_tensor(hn[:, :, :], hn[:, :, :], 0.0, xn5, ALU.max, ALU.add)
                v.drain()
                v.tensor_tensor(x5, x5, hn[:, :, :], ALU.add)
                v.drain()

        g2b, b2b, gammab, betab = vec["g2b"], vec["b2b"], vec["gammab"], vec["betab"]
        boutb, gamma1b, beta1b, attb = g2b, b2b, gammab, vec["attb"]
        gb0, gb1 = vec["gb0"], vec["gb1"]

        def halves(w):
            return w.rearrange("(h p) n -> p h n", p=128)

        def row(w):
            return w.rearrange("(a n) -> a n", a=1)

        hamilton = (("r", "i", "j", "k"), ("-i", "r", "k", "-j"), ("-j", "-k", "r", "i"), ("-k", "j", "-i", "r"))
        L0_DENSE = [(wkv[:, :, 0:D], halves(A["L0_mix_Wk"])), (wkv[:, :, D:2 * D], halves(A["L0_mix_Wv"])),
                    (wq, halves(A["L0_mix_Wq"])), (wm, halves(A["L0_mix_Wm"])), (w1, halves(A["L0_mix_W1"])),
                    (w2, halves(A["L0_mix_W2"]))]
        for a_ in range(4):
            for b_ in range(4):
                q_ = "rijk".index(hamilton[a_][b_][-1])
                L0_DENSE.append((ham[(a_ % 2) * 64:(a_ % 2) * 64 + 64, a_ // 2, b_ * 64:(b_ + 1) * 64],
                                 A["L0_gnn_weight"][:, q_ * 64:(q_ + 1) * 64]))
        W0 = len(L0_DENSE)
        L1_DENSE = [(wfx[:, :, 0:D], halves(A["L1_gnn_W_func_T"])), (wsm[:, :, 0:D], halves(A["L1_gnn_W_self_T"])),
                    (wkv1, halves(A["L1_mix_Wqkv_T"])[:, :, HID:3 * HID]), (wout, halves(A["L1_mix_Wout_T"])),
                    (wqo, halves(A["L1_mix_Wqkv"][0:HID, :]))]
        VECTORS = [(g2b, "L0_mix_g2"), (b2b, "L0_mix_b2"), (gammab, "L0_gnn_gamma"), (betab, "L0_gnn_beta"),
                   (gb0, "L0_ffn_gate_b"), (gb1, "L1_ffn_gate_b")]
        VECTORS1 = [(boutb, "L1_mix_bout"), (gamma1b, "L1_ffn_gamma"), (beta1b, "L1_ffn_beta")]
        NVEC = len(VECTORS) + 7
        ew = XN[:, 0:2, :].rearrange("p a b -> p (a b)")[:, 0:EC]
        SCA = NT // U5
        SCB = SC - SCA - M0 // 4
        assert 2 * (SCA + SCB) + M0 // 2 == 2 * SC
        CLEARS = sum(-(-T * 3 // 512) for T in (T0, T1))

        @block.sync
        def _(s):
            for dst, name in ((srcI[:, :], "src"), (dstI[:, :], "dst"), (ew, "edge_weight")):
                s.dma_start(dst, A[name].rearrange("(p c) -> p c", p=R)).then_inc(edges_in, 16)
            s.dma_start(X[:, :, :], tiles(A["x"])).then_inc(x_in, 16)
            for dst, src_ap in L0_DENSE:
                s.dma_start(dst, src_ap).then_inc(w0_raw, 16)
            s.wait_ge(consts, 1)
            for table, T in ((slot0, T0), (slot1, T1)):
                flat = table.rearrange("(p t) r -> p (t r)", p=128)
                for k in range(0, T * 3, 512):
                    w = min(512, T * 3 - k)
                    s.dma_start(flat[:, k:k + w], zeros[:, 0:w]).then_inc(S("slots_clear"), 16)
            for dst, name in VECTORS:
                s.dma_start(dst[:, :], row(A[name]).broadcast_to([128, dst.shape[1]])).then_inc(vec_in, 16)
            s.dma_start(attb[:, :], A["L1_gnn_W_att"].broadcast_to([128, 2 * D + EDIM])).then_inc(vec_in, 16)
            for dst, name in ((g1c, "L0_mix_g1"), (b1c, "L0_mix_b1")):
                for h in range(2):
                    s.dma_start(dst[:, h:h + 1], A[name][h * 128:(h + 1) * 128].rearrange("(p a) -> p a", a=1)
                                ).then_inc(vec_in, 16)
            s.dma_start(gw0[:, :, :], halves(A["L0_ffn_gate_w"])).then_inc(vec_in, 16)
            s.dma_start(gw1[:, :, :], halves(A["L1_ffn_gate_w"])).then_inc(vec_in, 16)
            s_a0(s)
            barrier(s, "sp")
            s_slots(s, (SC, SC), slot0, T0, 1)
            barrier(s, "sp")
            for dst, src_ap in L1_DENSE:
                s.dma_start(dst, src_ap).then_inc(S("w1_in"), 16)
            s_te(s)
            barrier(s, "sp")
            barrier(s, "sp")
            for dst, name in VECTORS1:
                s.dma_start(dst[:, :], row(A[name]).broadcast_to([128, dst.shape[1]])).then_inc(S("L1_vectors_in"), 16)
            s_gate(s, "g0", hrow0)
            barrier(s, "sp")
            s_expert(s, 0, M0, F0, A["L0_ffn_w1"], A["L0_ffn_b1"], A["L0_ffn_w2"], A["L0_ffn_b2"])
            barrier(s, "sp")
            barrier(s, "sp")
            s_a1(s)
            s_slots(s, (SC + SCB + M0 // 2 + SCA, SC + SCB + SCA), slot1, T1, 2)
            barrier(s, "sp")
            barrier(s, "sp")
            barrier(s, "sp")
            s_gate(s, "g1", hrow1)
            barrier(s, "sp")
            s_expert(s, M0 // 2, M1, F1, A["L1_ffn_w1"], A["L1_ffn_b1"], A["L1_ffn_w2"], A["L1_ffn_b2"])
            barrier(s, "sp")
            s_final(s)

        @block.gpsimd
        def _(p):
            p.iota(iotaI[:, :], [[1, MAXG]], base=0, channel_multiplier=0)
            p.iota(nodeI[:, :], [[1, NT]], base=0, channel_multiplier=NT)
            p.memset(ident[:, :], 0.0)
            p.memset(ones[:, :], 1.0)
            p.memset(tri[:, :], 1.0)
            p.memset(zeros[:, :], 0.0)
            p.memset(hm32[:, :], 0.0)
            p.memset(hm64[:, :], 0.0)
            p.memset(eps_t[:, :], EPS)
            p.memset(AGG[:, :, :], 0.0)
            p.drain()
            p.affine_select(out=ident[:, :], in_=ident[:, :], compare_op=ALU.not_equal, fill=1.0, base=0,
                            pattern=[[-1, 128]], channel_multiplier=1)
            p.affine_select(out=tri[:, :], in_=tri[:, :], compare_op=ALU.is_gt, fill=0.0, base=0,
                            pattern=[[1, 128]], channel_multiplier=-1)
            p.drain().then_inc(consts, 1)
            p_a0(p)
            barrier(p, "pool")
            p.wait_ge(S("placed"), 1)
            p.wait_ge(S("slots_clear"), 16 * CLEARS)
            for h in range(2):
                p_scatter(p, h, 0, h, slot0, first=True)
            with p.Fori(1, SC) as i:
                for h in range(2):
                    p_scatter(p, h, i, i * 2 + h, slot0)
            barrier(p, "pool")
            with p.Fori(0, T0 // EU) as i:
                p_gather(p, 0, i, tab0, g0)
            barrier(p, "pool")
            for first, end in ((0, 3), (3, SCB)):
                with p.Fori(first, end) as i:
                    for h in range(2):
                        p_scatter(p, h, SC + i, i * 2 + h, slot1)
                barrier(p, "pool")
            p_expert(p, 0, M0, hrow0, also=lambda i: p_scatter(p, 0, SC + SCB + i, 2 * SCB + i, slot1))
            barrier(p, "pool")
            p_back(p, "m0", 1, ys0)
            barrier(p, "pool")
            p_a1(p)
            barrier(p, "pool")
            with p.Fori(0, T1 // EU) as i:
                p_gather(p, T0 // EU, i, tab1, g1)
            barrier(p, "pool")
            p_c1(p)
            barrier(p, "pool")
            p_keep(p, "g1")
            barrier(p, "pool")
            p_expert(p, M0 // 2, M1, hrow1)
            barrier(p, "pool")
            p_back(p, "m1", 2, ys1)

        @block.vector
        def _(v):
            v.wait_ge(consts, 1)
            v.tensor_copy(iota[:, :], iotaI[:, :])
            v.tensor_copy(node[:, :], nodeI[:, :])
            v.tensor_copy(identb[:, :], ident[:, :])
            for k in range(4):
                v.memset(hm32[k * 32:(k + 1) * 32, k * 32:(k + 1) * 32], 1.0)
            for k in range(2):
                v.memset(hm64[k * 64:(k + 1) * 64, k * 64:(k + 1) * 64], 1.0)
            v.drain()
            v.wait_ge(edges_in, 48)
            v_sort_start(v)
            v_keys(v, srcI, dstI)
            v.tensor_copy(rec[:, :, 2], ew)
            with v.Fori(0, NT) as b:
                v_count(v, EC, b)
            v_totals(v, "s0", NT, GT0)
            with v.Fori(0, NT) as b:
                v_place(v, EC, G0, b)
            v_edges_placed(v, G0, T0, gblk0)
            v.drain().then_inc(S("placed"), 1)
            v.wait_ge(w0_raw, 16 * W0)
            for a_ in range(4):
                for b_ in range(4):
                    if hamilton[a_][b_][0] == "-":
                        h_ = ham[(a_ % 2) * 64:(a_ % 2) * 64 + 64, a_ // 2, b_ * 64:(b_ + 1) * 64]
                        v.tensor_scalar(h_, h_, -1.0, None, ALU.mult)
            v.drain().then_inc(consts, 2)
            v.wait_ge(x_in, 16)
            v_a0(v)
            barrier(v, "dve")
            v.wait_ge(vec_in, 16 * NVEC)
            v_kv(v)
            v.drain().then_inc(S("b0_kvbd"), 1)
            v_b0(v)
            barrier(v, "dve")
            seed(v, "e0_acc", n=EU)
            seed(v, "te_read", n=2)

            def e0_turn(i):
                for u in range(EU + 2):
                    if u < EU:
                        v_sel0(v, i, u)
                    if u >= 2:
                        v_acc0(v, i, u - 2)

            HT = NT // 2
            assert T0 // EU == 2 * HT + 2 and 2 * TC * (2 * HT + 1) == EC
            v_sort_start(v)
            v_keys(v, dstI, srcI)
            with v.Fori(0, HT) as i:
                e0_turn(i)
                v_te(v, i)
                for b in range(2):
                    v_count(v, EC, i * 2 + b)
            e0_turn(HT)
            v_te(v, HT)
            v_count(v, EC, NT - 1)
            v_totals(v, "s1", NT, GT1)
            with v.Fori(0, HT) as i:
                e0_turn(i + (HT + 1))
                v_te(v, i + (HT + 1))
                for b in range(2):
                    v_place(v, EC, G1, i * 2 + b)
            e0_turn(2 * HT + 1)
            v_place(v, EC, G1, NT - 1)
            v_edges_placed(v, G1, T1, gblk1)
            v.drain()
            barrier(v, "dve")
            v_bn(v)
            barrier(v, "dve")
            v_gate(v, "g0", gb0, X0, False)
            v.drain()
            v_choose(v, "g0", X0, K0)
            v_route(v, "r0", K0, X0, M0)
            barrier(v, "dve")
            v_expert(v, 0, M0)
            barrier(v, "dve")
            v_back0(v)
            v.wait_ge(S("w1_in"), 16 * len(L1_DENSE))
            v.wait_ge(S("L1_vectors_in"), 16 * len(VECTORS1))
            v_w1(v)
            barrier(v, "dve")
            v_a1(v)
            barrier(v, "dve")
            v_e1(v)
            barrier(v, "dve")
            v_c1(v)
            barrier(v, "dve")
            v_gate(v, "g1", gb1, X1, True)
            v.drain()
            v_choose(v, "g1", X1, K1)
            v_route(v, "r1", K1, X1, M1)
            barrier(v, "dve")
            v_expert(v, M0 // 2, M1)
            barrier(v, "dve")
            v_back1(v)

        @block.scalar
        def _(a):
            a.wait_ge(consts, 3)
            a_a0(a)
            barrier(a, "act")
            a_b0(a)
            barrier(a, "act")
            with a.Fori(0, T0 // EU) as i:
                for h in range(EU // 4):
                    a_rows(a, "e0", i, h)
            barrier(a, "act")
            a_bn(a)
            barrier(a, "act")
            a_gate(a, "g0")
            a_choose(a, "g0", X0, K0)
            barrier(a, "act")
            a_expert(a, 0, M0, F0, ys0)
            barrier(a, "act")
            barrier(a, "act")
            a_a1(a)
            barrier(a, "act")
            a_e1(a)
            barrier(a, "act")
            barrier(a, "act")
            a_gate(a, "g1")
            a_choose(a, "g1", X1, K1)
            barrier(a, "act")
            a_expert(a, M0 // 2, M1, F1, ys1)
            barrier(a, "act")
            with a.Fori(0, NT // U5) as i:
                a_sqrt(a, BEFORE["fin"], i)

        @block.tensor
        def _(t):
            t.wait_ge(consts, 1)
            t_count(t, "s0", NT)
            t_a0(t)
            barrier(t, "pe")
            t.wait_ge(S("b0_kvbd"), 1)
            t_b0(t)
            barrier(t, "pe")
            seed(t, "e0_sum", n=EU)
            with t.Fori(0, NT // 2 + 1) as i:
                for u in range(EU):
                    t_e0(t, i, u)
            t_count(t, "s1", NT)
            with t.Fori(NT // 2 + 1, T0 // EU) as i:
                for u in range(EU):
                    t_e0(t, i, u)
            barrier(t, "pe")
            t_bn(t, AGG, 0, "bn_agg", "bn_sum")
            t_bn(t, bnm, 1, "bn_sq", "bn_ssq")
            barrier(t, "pe")
            seed(t, "s_used")
            t_gate(t, "g0", gw0, X0)
            t_route(t, "r0", K0, X0, M0)
            barrier(t, "pe")
            t_expert(t, 0, M0, F0)
            barrier(t, "pe")
            barrier(t, "pe")
            t_a1(t)
            barrier(t, "pe")
            t_e1(t)
            barrier(t, "pe")
            t_c1(t)
            barrier(t, "pe")
            t_gate(t, "g1", gw1, X1)
            t_route(t, "r1", K1, X1, M1)
            barrier(t, "pe")
            t_expert(t, M0 // 2, M1, F1)
            barrier(t, "pe")


_INS = ("x", "src", "dst", "edge_attr_64", "edge_weight", "L0_gnn_weight", "L0_gnn_gamma", "L0_gnn_beta",
        "L0_mix_Wq", "L0_mix_Wk", "L0_mix_Wv", "L0_mix_Wm", "L0_mix_W1", "L0_mix_W2", "L0_mix_g1", "L0_mix_b1",
        "L0_mix_g2", "L0_mix_b2", "L0_ffn_gate_w", "L0_ffn_gate_b", "L0_ffn_w1", "L0_ffn_b1", "L0_ffn_w2",
        "L0_ffn_b2", "L1_gnn_W_self", "L1_gnn_W_func", "L1_gnn_W_att", "L1_mix_Wqkv", "L1_mix_Wout",
        "L1_mix_bout", "L1_ffn_gate_w", "L1_ffn_gate_b", "L1_ffn_w1", "L1_ffn_b1", "L1_ffn_w2", "L1_ffn_b2",
        "L1_ffn_gamma", "L1_ffn_beta")
_TURNED = ("L1_gnn_W_func", "L1_gnn_W_self", "L1_mix_Wqkv", "L1_mix_Wout")


def kernel(**inputs):
    import numpy as _np
    import concourse.bacc as _bacc
    from concourse import mybir as _mybir
    from concourse.bass_utils import run_bass_kernel_spmd as _run

    laid = {n: _np.ascontiguousarray(inputs[n]) for n in _INS}
    for n in _TURNED:
        laid[n + "_T"] = _np.ascontiguousarray(_np.transpose(laid[n]))
    for n in ("L1_gnn_W_func", "L1_gnn_W_self", "L1_mix_Wout"):
        del laid[n]
    nc = _bacc.Bacc("TRN2", target_bir_lowering=False, num_devices=1)
    arrays, A = {}, {}
    for n, a in laid.items():
        arrays["in_" + n] = a
        A[n] = nc.dram_tensor("in_" + n, a.shape, _mybir.dt.from_np(a.dtype), kind="ExternalInput").ap()
    out = nc.dram_tensor("out", (N, D), F32, kind="ExternalOutput").ap()
    gps_kernel(nc, A, out)
    r = _run(nc, [arrays], core_ids=[0])
    return r.results[0]["out"]
```

```python
from contextlib import ExitStack

import concourse.bass as bass
from concourse import mybir

ALU = mybir.AluOpType
ACT = mybir.ActivationFunctionType
F32 = mybir.dt.float32
BF16 = mybir.dt.bfloat16
I32 = mybir.dt.int32
AX_X = mybir.AxisListType.X
ds = bass.ds

N, D = 3125, 256
NT = 25
R = N // NT
E = 50000
EC = E // R
HID = 512
EDIM = 64
U5 = 5
EPS = 1e-5
BIG = 2.0 ** 100
LOWEST = -1e20
TOKS = ((0, 2), (2, 3))

GT0, GT1 = 2, 4
EU = 16
EU1 = 32


def slots(count, blocks, gt):
    size = 128 * gt
    return (count + blocks * (size - 1)) // size


G0 = -(-slots(E, NT, GT0) * GT0 // EU) * EU // GT0
G1 = -(-slots(E, NT, GT1) * GT1 // EU1) * EU1 // GT1
T0, T1 = G0 * GT0, G1 * GT1
ROW1 = D + 2

X0, F0, K0 = 8, 1024, 1
X1, F1, K1 = 16, 512, 2
CAP = -(-5 * N // (4 * X0))
GX0, GX1 = -(-CAP // 128), 2
NG0 = X0
NG1 = -(-slots(N * K1, X1, GX1) // 2) * 2
M0, M1 = NG0 * GX0, NG1 * GX1
MAXG = max(G0, G1, 128)
SH = 8
SC = EC // (2 * SH)


def done(i, u, per=U5):
    return i * per + (u + 1 + per)


def freed(i, u, bufs, per=U5):
    before = u - bufs if u >= bufs else max(w for w in range(per) if w % bufs == u % bufs) - per
    return i * per + (before + 1 + per)


def landed(turns):
    return 16 * (turns + 1)


def gathered(turns, per):
    return 16 * per * turns


def gps_kernel(nc, A, out):
    ctx = ExitStack()
    with ctx:
        def sb(name, shape, dt=F32):
            return ctx.enter_context(nc.sbuf_tensor(name, shape, dt))

        def sem(name):
            return ctx.enter_context(nc.semaphore(name))

        X = sb("X", [R, NT, D])
        AGG = sb("AGG", [R, NT, D])
        XN = sb("XN", [R, NT, D])
        xnT = sb("xnT", [128, 2, N])
        WD = sb("WD", [128, 5636])
        SCR = sb("SCR", [128, 12320])
        iota = sb("iota", [128, MAXG])
        ident = sb("ident", [128, 128])
        nident = sb("nident", [128, 128], BF16)
        ones = sb("ones", [128, 128])
        tri = sb("tri", [128, 128])
        zeros = sb("zeros", [128, 512])
        node = sb("node", [R, NT])
        hm32 = sb("hm32", [128, 128])
        hm64 = sb("hm64", [128, 128])
        eps_t = sb("eps_t", [128, 1])
        srcI = sb("srcI", [R, EC], I32)
        dstI = sb("dstI", [R, EC], I32)
        rec = sb("rec", [R, EC, 3])
        place = sb("place", [R, EC], I32)
        recS = sb("recS", [R, 2, SH, 3])
        placeS = sb("placeS", [R, 2, SH], I32)
        gi = sb("gi", [128, EU1], I32)
        slots_ = sb("slots", [128, T1, 3])
        gblk0 = sb("gblk0", [128, G0], I32)
        gblk1 = sb("gblk1", [128, G1], I32)
        gblkX = sb("gblkX", [128, NG1], I32)
        st6 = sb("st6", [R, U5, 6])
        mv = sb("mv", [R, U5, 2])
        sd = sb("sd", [R, U5])
        rs = sb("rs", [R, U5])
        gwt = sb("gwt", [R, 2, NT])
        slotI = sb("slotI", [R, 2 * NT], I32)
        idxX = sb("idxX", [128, M1], I32)

        psum = [ctx.enter_context(nc.psum_tensor(f"bank{b}", [128, 512], F32)) for b in range(8)]

        class Carver:
            def __init__(self, t):
                self.t, self.at = t, 0

            def __call__(self, *shape, rows=128, dt=F32):
                n = 1
                for k in shape:
                    n *= k
                v = self.t[0:rows, self.at:self.at + n]
                self.at += n
                assert self.at <= self.t.shape[1], (self.at, shape)
                if dt is not F32:
                    v = v.bitcast(dt)
                if len(shape) == 2:
                    v = v.rearrange("p (a b) -> p a b", a=shape[0])
                if len(shape) == 3:
                    v = v.rearrange("p (a b c) -> p a b c", a=shape[0], b=shape[1])
                return v

        c = Carver(SCR)
        iotaI = c(MAXG, dt=I32)
        nodeI = c(NT, rows=R, dt=I32)

        dram = lambda name, shape: nc.dram_tensor(name, shape, F32, kind="Internal").ap()
        tab0 = dram("tab0", [N, D])
        tab1 = dram("tab1", [N, ROW1])
        slot0 = dram("slot0", [128 * T0, 3])
        slot1 = dram("slot1", [128 * T1, 3])
        hrow0 = dram("hrow0", [N, D])
        hrow1 = dram("hrow1", [N, D])
        ys0 = dram("ys0", [M0 * 128, D])
        ys1 = dram("ys1", [M1 * 128, D])

        def tiles(t):
            return t.rearrange("(p j) d -> p j d", j=NT)

        c = Carver(WD)
        wkv = c(2, 2 * D)
        ham = c(2, D)
        wq = c(2, D)
        wm = c(2, D)
        w1 = c(4, HID)
        w2 = c(4, D)
        c = Carver(WD)
        wfx = c(2, ROW1)
        wsm = c(2, 2 * D)
        wkv1 = c(2, 2 * HID)
        wout = c(4, D)
        wqo = c(4, D)

        vec = {n: sb(n, [128, w]) for n, w in (
            ("g2b", D), ("b2b", D), ("gammab", D), ("betab", D),
            ("attb", 2 * D + EDIM), ("gb0", X0), ("gb1", X1))}
        gw0 = sb("gw0", [128, 2, X0])
        gw1 = sb("gw1", [128, 2, X1])
        LG = sb("LG", [R, NT, X1])
        dm = sb("dm", [R, NT, 3])
        den = sb("den", [R, NT])
        has = sb("has", [R, NT])
        g1c = sb("g1c", [128, 2])
        b1c = sb("b1c", [128, 2])

        bar = sem("all_engines_here")
        consts = sem("constants_ready")
        x_in = sem("x_in")
        edges_in = sem("edges_in")
        w0_raw = sem("L0_dense_weights_in")
        vec_in = sem("L0_vectors_in")
        step = {}

        def S(name):
            if name not in step:
                step[name] = sem(name)
            return step[name]

        block = ctx.enter_context(nc.Block())
        barriers = {}

        def barrier(eng, key):
            barriers[key] = barriers.get(key, 0) + 1
            eng.drain().then_inc(bar, 1)
            eng.wait_ge(bar, 5 * barriers[key])


        def turn(ap):
            return ap.rearrange("p a d -> p (a d)")

        c = Carver(SCR)
        xs = c(U5, D, rows=R)
        xT = c(U5, 2, R)
        norm_end = c.at

        BEFORE = {ph: n * (NT // U5) for n, ph in enumerate(("a0", "g0", "a1", "g1", "fin"))}

        def v_norm(v, b, i, kept):
            for u in range(U5):
                v.bn_stats(st6[:, u, :], turn(X[:, ds(i * U5 + u, 1), :]))
            v.drain()
            for u in range(U5):
                k = v.bn_aggr(mv[:, u, :], st6[:, u, :])
            k.then_inc(S("x_var"), 1)
            v.wait_ge(S("x_sd"), b + i + 1)
            v.reciprocal(rs[:, :], sd[:, :])
            v.drain()
            v.wait_ge(S("x_turned"), freed(b + i, U5 - 1, U5))
            kept()
            for u in range(U5):
                v.tensor_scalar(xs[:, u, :], turn(X[:, ds(i * U5 + u, 1), :]), mv[:, u, 0:1],
                                rs[:, u:u + 1], ALU.subtract, ALU.mult).then_inc(S("x_xs"), 1)

        def a_sqrt(a, b, i):
            a.wait_ge(S("x_var"), b + i + 1)
            a.activation(sd[:, :], mv[:, :, 1], ACT.Sqrt, bias=eps_t[0:R, 0:1]).then_inc(S("x_sd"), 1)

        def half(u):
            return psum[u % 2][:, 0:256].rearrange("p (h r) -> p h r", h=2)

        def t_turn(t, b, i, u):
            t.wait_ge(S("x_xs"), (b + i) * U5 + (u + 1))
            t.wait_ge(S("x_xT"), freed(b + i, u, 2))
            for h in range(2):
                k = t.transpose(half(u)[:, h, 0:R], xs[:, u, h * 128:(h + 1) * 128], ident[0:R, 0:R])
            k.then_inc(S("x_turned"), 1)

        def a_turned(a, b, i, u, users, keep=False):
            a.wait_ge(S("x_turned"), done(b + i, u))
            users()
            if keep:
                a.wait_ge(consts, 1)
                a.copy(xnT[:, :, ds((i * U5 + u) * R, R)], half(u)[:, :, 0:R])
            a.copy(xT[:, u, :, :], half(u)[:, :, 0:R]).then_inc(S("x_xT"), 1)

        def seed(eng, *names, n=U5):
            for name in names:
                eng.sem_inc(S(name), n)

        c = Carver(SCR)
        c.at = norm_end
        ek = c(U5, D, rows=R)
        Kt = c(U5, D, rows=R)
        Vt = c(U5, 2, 129, rows=R)
        sup = c(U5, D, rows=R)

        def t_a0(t):
            seed(t, "x_turned", "a0_kv", "a0_sup", "a0_KV")
            t.wait_ge(consts, 3)
            t_bounds(t, 258, True, (4,))
            with t.Fori(0, NT // U5) as i:
                for u in range(U5):
                    t_turn(t, 0, i, u)

                def sums(u):
                    t.wait_ge(S("a0_K"), done(i, u))
                    t.wait_ge(S("a0_V"), done(i, u))
                    for h in range(2):
                        k = t.matmul(psum[4][:, h * 129:(h + 1) * 129], Kt[:, u, h * 128:(h + 1) * 128], Vt[:, u, h, :],
                                     start=False, stop=False, skip_group_check=True)
                    k.then_inc(S("a0_KV"), 1)

                for u in range(U5):
                    t.wait_ge(S("x_xT"), done(i, u))
                    t.wait_ge(S("a0_K"), freed(i, u, 2))
                    for h in range(2):
                        k = t.matmul(psum[2 + u % 2][0:R, :], xT[:, u, h, :], wkv[:, h, :],
                                     start=(h == 0), stop=(h == 1))
                    k.then_inc(S("a0_kv"), 1)
                    t.wait_ge(S("a0_supc"), freed(i, u, 2))
                    for h in range(2):
                        k = t.matmul(psum[5 + u % 2][0:R, 0:D], xT[:, u, h, :], ham[:, h, :],
                                     start=(h == 0), stop=(h == 1))
                    k.then_inc(S("a0_sup"), 1)
                    if u:
                        sums(u - 1)
                sums(U5 - 1)
            t_bounds(t, 258, False, (4,))

        def a_a0(a):
            seed(a, "x_xT", "a0_V", "a0_ek")
            with a.Fori(0, NT // U5) as i:
                a_sqrt(a, 0, i)
                for u in range(U5):
                    a_turned(a, 0, i, u, lambda: a.wait_ge(S("a0_sup"), freed(i, u, U5)), keep=True)
                for u in range(U5):
                    a.wait_ge(S("a0_kv"), done(i, u))
                    a.wait_ge(S("a0_K"), freed(i, u, U5))
                    a.activation(ek[:, u, :], psum[2 + u % 2][0:R, 0:D], ACT.Exp).then_inc(S("a0_ek"), 1)
                    a.wait_ge(S("a0_KV"), freed(i, u, U5))
                    a.copy(Vt[:, u, :, 0:128], psum[2 + u % 2][0:R, D:2 * D].rearrange("p (h f) -> p h f", h=2)
                           ).then_inc(S("a0_V"), 1)

        def v_a0(v):
            seed(v, "a0_K", "a0_supc")
            v.memset(Vt[:, :, :, 128:129].rearrange("p u h o -> p (u h) o"), 1.0)
            with v.Fori(0, NT // U5) as i:
                v_norm(v, 0, i, lambda: None)
                v.drain()
                x5 = X[:, ds(i * U5, U5), :]
                v.tensor_tensor(x5, x5, xs[:, :, :], ALU.add)
                for u in range(U5):
                    v.wait_ge(S("a0_ek"), done(i, u))
                    v.tensor_scalar(ek[:, u, :], ek[:, u, :], 1.0, None, ALU.min)
                    v.drain()
                    v.wait_ge(S("a0_KV"), freed(i, u, U5))
                    v.wait_ge(S("a0_V"), done(i, u))
                    v.scalar_tensor_tensor(Kt[:, u, :], psum[2 + u % 2][0:R, 0:D], 0.0, ek[:, u, :],
                                           ALU.max, ALU.add).then_inc(S("a0_K"), 1)
                    v.wait_ge(S("a0_sup"), done(i, u))
                    v.wait_ge(S(f"a_out{u}"), landed(i))
                    v.wait_ge(consts, 1)
                    v.tensor_copy(sup[:, u, :], psum[5 + u % 2][0:R, 0:D]).then_inc(S("a0_supc"), 1)

        def s_a0(s):
            seed(s, *(f"a_out{u}" for u in range(U5)), n=16)
            with s.Fori(0, NT // U5) as i:
                for u in range(U5):
                    s.wait_ge(S("a0_supc"), done(i, u))
                    s.dma_start(tiles(tab0)[:, ds(i * U5 + u, 1), :].rearrange("p a d -> p (a d)"), sup[:, u, :]
                                ).then_inc(S(f"a_out{u}"), 16)
            for u in range(U5):
                s.wait_ge(S(f"a_out{u}"), landed(NT // U5))

        c = Carver(SCR)
        kvbd = c(2, 128)
        ksx = c(2, 128)
        WMAX = 3 * R
        eq = c(2, WMAX)
        QT = c(2, WMAX)
        dn = c(2, WMAX)
        msgT = c(2, WMAX)
        mn = c(3, D, rows=R)
        mT = c(2, WMAX)
        hT = c(4, WMAX)
        yr = c(3, D, rows=R)

        def v_kv(v):
            for h in range(2):
                v.scalar_tensor_tensor(kvbd[:, h, :], psum[4][:, h * 129:h * 129 + 128], 1.0 / N, hm32[:, :], ALU.mult, ALU.mult)
                v.tensor_scalar(ksx[:, h, :], hm32[:, :], psum[4][:, h * 129 + 128:h * 129 + 129], None, ALU.mult)

        def row_ps(k):
            return psum[4 + k // 2][0:R, (k % 2) * 256:(k % 2) * 256 + 256]

        def runs(eng, run_):
            def both(i):
                run_(i * 2, i * U5, TOKS[0][1], i * U5 + TOKS[1][0], TOKS[1][1])
                run_(i * 2 + 1, i * U5 + TOKS[1][0], TOKS[1][1], i * U5 + U5, TOKS[0][1])

            with eng.Fori(0, NT // U5 - 1) as i:
                both(i)
            i = NT // U5 - 1
            run_(i * 2, i * U5, TOKS[0][1], i * U5 + TOKS[1][0], TOKS[1][1])
            run_(i * 2 + 1, i * U5 + TOKS[1][0], TOKS[1][1], None, 0)

        def t_q(t, tile, nt):
            for f in range(2):
                for h in range(2):
                    k = t.matmul(psum[f][:, 0:nt * R], wq[:, h, f * 128:(f + 1) * 128], xnT[:, h, ds(tile * R, nt * R)],
                                 start=(h == 0), stop=(h == 1))
            k.then_inc(S("b0_q"), 1)

        def t_b0(t):
            t_q(t, 0, TOKS[0][1])

            def one(n, tile, nt, next_tile, next_nt):
                w = nt * R
                cols = ds(tile * R, w)

                def hidden(f, halves_):
                    for h in halves_:
                        src_t = xnT[:, h, cols] if h < 2 else mT[:, h - 2, 0:w]
                        k = t.matmul(psum[6 + f % 2][:, 0:w], w1[:, h, f * 128:(f + 1) * 128], src_t,
                                     start=(h == 0), stop=(h == 3))
                    return k

                t.wait_ge(S("b0_Q"), n + 1)
                t.wait_ge(S("b0_x"), n + 1)
                for h in range(2):
                    t.matmul(psum[2 + 2 * h][:, 0:w], kvbd[:, h, :], QT[:, h, 0:w], start=True, stop=True)
                    t.matmul(psum[3 + 2 * h][:, 0:w], ksx[:, h, :], QT[:, h, 0:w], start=True, stop=True
                             ).then_inc(S("b0_nd"), 1)
                for f in range(2):
                    t.wait_ge(S("b0_h"), n * 4 + (f + 2))
                    hidden(f, (0, 1))
                t.wait_ge(S("b0_msg"), n * 2 + 2)
                for j in range(nt):
                    for h in range(2):
                        k = t.matmul(row_ps(j), msgT[:, h, j * R:(j + 1) * R], wm[:, h, :],
                                     start=(h == 0), stop=(h == 1))
                k.then_inc(S("b0_m"), 1)
                t.wait_ge(S("b0_mn"), n + 1)
                for h in range(2):
                    for j in range(nt):
                        k = t.transpose(psum[h][:, j * R:(j + 1) * R], mn[:, j, h * 128:(h + 1) * 128],
                                        ident[0:R, 0:R])
                k.then_inc(S("b0_mt"), 1)
                t.wait_ge(S("b0_mT"), n + 1)
                for f in range(4):
                    if f >= 2:
                        t.wait_ge(S("b0_h"), n * 4 + (f + 2))
                    hidden(f, (2, 3) if f < 2 else (0, 1, 2, 3)).then_inc(S("b0_hp"), 1)
                if next_tile is not None:
                    t_q(t, next_tile, next_nt)
                t.wait_ge(S("b0_h"), n * 4 + 7)
                for j in range(nt):
                    for f in range(4):
                        k = t.matmul(row_ps(j), hT[:, f, j * R:(j + 1) * R], w2[:, f, :],
                                     start=(f == 0), stop=(f == 3))
                k.then_inc(S("b0_y"), 1)

            runs(t, one)

        def a_q(a, n, nt):
            a.wait_ge(S("b0_q"), n + 1)
            for f in range(2):
                a.activation(eq[:, f, 0:nt * R], psum[f][:, 0:nt * R], ACT.Exp).then_inc(S("b0_eq"), 1)

        def a_b0(a):
            a.sem_inc(S("b0_h"), 3)
            a_q(a, 0, TOKS[0][1])

            def one(n, tile, nt, next_tile, next_nt):
                w = nt * R
                a.wait_ge(S("b0_var1"), n + 1)
                a.activation(sd[:, 0:nt], mv[:, 0:nt, 1], ACT.Sqrt, bias=eps_t[0:R, 0:1]).then_inc(S("b0_sd1"), 1)
                a.wait_ge(S("b0_mt"), n + 1)
                for h in range(2):
                    k = a.activation(mT[:, h, 0:w], psum[h][:, 0:w], ACT.Identity, bias=b1c[:, h:h + 1],
                                     scale=g1c[:, h:h + 1])
                k.then_inc(S("b0_mT"), 1)
                for f in range(4):
                    a.wait_ge(S("b0_hp"), n * 4 + (f + 1))
                    a.activation(hT[:, f, 0:w], psum[6 + f % 2][:, 0:w], ACT.Relu).then_inc(S("b0_h"), 1)
                if next_tile is not None:
                    a_q(a, n + 1, next_nt)
                a.wait_ge(S("b0_var2"), n + 1)
                a.activation(sd[:, 0:nt], mv[:, 0:nt, 1], ACT.Sqrt, bias=eps_t[0:R, 0:1]).then_inc(S("b0_sd2"), 1)

            runs(a, one)

        def v_rows_norm(v, nt, ps, dst, var, sdn, n, free):
            for j in range(nt):
                v.bn_stats(st6[:, j, :], ps(j))
            v.drain()
            for j in range(nt):
                k = v.bn_aggr(mv[:, j, :], st6[:, j, :])
            k.then_inc(S(var), 1)
            v.wait_ge(S(sdn), n + 1)
            v.reciprocal(rs[:, 0:nt], sd[:, 0:nt])
            v.drain()
            free()
            for j in range(nt):
                k = v.tensor_scalar(dst[:, j, :], ps(j), mv[:, j, 0:1], rs[:, j:j + 1], ALU.subtract, ALU.mult)
            return k

        def v_q(v, n, nt):
            w = nt * R
            v.wait_ge(S("b0_eq"), n * 2 + 2)
            v.tensor_scalar(eq[:, :, 0:w], eq[:, :, 0:w], 1.0, None, ALU.min)
            v.drain()
            for f in range(2):
                k = v.scalar_tensor_tensor(QT[:, f, 0:w], psum[f][:, 0:w], 0.0, eq[:, f, 0:w], ALU.max, ALU.add)
            k.then_inc(S("b0_Q"), 1)

        def v_b0(v):
            seed(v, "b0_x", n=1)
            v_q(v, 0, TOKS[0][1])

            def one(n, tile, nt, next_tile, next_nt):
                w = nt * R
                for h in range(2):
                    v.wait_ge(S("b0_nd"), n * 2 + (h + 1))
                    v.tensor_scalar(dn[:, h, 0:w], psum[3 + 2 * h][:, 0:w], 1e-6, None, ALU.add)
                v.drain()
                v.reciprocal(dn[:, :, 0:w], dn[:, :, 0:w])
                v.drain()
                for h in range(2):
                    v.scalar_tensor_tensor(msgT[:, h, 0:w], psum[2 + 2 * h][:, 0:w], float(N), dn[:, h, 0:w],
                                           ALU.mult, ALU.mult).then_inc(S("b0_msg"), 1)
                v.wait_ge(S("b0_m"), n + 1)
                v.wait_ge(consts, 1)
                v_rows_norm(v, nt, row_ps, mn, "b0_var1", "b0_sd1", n, lambda: None).then_inc(S("b0_mn"), 1)
                if next_tile is not None:
                    v_q(v, n + 1, next_nt)
                v.drain()
                v.wait_ge(S("b0_y"), n + 1)
                v.wait_ge(consts, 1)
                v_rows_norm(v, nt, row_ps, yr, "b0_var2", "b0_sd2", n, lambda: None).then_inc(S("b0_x"), 1)
                v.drain()
                v.tensor_tensor(yr[:, 0:nt, :], yr[:, 0:nt, :], g2b[0:R, :].unsqueeze(1).broadcast_to([R, nt, D]), ALU.mult)
                v.drain()
                xr = X[:, ds(tile, nt), :]
                v.tensor_tensor(xr, xr, yr[:, 0:nt, :], ALU.add)
                v.drain()
                v.tensor_tensor(xr, xr, b2b[0:R, :].unsqueeze(1).broadcast_to([R, nt, D]), ALU.add)

            runs(v, one)

        c = Carver(SCR)
        blkF = c(EC, rows=R)
        loI = c(EC, rows=R, dt=I32)
        inb = c(2, EC, rows=R, dt=I32)
        run = c(2, EC, rows=R)
        pos = c(EC, rows=R)
        bsum = c(EC, rows=R)
        posI = c(EC, rows=R, dt=I32)
        tI = loI
        one_row = c(EC, rows=R)
        tF = c(EC, rows=R)
        qF = c(EC, rows=R)
        packed = c(2 * NT, rows=R)
        cnt = c(NT, rows=R)
        ngI = c(NT, dt=I32)
        ngF = c(NT)
        cum = c(NT)
        base = c(NT)
        offs = c(NT, rows=R)
        gbF = c(MAXG)
        sort_end = c.at
        SORT = {"s0": 1, "s1": 2, "r0": 3, "r1": 4}
        MOVED = {"r0": 0, "r1": K0 * NT}

        def v_keys(v, keyI, idxI):
            v.tensor_scalar(loI[:, :], keyI[:, :], 1311.0, None, ALU.mult)
            v.drain()
            v.tensor_scalar(loI[:, :], loI[:, :], 15, None, ALU.logical_shift_right)
            v.drain()
            v.scalar_tensor_tensor(blkF[:, :], loI[:, :], -float(NT), keyI[:, :], ALU.mult, ALU.add)
            v.tensor_scalar(rec[:, :, 0], loI[:, :], 1.0, None, ALU.add)
            v.tensor_copy(rec[:, :, :].bitcast(I32)[:, :, 1], idxI[:, :])
            v.drain()

        def v_sort_start(v):
            for t, x in ((pos, 0.0), (bsum, 0.0), (gbF, 0.0), (one_row, 1.0)):
                v.memset(t[:, :], x)
            v.drain()

        def v_count(v, C, *blocks_):
            for n, b in enumerate(blocks_):
                v.tensor_scalar(inb[:, n, 0:C], blkF[:, 0:C], iota[0:R, ds(b, 1)], 0.0, ALU.is_equal, ALU.add,
                                accum_out=cnt[:, ds(b, 1)])
            v.drain()

        def t_count(t, ph, K):
            t.wait_ge(S("s_cnt"), SORT[ph])
            t.matmul(psum[0][:, 0:K], ones[0:R, :], cnt[:, 0:K], start=True, stop=True)
            t.matmul(psum[1][0:R, 0:K], tri[0:R, 0:R], cnt[:, 0:K], start=True, stop=True
                     ).then_inc(S("s_tot"), 1)

        def v_totals(v, ph, K, gt, fixed=False):
            shift = (128 * gt).bit_length() - 1
            v.drain().then_inc(S("s_cnt"), 1)
            v.wait_ge(S("s_tot"), SORT[ph])
            v.tensor_scalar(ngI[:, 0:K], psum[0][:, 0:K], float(128 * gt - 1), None, ALU.add)
            v.drain()
            v.tensor_scalar(ngI[:, 0:K], ngI[:, 0:K], shift, None, ALU.logical_shift_right)
            v.drain()
            v.tensor_copy(ngF[:, 0:K], ngI[:, 0:K])
            v.drain()
            v.tensor_tensor_scan(cum[:, 0:K], ones[:, 0:K], ngF[:, 0:K], 0.0, ALU.mult, ALU.add)
            v.drain()
            v.tensor_tensor(base[:, 0:K], cum[:, 0:K], ngF[:, 0:K], ALU.subtract)
            v.drain()
            v.tensor_scalar(base[:, 0:K], iota[:, 0:K] if fixed else base[:, 0:K], float(128 * gt), None, ALU.mult)
            v.drain()
            v.scalar_tensor_tensor(offs[:, 0:K], psum[1][0:R, 0:K], -1.0, base[0:R, 0:K], ALU.add, ALU.add)
            v.drain()

        def v_place(v, C, G, *blocks_, bases=False):
            def passed(b):
                v.scalar_tensor_tensor(gbF[:, 0:G], iota[:, 0:G], cum[:, ds(b, 1)], gbF[:, 0:G], ALU.is_ge, ALU.add)

            for n, b in enumerate(blocks_):
                v.tensor_scalar(inb[:, n, 0:C], blkF[:, 0:C], iota[0:R, ds(b, 1)], None, ALU.is_equal)
            passed(blocks_[0])
            v.drain()
            for n, b in enumerate(blocks_):
                v.tensor_tensor_scan(run[:, n, 0:C], one_row[0:R, 0:C], inb[:, n, 0:C], offs[:, ds(b, 1)],
                                     ALU.mult, ALU.add)
            if bases:
                v.scalar_tensor_tensor(bsum[:, 0:C], inb[:, 0, 0:C], base[0:R, ds(blocks_[0], 1)], bsum[:, 0:C],
                                       ALU.mult, ALU.add)
            v.drain()
            v.copy_predicated(pos[:, 0:C], inb[:, 0, 0:C], run[:, 0, 0:C])
            for n, b in list(enumerate(blocks_))[1:]:
                passed(b)
                v.drain()
                v.copy_predicated(pos[:, 0:C], inb[:, n, 0:C], run[:, n, 0:C])
            if bases:
                for n, b in list(enumerate(blocks_))[1:]:
                    v.scalar_tensor_tensor(bsum[:, 0:C], inb[:, n, 0:C], base[0:R, ds(b, 1)], bsum[:, 0:C],
                                           ALU.mult, ALU.add)
            v.drain()

        def v_placed(v, C, K, G, gblk):
            v.tensor_scalar(gbF[:, 0:G], gbF[:, 0:G], float(K - 1), None, ALU.min)
            v.tensor_copy(posI[:, 0:C], pos[:, 0:C])
            v.drain()
            v.tensor_copy(gblk[:, 0:G], gbF[:, 0:G])
            v.tensor_scalar(tI[:, 0:C], posI[:, 0:C], 7, None, ALU.logical_shift_right)
            v.tensor_scalar(posI[:, 0:C], posI[:, 0:C], 127, None, ALU.bitwise_and)
            v.drain()

        def v_edges_placed(v, G, T, gblk):
            v_placed(v, EC, NT, G, gblk)
            v.scalar_tensor_tensor(place[:, :], posI[:, :], float(T), tI[:, :], ALU.mult, ALU.add)
            v.drain()

        def p_scatter(p, h, sent, i, table, first=False):
            if not first:
                p.wait_ge(S(f"sent{h}"), 16 * SH * sent)
            p.sem_inc(S("holds_waits"), 1)
            p.tensor_copy(recS[:, h, :, :], rec[:, ds(i * SH, SH), :]).then_inc(S("aside_rec"), 1)
            p.tensor_copy(placeS[:, h, :], place[:, ds(i * SH, SH)]).then_inc(S("aside"), 1)
            p.wait_ge(S("aside_rec"), sent * 2 + (h + 1))
            p.wait_ge(S("aside"), sent * 2 + (h + 1))
            p.sem_inc(S("holds_waits"), 1)
            for k in range(SH):
                p.indirect_dma_start(table, bass.IndirectOffsetOnAxis(ap=placeS[:, h, k:k + 1], axis=0),
                                     recS[:, h, k, :], None).then_inc(S(f"sent{h}"), 16)

        def s_slots(s, sent, table, T, n):
            for h in range(2):
                s.wait_ge(S(f"sent{h}"), 16 * SH * sent[h])
            s.dma_start(slots_[:, 0:T, :], table.rearrange("(p t) r -> p t r", p=128)).then_inc(S("slots_in"), 16)
            s.wait_ge(S("slots_in"), 16 * n)

        OB = 4
        c = Carver(SCR)
        c.at = sort_end
        tF = c(2 * NT, rows=R)
        qF = c(2 * NT, rows=R)
        ot = c(OB, 128, rows=R)
        oq = c(OB, 128, rows=R)
        move_end = c.at

        def v_onehot(v, ph, i, u, T, per):
            col = i * per + u
            v.wait_ge(S("s_used"), freed(i, u, OB, per) + MOVED[ph])
            v.tensor_scalar(ot[:, u % OB, 0:T], iota[0:R, 0:T], tF[:, ds(col, 1)], None, ALU.is_equal)
            v.tensor_scalar(oq[:, u % OB, :], iota[0:R, 0:128], qF[:, ds(col, 1)], packed[:, ds(col, 1)],
                            ALU.is_equal, ALU.mult).then_inc(S("s_onehot"), 1)

        def t_move(t, ph, i, u, T, per):
            t.wait_ge(S("s_onehot"), i * per + (u + 1 + MOVED[ph]))
            t.matmul(psum[6][:, 0:T], oq[:, u % OB, :], ot[:, u % OB, 0:T], start=False, stop=False,
                     skip_group_check=True).then_inc(S("s_used"), 1)

        def t_bounds(t, T, start, banks):
            for b in banks:
                k = t.matmul(psum[b][:, 0:T], zeros[:, 0:128], zeros[:, 0:T], start=start, stop=not start,
                             skip_group_check=True)
            return k

        c = Carver(SCR)
        c.at = sort_end
        g0 = c(EU, D)
        s0 = c(EU, R)

        def a_rows(a, ph, i, w):
            gt, per = (GT0, EU) if ph == "e0" else (GT1, EU1)
            a.wait_ge(S(ph + "_sum"), freed(i, w * gt + gt - 1, per, per))
            a.wait_ge(consts, 1)
            a.copy(gi[:, w * gt:(w + 1) * gt], slots_[:, :, :].bitcast(I32)[:, ds(i * per + w * gt, gt), 1]
                   ).then_inc(S("rows"), 1)

        def p_gather(p, before, i, gt, per, table, dst):
            for w in range(per // gt):
                p.wait_ge(S("rows"), i * (per // gt) + (w + 1 + before))
                p.sem_inc(S("holds_waits"), 1)
                for u in range(w * gt, (w + 1) * gt):
                    p.indirect_dma_start(dst[:, u, :], None, table,
                                         bass.IndirectOffsetOnAxis(ap=gi[:, u:u + 1], axis=0)
                                         ).then_inc(S(f"e_g{w}"), 16)

        def v_sel0(v, i, u):
            t = i * EU + u
            v.wait_ge(S("e0_sum"), freed(i, u, EU, EU))
            v.tensor_scalar(s0[:, u, :], iota[:, 1:R + 1], slots_[:, ds(t, 1), 0], slots_[:, ds(t, 1), 2],
                            ALU.is_equal, ALU.mult).then_inc(S("e0_sel"), 1)

        GU0 = EU // GT0

        def load_blocks(table, first, n):
            return nc.values_load_multi_w_load_instructions(
                table[0:1, ds(first, n)], engines=[mybir.EngineType.DVE], min_val=0, max_val=NT - 1,
                skip_runtime_bounds_check_because="v_placed keeps a group's block between 0 and NT - 1")[1]

        def t_e0(t, i, w):
            t.wait_ge(S("e0_acc"), freed(i, w, 4, GU0))
            t.wait_ge(S(f"e_g{w}"), gathered(i + 1, GT0))
            for k in range(GT0):
                u = w * GT0 + k
                t.wait_ge(S("e0_sel"), i * EU + (u + 1))
                t.matmul(psum[2 + w % 4][0:R, 0:D], s0[:, u, :], g0[:, u, :], start=(k == 0), stop=(k == GT0 - 1)
                         ).then_inc(S("e0_sum"), 1)

        def v_acc0(v, i, w, blk):
            v.drain()
            v.wait_ge(S("e0_sum"), done(i, w * GT0 + GT0 - 1, EU))
            a = turn(AGG[:, ds(blk, 1), :])
            v.tensor_tensor(a, a, psum[2 + w % 4][0:R, 0:D], ALU.add).then_inc(S("e0_acc"), 1)

        bnm = XN
        c = Carver(SCR)
        mean = c(D, rows=R)
        var = c(D, rows=R)
        rstd = c(D, rows=R)

        def t_bn(t, src_t, bank, wait, name):
            t.wait_ge(S(wait), 1)
            for j in range(NT):
                k = t.matmul(psum[bank][0:R, 0:D], ones[0:R, 0:R], src_t[:, j, :], start=(j == 0), stop=(j == NT - 1))
            k.then_inc(S(name), 1)

        def bc(v2):
            return v2[:, :].unsqueeze(1).broadcast_to([R, NT, D])

        def v_bn(v):
            v.drain().then_inc(S("bn_agg"), 1)
            v.wait_ge(S("bn_sum"), 1)
            v.tensor_scalar(mean[:, :], psum[0][0:R, 0:D], 1.0 / N, None, ALU.mult)
            v.drain()
            v.tensor_tensor(AGG[:, :, :], AGG[:, :, :], bc(mean), ALU.subtract).then_inc(S("bn_centred"), 1)
            v.wait_ge(S("bn_ssq"), 1)
            v.tensor_scalar(var[:, :], psum[1][0:R, 0:D], 1.0 / N, None, ALU.mult).then_inc(S("bn_var"), 1)
            v.wait_ge(S("bn_sd"), 1)
            v.reciprocal(rstd[:, :], rstd[:, :])
            v.drain()
            v.tensor_tensor(rstd[:, :], rstd[:, :], gammab[0:R, :], ALU.mult)
            v.drain()
            v.tensor_tensor(AGG[:, :, :], AGG[:, :, :], bc(rstd), ALU.mult)
            v.drain()
            v.tensor_tensor(AGG[:, :, :], AGG[:, :, :], bc(betab[0:R, :]), ALU.add).then_inc(S("bn_y"), 1)
            v.wait_ge(S("bn_tanh"), 1)
            v.tensor_tensor(X[:, :, :], X[:, :, :], bnm[:, :, :], ALU.add)

        def a_bn(a):
            a.wait_ge(S("bn_centred"), 1)
            a.activation(bnm[:, :, :], AGG[:, :, :], ACT.Square).then_inc(S("bn_sq"), 1)
            a.wait_ge(S("bn_var"), 1)
            a.activation(rstd[:, :], var[:, :], ACT.Sqrt, bias=eps_t[0:R, 0:1]).then_inc(S("bn_sd"), 1)
            a.wait_ge(S("bn_y"), 1)
            a.activation(bnm[:, :, :], AGG[:, :, :], ACT.Tanh).then_inc(S("bn_tanh"), 1)


        TC = EC // NT // 2
        ea = XN[:, 0:4, :].rearrange("p a b -> p (a b)").rearrange("p (s c e) -> p s c e", s=2, c=TC)

        def s_te(s):
            av = A["edge_attr_64"].rearrange("(p c) e -> p c e", p=R)
            with s.Fori(0, NT) as i:
                for u in range(2):
                    s.wait_ge(S("te_read"), freed(i, u, 2, 2))
                    s.dma_start(ea[:, u], av[:, ds((i * 2 + u) * TC, TC), :]).then_inc(S(f"te_in{u}"), 16)

        def v_te(v, i):
            for u in range(2):
                v.wait_ge(S(f"te_in{u}"), 16 * (i + 1))
                v.tensor_tensor(ea[:, u], ea[:, u], attb[0:R, 2 * D:2 * D + EDIM].unsqueeze(1)
                                .broadcast_to([R, TC, EDIM]), ALU.mult)
            v.drain()
            for u in range(2):
                v.tensor_reduce(rec[:, ds((i * 2 + u) * TC, TC), 2], ea[:, u], AX_X, ALU.add
                                ).then_inc(S("te_read"), 1)

        GATE = {"g0": 0, "g1": NT // U5}

        def t_gate(t, ph, gw, NX):
            if ph == "g0":
                seed(t, "g_lgp")
            with t.Fori(0, NT // U5) as i:
                for u in range(U5):
                    t_turn(t, BEFORE[ph], i, u)
                t.wait_ge(S("g_lg"), GATE[ph] + i + 1)
                for u in range(U5):
                    t.wait_ge(S("x_xT"), done(BEFORE[ph] + i, u))
                    for h in range(2):
                        k = t.matmul(psum[2][0:R, u * NX:(u + 1) * NX], xT[:, u, h, :], gw[:, h, :],
                                     start=(h == 0), stop=(h == 1))
                    k.then_inc(S("g_lgp"), 1)

        def a_gate(a, ph):
            with a.Fori(0, NT // U5) as i:
                a_sqrt(a, BEFORE[ph], i)
                for u in range(U5):
                    a_turned(a, BEFORE[ph], i, u, lambda: a.wait_ge(S("g_lgp"), freed(GATE[ph] + i, u, U5)))

        def v_gate(v, ph, gb, NX, keep):
            if ph == "g0":
                seed(v, "g_lg", n=1)
            with v.Fori(0, NT // U5) as i:
                def kept():
                    v.wait_ge(S("g_hout"), landed(GATE[ph] + i))
                    if keep:
                        v.wait_ge(S("g_keep"), i + 1)
                v_norm(v, BEFORE[ph], i, kept)
                v.wait_ge(S("g_lgp"), done(GATE[ph] + i, U5 - 1))
                v.tensor_tensor(LG[:, ds(i * U5, U5), 0:NX],
                                psum[2][0:R, 0:U5 * NX].rearrange("p (a b) -> p a b", a=U5),
                                gb[0:R, 0:NX].unsqueeze(1).broadcast_to([R, U5, NX]), ALU.add
                                ).then_inc(S("g_lg"), 1)

        def s_gate(s, ph, hrow):
            if ph == "g0":
                seed(s, "g_hout", n=16)
            with s.Fori(0, NT // U5) as i:
                s.wait_ge(S("x_xs"), (BEFORE[ph] + i) * U5 + U5)
                s.dma_start(tiles(hrow)[:, ds(i * U5, U5), :], xs[:, :, :]).then_inc(S("g_hout"), 16)
            s.wait_ge(S("g_hout"), landed(GATE[ph] + NT // U5))

        def p_keep(p, ph):
            seed(p, "g_keep", n=1)
            with p.Fori(0, NT // U5) as i:
                p.wait_ge(S("x_xs"), (BEFORE[ph] + i) * U5 + U5)
                p.sem_inc(S("holds_waits"), 1)
                p.tensor_copy(XN[:, ds(i * U5, U5), :], xs[:, :, :]).then_inc(S("g_keep"), 1)

        c = Carver(SCR)
        c.at = move_end
        mx = c(2, NT, rows=R)
        low = c(NT, rows=R)
        eqm = c(NT, X1, rows=R)
        eqx = c(NT, X1, rows=R)
        sm = c(NT, rows=R)

        def bx(v2, NX):
            return v2.unsqueeze(2).broadcast_to([R, NT, NX])

        def v_choose(v, ph, NX, K):
            v.wait_ge(S("g_hout"), landed(GATE[ph] + NT // U5))
            if K > 1:
                v.wait_ge(S("g_keep"), NT // U5 + 1)
            sc = LG[:, :, 0:NX]
            ids = iota[0:R, 0:NX].unsqueeze(1).broadcast_to([R, NT, NX])
            for k in range(K):
                v.tensor_reduce(mx[:, k, :], sc, AX_X, ALU.max)
                v.drain()
                v.tensor_tensor(eqm[:, :, 0:NX], sc, bx(mx[:, k, :], NX), ALU.is_equal)
                v.drain()
                v.scalar_tensor_tensor(eqm[:, :, 0:NX], eqm[:, :, 0:NX], -100.0, ids, ALU.mult, ALU.add)
                v.drain()
                v.tensor_reduce(low[:, :], eqm[:, :, 0:NX], AX_X, ALU.min)
                v.drain()
                b = blkF[:, k * NT:(k + 1) * NT]
                v.tensor_scalar(b, low[:, :], 100.0, None, ALU.add)
                v.tensor_copy(packed[:, k * NT:(k + 1) * NT], node[:, :])
                v.drain()
                if K == 1:
                    v.tensor_tensor(eqx[:, :, 0:NX], sc, bx(mx[:, 0, :], NX), ALU.subtract)
                elif k == 0:
                    v.tensor_tensor(eqm[:, :, 0:NX], ids, bx(b, NX), ALU.is_equal)
                    v.drain()
                    v.scalar_tensor_tensor(sc, eqm[:, :, 0:NX], -BIG, sc, ALU.mult, ALU.add)
                    v.drain()
            if K == 1:
                v.drain().then_inc(S("g_x"), 1)
                v.wait_ge(S("g_ex"), K)
                v.tensor_reduce(sm[:, :], eqx[:, :, 0:NX], AX_X, ALU.add)
                v.drain()
                v.reciprocal(gwt[:, 0, :], sm[:, :])
            else:
                v.tensor_tensor(sm[:, :], mx[:, 1, :], mx[:, 0, :], ALU.subtract).then_inc(S("g_x"), 1)
                v.wait_ge(S("g_ex"), K)
                v.tensor_scalar(low[:, :], sm[:, :], 1.0, None, ALU.add)
                v.drain()
                v.reciprocal(gwt[:, 0, :], low[:, :])
                v.drain()
                v.tensor_tensor(gwt[:, 1, :], gwt[:, 0, :], sm[:, :], ALU.mult)
            v.drain()

        def a_choose(a, ph, NX, K):
            a.wait_ge(S("g_x"), K)
            z = eqx[:, :, 0:NX] if K == 1 else sm[:, :]
            a.activation(z, z, ACT.Exp).then_inc(S("g_ex"), 1)

        def v_route(v, ph, K, NX, M):
            C = NT * K
            GX = GX0 if K == 1 else GX1
            v_sort_start(v)
            with v.Fori(0, NX // 2) as b:
                v_count(v, C, b * 2, b * 2 + 1)
            v_totals(v, ph, NX, GX, fixed=(K == 1))
            with v.Fori(0, NX // 2) as b:
                v_place(v, C, NG0 if K == 1 else NG1, b * 2, b * 2 + 1, bases=(K == 1))
            if K == 1:
                v.tensor_tensor(low[:, :], pos[:, 0:C], bsum[:, 0:C], ALU.subtract)
                v.drain()
                v.tensor_scalar(sm[:, :], low[:, :], float(CAP), None, ALU.is_lt)
                v.scalar_tensor_tensor(slotI[:, 0:C], low[:, :], float(CAP - 1), bsum[:, 0:C], ALU.min, ALU.add)
                v.drain()
                v.tensor_tensor(gwt[:, 0, :], gwt[:, 0, :], sm[:, :], ALU.mult)
                v.tensor_scalar(low[:, :], low[:, :], float(CAP), 128.0 * M, ALU.is_ge, ALU.mult)
                v.drain()
                v.tensor_tensor(pos[:, 0:C], pos[:, 0:C], low[:, :], ALU.add)
                v.drain()
            else:
                v.tensor_copy(slotI[:, 0:C], pos[:, 0:C])
            v_placed(v, C, NX, NG0 if K == 1 else NG1, gblkX)
            v.tensor_copy(tF[:, 0:C], tI[:, 0:C])
            v.tensor_copy(qF[:, 0:C], posI[:, 0:C])
            v.drain()
            with v.Fori(0, C // U5) as i:
                for u in range(U5):
                    v_onehot(v, ph, i, u, M, U5)
            v.wait_ge(S("s_moved"), K)
            v.tensor_copy(idxX[:, 0:M], psum[6][:, 0:M])
            v.drain()

        def t_route(t, ph, K, NX, M):
            t_count(t, ph, NX)
            t_bounds(t, M, True, (6,))
            with t.Fori(0, NT * K // U5) as i:
                for u in range(U5):
                    t_move(t, ph, i, u, M, U5)
            t_bounds(t, M, False, (6,)).then_inc(S("s_moved"), 1)

        c = Carver(SCR)
        ew1 = c(2, 2 * F0)
        ew2 = c(2, 2 * F0)
        ht = c(F0 // 128, 128 * GX0)
        eb1 = c(2, F0 // 128)
        gx = c(2, GX0, dt=I32)
        cx = c = Carver(xnT.rearrange("p h n -> p (h n)"))
        xg = c(2, GX0, D)
        xgT = c(2, 2, 128 * GX0)
        yo = c(4, D)
        eb2 = c(2, D)

        class Experts:
            def __init__(self, GX, F, groups, before=None):
                self.GX, self.F, self.FC, self.turns = GX, F, F // 128, groups // 2
                self.tiles = before.tiles + 2 * before.GX * before.turns if before else 0
                self.chunks = before.chunks + 2 * before.FC * before.turns if before else 0
                self.past = before.past + before.turns if before else 0
                self.outs = before.outs + before.GX * before.turns // 2 if before else 0

            def tile(self, i, u, k):
                return i * (2 * self.GX) + (u * self.GX + k + 9 + self.tiles)

            def chunk(self, i, u, f):
                return i * (2 * self.FC) + (u * self.FC + f + 17 + self.chunks)

            def out(self, i, u, k):
                return i * (self.GX // 2) + ((u * self.GX + k) // 4 + self.outs)

        m0 = Experts(GX0, F0, NG0)
        m1 = Experts(GX1, F1, NG1, m0)

        def s_expert(s, m, w1d, b1d, w2d, b2d):
            F, FC = m.F, m.FC
            with s.Fori(0, m.turns) as i:
                for u in range(2):
                    e = i * 2 + u if m is m0 else s.value_load(gblkX[0:1, ds(i * 2 + u, 1)], min_val=0, max_val=X1 - 1)
                    s.wait_ge(S("m_yp"), m.tile(i, u - 2, m.GX - 1))
                    s.wait_ge(S("m_y"), m.tile(i, u - 2, m.GX - 1))
                    s.dma_start(ew1[:, u, 0:2 * F].rearrange("p (h f) -> p h f", h=2),
                                w1d[ds(e, 1), :, :].rearrange("a (h p) f -> p (a h) f", p=128)
                                ).then_inc(S(f"m_w{u}"), 16)
                    s.dma_start(ew2[:, u, 0:2 * F], w2d[ds(e, 1), :, :].rearrange("a (p c) d -> p (a c d)", p=128)
                                ).then_inc(S(f"m_w{u}"), 16)
                    s.dma_start(eb1[:, u, 0:FC], b1d[ds(e, 1), :].rearrange("a (p c) -> p (a c)", p=128)
                                ).then_inc(S(f"m_w{u}"), 16)
                    s.dma_start(eb2[:, u, :], b2d[ds(e, 1), :].broadcast_to([128, D])).then_inc(S(f"m_w{u}"), 16)

        def p_expert(p, m, hrow, also=None):
            GX = m.GX
            with p.Fori(0, m.turns) as i:
                for u in range(2):
                    p.wait_ge(S("m_tp"), m.tile(i, u - 2, GX - 1))
                    p.sem_inc(S("holds_waits"), 1)
                    p.tensor_copy(gx[:, u, 0:GX], idxX[:, ds(i * (2 * GX) + u * GX, GX)])
                    p.drain()
                    for k in range(GX):
                        p.indirect_dma_start(xg[:, u, k, :], None, hrow,
                                             bass.IndirectOffsetOnAxis(ap=gx[:, u, k:k + 1], axis=0)
                                             ).then_inc(S(f"m_g{u}"), 16)
                if also is not None:
                    also(i)

        def t_expert(t, m):
            GX, F, FC = m.GX, m.F, m.FC
            if m is m0:
                t.sem_inc(S("m_yp"), 8)
                t.sem_inc(S("m_tp"), 8)
                t.sem_inc(S("m_hp"), 16)
            with t.Fori(0, m.turns) as i:
                def rows_turned(u):
                    t.wait_ge(S(f"m_g{u}"), gathered(i + 1, GX) + gathered(m.past, GX0))
                    for k in range(GX):
                        t.wait_ge(S("m_xT"), m.tile(i, u, k - 2))
                        for h in range(2):
                            j = t.transpose(psum[k % 2][:, h * 128:(h + 1) * 128], xg[:, u, k, h * 128:(h + 1) * 128],
                                            ident[:, :])
                        j.then_inc(S("m_tp"), 1)

                def hidden(u):
                    w = ew1[:, u, 0:2 * F].rearrange("p (h q c) -> p h q c", h=2, c=FC)
                    t.wait_ge(S(f"m_w{u}"), 64 * (m.past + i + 1))
                    t.wait_ge(S("m_xT"), m.tile(i, u, GX - 1))
                    for f in range(FC):
                        t.wait_ge(S("m_h"), m.chunk(i, u, f - 2))
                        for h in range(2):
                            j = t.matmul(psum[2 + f % 2][:, 0:128 * GX], w[:, h, :, f], xgT[:, u, h, 0:128 * GX],
                                         start=(h == 0), stop=(h == 1))
                        j.then_inc(S("m_hp"), 1)

                def outputs(u):
                    t.wait_ge(S("m_h"), m.chunk(i, u, FC - 1))
                    for k in range(GX):
                        o = psum[4 + (u * GX + k) % 4][:, 0:D]
                        t.wait_ge(S("m_y"), m.tile(i, u, k - 4))
                        for f in range(FC):
                            j = t.matmul(o, ht[:, f, k * 128:(k + 1) * 128], ew2[:, u, f * D:(f + 1) * D],
                                         start=(f == 0), stop=(f == FC - 1))
                        j.then_inc(S("m_yp"), 1)

                rows_turned(0)
                hidden(0)
                rows_turned(1)
                outputs(0)
                hidden(1)
                outputs(1)

        def a_expert(a, m, ys):
            GX, FC = m.GX, m.FC
            if m is m0:
                a.sem_inc(S("m_xT"), 8)
                a.sem_inc(S("m_h"), 16)
                seed(a, *(f"m_out{k}" for k in range(4)), n=16)
            with a.Fori(0, m.turns) as i:
                def turned(u):
                    a.wait_ge(S("m_hp"), m.chunk(i, u - 2, FC - 1))
                    for k in range(GX):
                        a.wait_ge(S("m_tp"), m.tile(i, u, k))
                        a.wait_ge(consts, 1)
                        a.copy(xgT[:, u, :, k * 128:(k + 1) * 128],
                               psum[k % 2][:, 0:256].rearrange("p (h r) -> p h r", h=2)).then_inc(S("m_xT"), 1)

                def hidden(u):
                    a.wait_ge(S("m_yp"), m.tile(i, u - 1, GX - 1))
                    for f in range(FC):
                        a.wait_ge(S("m_hp"), m.chunk(i, u, f))
                        a.activation(ht[:, f, 0:128 * GX], psum[2 + f % 2][:, 0:128 * GX], ACT.Relu,
                                     bias=eb1[:, u, f:f + 1]).then_inc(S("m_h"), 1)

                def sent(u):
                    for k in range(GX):
                        b = (u * GX + k) % 4
                        a.wait_ge(S("m_y"), m.tile(i, u, k))
                        a.dma_start(ys[ds((i * (2 * GX) + (u * GX + k)) * 128, 128), :], yo[:, b, :]
                                    ).then_inc(S(f"m_out{b}"), 16)

                turned(0)
                hidden(0)
                turned(1)
                sent(0)
                hidden(1)
                sent(1)
            for b in range(4):
                a.wait_ge(S(f"m_out{b}"), landed(m.outs + GX * m.turns // 2))

        def v_expert(v, m):
            GX = m.GX
            if m is m0:
                v.sem_inc(S("m_y"), 8)
            with v.Fori(0, m.turns) as i:
                for u in range(2):
                    for k in range(GX):
                        b = (u * GX + k) % 4
                        v.wait_ge(S("m_yp"), m.tile(i, u, k))
                        v.wait_ge(S(f"m_out{b}"), landed(m.out(i, u, k)))
                        v.tensor_tensor(yo[:, b, :], psum[4 + b][:, 0:D], eb2[:, u, :], ALU.add).then_inc(S("m_y"), 1)

        c = Carver(SCR)
        c.at = norm_end
        yg = c(2 * K1 * U5, D, rows=R)
        fin = c(U5, D, rows=R, dt=I32)
        nan = c(U5, D, rows=R, dt=I32)
        out2 = fin.bitcast(F32)

        def back_slot(i, k, u):
            return (i % 2) * K1 * U5 + k * U5 + u

        def back_in(i, K):
            before = 0 if K == K0 else len(range(i % 2, NT // U5, 2)) * K0
            return 16 * U5 * (before + K * (i // 2 + 1))

        def p_back(p, ph, K, ys):
            for i in range(NT // U5):
                if i >= 2:
                    p.wait_ge(S(ph + "_took"), i - 1)
                for k in range(K):
                    for u in range(U5):
                        at = k * NT + i * U5 + u
                        p.indirect_dma_start(yg[:, back_slot(i, k, u), :], None, ys,
                                             bass.IndirectOffsetOnAxis(ap=slotI[:, at:at + 1], axis=0)
                                             ).then_inc(S(f"b{i % 2}"), 16)

        def v_back0(v):
            for i in range(NT // U5):
                v.wait_ge(S(f"b{i % 2}"), back_in(i, K0))
                for u in range(U5):
                    y = yg[:, back_slot(i, 0, u), :]
                    v.tensor_scalar(y, y, gwt[:, 0, i * U5 + u:i * U5 + u + 1], None, ALU.mult)
                v.drain()
                first = back_slot(i, 0, 0)
                y5, y5b = yg[:, first:first + U5, :], yg[:, first + U5:first + 2 * U5, :]
                v.tensor_scalar(fin[:, :, :], y5, 0.0, 0.0, ALU.mult, ALU.is_equal)
                v.tensor_tensor(nan[:, :, :], y5, y5, ALU.not_equal)
                v.tensor_scalar(y5b, y5, 1e4, -1e4, ALU.min, ALU.max)
                v.drain()
                v.copy_predicated(y5b, fin[:, :, :], y5)
                v.drain()
                v.copy_predicated(y5b, nan[:, :, :], zero3)
                v.drain()
                x5 = X[:, i * U5:(i + 1) * U5, :]
                v.tensor_tensor(x5, x5, y5b, ALU.add).then_inc(S("m0_took"), 1)

        zero3 = zeros[0:R, 0:D].unsqueeze(1).broadcast_to([R, U5, D])

        def v_back1(v):
            for i in range(NT // U5):
                v.wait_ge(S(f"b{i % 2}"), back_in(i, K1))
                for k in range(2):
                    for u in range(U5):
                        n = i * U5 + u
                        v.scalar_tensor_tensor(XN[:, n, :], yg[:, back_slot(i, k, u), :], gwt[:, k, n:n + 1],
                                               XN[:, n, :], ALU.mult, ALU.add)
                    v.drain()
                v.drain().then_inc(S("m1_took"), 1)
                for u in range(U5):
                    v.bn_stats(st6[:, u, :], XN[:, i * U5 + u, :])
                v.drain()
                for u in range(U5):
                    k = v.bn_aggr(mv[:, u, :], st6[:, u, :])
                k.then_inc(S("x_var"), 1)
                v.wait_ge(S("x_sd"), BEFORE["fin"] + i + 1)
                v.reciprocal(rs[:, :], sd[:, :])
                v.drain()
                if i >= 2:
                    v.wait_ge(S(f"fin_out{i % 2}"), 16 * (i // 2))
                o = (xs, out2)[i % 2]
                for u in range(U5):
                    v.tensor_scalar(o[:, u, :], XN[:, i * U5 + u, :], mv[:, u, 0:1], rs[:, u:u + 1],
                                    ALU.subtract, ALU.mult)
                v.drain()
                v.tensor_tensor(o[:, :, :], o[:, :, :], gamma1b[0:R, :].unsqueeze(1).broadcast_to([R, U5, D]), ALU.mult)
                v.drain()
                v.tensor_tensor(o[:, :, :], o[:, :, :], beta1b[0:R, :].unsqueeze(1).broadcast_to([R, U5, D]), ALU.add)
                v.drain()
                v.tensor_tensor(o[:, :, :], o[:, :, :], X[:, i * U5:(i + 1) * U5, :], ALU.add).then_inc(S("fin_y"), 1)

        def s_final(s):
            for i in range(NT // U5):
                s.wait_ge(S("fin_y"), i + 1)
                s.dma_start(tiles(out)[:, i * U5:(i + 1) * U5, :], (xs, out2)[i % 2][:, :, :]
                            ).then_inc(S(f"fin_out{i % 2}"), 16)
            for b in range(2):
                s.wait_ge(S(f"fin_out{b}"), 16 * len(range(b, NT // U5, 2)))

        c = cx
        wtmp = c(2, D)
        wmean = c(2, 16)

        def v_w1(v):
            for n in range(2):
                v.tensor_tensor(wtmp[:, :, :], wfx[:, :, 0:D],
                                attb[:, n * D:(n + 1) * D].unsqueeze(1).broadcast_to([128, 2, D]), ALU.mult)
                v.drain()
                v.tensor_reduce(wfx[:, :, D + n:D + n + 1], wtmp[:, :, :], AX_X, ALU.add)
                v.drain()
            for h in range(2):
                g = wkv1[:, h, :].rearrange("p (g e) -> p g e", e=64)
                v.tensor_reduce(wmean[:, h, :], g, AX_X, ALU.add)
                v.drain()
                v.tensor_scalar(wmean[:, h, :], wmean[:, h, :], 1.0 / 64, None, ALU.mult)
                v.drain()
                v.tensor_tensor(g, g, wmean[:, h, :].unsqueeze(2).broadcast_to([128, 16, 64]), ALU.subtract)
            v.memset(den[:, :], 0.0)
            v.memset(AGG[:, :, :], 0.0)

        c = Carver(SCR)
        c.at = norm_end
        zrow = c(U5, ROW1, rows=R)
        sq = c(2, 2 * HID, rows=R)
        K1t = c(2, HID, rows=R)
        V1t = c(2, HID, rows=R)
        ss = c(2, 16, rows=R)
        rr = c(2, 8, rows=R)
        dts = c(4, 128)
        Bm = c(4, D)

        def t_a1(t):
            seed(t, "a1_z", "a1_kp", "a1_vp", "a1_sum")
            t_bounds(t, 512, True, (5,))
            with t.Fori(0, NT // U5) as i:
                for u in range(U5):
                    t_turn(t, BEFORE["a1"], i, u)

                def sums(u):
                    t.wait_ge(S("a1_V"), done(i, u))
                    for q in range(4):
                        k = t.matmul(psum[5][:, q * 128:(q + 1) * 128], V1t[:, u % 2, q * 128:(q + 1) * 128],
                                     K1t[:, u % 2, q * 128:(q + 1) * 128], start=False, stop=False,
                                     skip_group_check=True)
                    k.then_inc(S("a1_sum"), 1)

                for u in range(U5):
                    t.wait_ge(S("x_xT"), done(BEFORE["a1"] + i, u))
                    t.wait_ge(S("a1_zr"), freed(i, u, 2))
                    for h in range(2):
                        k = t.matmul(psum[2 + 4 * (u % 2)][0:R, 0:ROW1], xT[:, u, h, :], wfx[:, h, :],
                                     start=(h == 0), stop=(h == 1))
                    k.then_inc(S("a1_z"), 1)
                    t.wait_ge(S("a1_kc"), freed(i, u, 2))
                    for h in range(2):
                        k = t.matmul(psum[3 + 4 * (u % 2)][0:R, :], xT[:, u, h, :], wkv1[:, h, 0:HID],
                                     start=(h == 0), stop=(h == 1))
                    k.then_inc(S("a1_kp"), 1)
                    t.wait_ge(S("a1_vc"), freed(i, u, 1))
                    for h in range(2):
                        k = t.matmul(psum[4][0:R, :], xT[:, u, h, :], wkv1[:, h, HID:2 * HID],
                                     start=(h == 0), stop=(h == 1))
                    k.then_inc(S("a1_vp"), 1)
                    if u:
                        sums(u - 1)
                sums(U5 - 1)
            t_bounds(t, 512, False, (5,)).then_inc(S("a1_all"), 1)
            t.wait_ge(S("a1_dts"), 1)
            for q in range(4):
                k = t.matmul(psum[6 + q // 2][:, (q % 2) * 256:(q % 2) * 256 + 256], dts[:, q, :], wout[:, q, :],
                             start=True, stop=True)
            k.then_inc(S("a1_B"), 1)
            t.wait_ge(S("a1_Bm"), 1)
            for h in range(2):
                for q in range(4):
                    k = t.matmul(psum[2][:, h * 256:(h + 1) * 256], wqo[:, q, h * 128:(h + 1) * 128], Bm[:, q, :],
                                 start=(q == 0), stop=(q == 3))
            k.then_inc(S("a1_M"), 1)

        def a_a1(a):
            seed(a, "a1_zr", "a1_kc", "a1_vc")
            with a.Fori(0, NT // U5) as i:
                a_sqrt(a, BEFORE["a1"], i)
                for u in range(U5):
                    def users():
                        a.wait_ge(S("a1_vp"), freed(i, u, U5))
                        a.wait_ge(S("a1_xkeep"), freed(i, u, U5))
                    a_turned(a, BEFORE["a1"], i, u, users)
                for u in range(U5):
                    a.wait_ge(S("a1_z"), done(i, u))
                    a.wait_ge(S(f"a_out{u}"), landed(NT // U5 + i))
                    a.wait_ge(S("a1_dcol"), i + 1)
                    a.copy(zrow[:, u, :], psum[2 + 4 * (u % 2)][0:R, 0:ROW1]).then_inc(S("a1_zr"), 1)
                    a.wait_ge(S("a1_kp"), done(i, u))
                    a.wait_ge(S("a1_ss"), freed(i, u, 2))
                    a.activation(sq[:, u % 2, 0:HID], psum[3 + 4 * (u % 2)][0:R, :], ACT.Square)
                    a.wait_ge(S("a1_sum"), freed(i, u, 2))
                    a.copy(K1t[:, u % 2, :], psum[3 + 4 * (u % 2)][0:R, :]).then_inc(S("a1_kc"), 1)
                    a.wait_ge(S("a1_vp"), done(i, u))
                    a.activation(sq[:, u % 2, HID:2 * HID], psum[4][0:R, :], ACT.Square)
                    a.copy(V1t[:, u % 2, :], psum[4][0:R, :]).then_inc(S("a1_vc"), 1)
                    a.wait_ge(S("a1_ss"), done(i, u))
                    a.activation(ss[:, u % 2, :], ss[:, u % 2, :], ACT.Sqrt, bias=eps_t[0:R, 0:1], scale=1.0 / 64
                                 ).then_inc(S("a1_sq"), 1)

        def v_a1(v):
            seed(v, "a1_ss", "a1_V")
            seed(v, "a1_dcol", n=1)
            with v.Fori(0, NT // U5) as i:
                def kept():
                    v.wait_ge(S("a1_keep"), i + 1)
                v_norm(v, BEFORE["a1"], i, kept)
                for u in range(U5):
                    v.drain()
                    v.wait_ge(S("a1_vc"), done(i, u))
                    v.tensor_reduce(ss[:, u % 2, :], sq[:, u % 2, :].rearrange("p (g e) -> p g e", e=64),
                                    AX_X, ALU.add).then_inc(S("a1_ss"), 1)
                    v.wait_ge(S("a1_sq"), i * U5 + (u + 1))
                    v.reciprocal(ss[:, u % 2, :], ss[:, u % 2, :])
                    v.drain()
                    v.tensor_tensor(rr[:, u % 2, :], ss[:, u % 2, 0:8], ss[:, u % 2, 8:16], ALU.mult)
                    v.drain()
                    v1 = V1t[:, u % 2, :].rearrange("p (g e) -> p g e", e=64)
                    v.tensor_tensor(v1, v1, rr[:, u % 2, :].unsqueeze(2).broadcast_to([R, 8, 64]), ALU.mult
                                    ).then_inc(S("a1_V"), 1)
                v.wait_ge(S("a1_zr"), done(i, U5 - 1))
                v.tensor_scalar(dm[:, ds(i * U5, U5), 0], zrow[:, :, D + 1], 1.0, None, ALU.mult
                                ).then_inc(S("a1_dcol"), 1)
            v.drain()
            v.tensor_scalar(dm[:, :, 1], dm[:, :, 0], 0.01, None, ALU.mult)
            v.memset(dm[:, :, 2], LOWEST)
            v.wait_ge(S("a1_all"), 1)
            for q in range(4):
                k = v.scalar_tensor_tensor(dts[:, q, :], psum[5][:, q * 128:(q + 1) * 128], 1.0 / N, hm64[:, :],
                                           ALU.mult, ALU.mult)
            k.then_inc(S("a1_dts"), 1)
            v.wait_ge(S("a1_B"), 1)
            v.tensor_copy(Bm[:, 0:2, :], psum[6][:, :].rearrange("p (a b) -> p a b", a=2))
            v.tensor_copy(Bm[:, 2:4, :], psum[7][:, :].rearrange("p (a b) -> p a b", a=2)).then_inc(S("a1_Bm"), 1)
            v.wait_ge(S("a1_M"), 1)
            v.tensor_copy(wsm[:, :, D:2 * D], psum[2][:, :].rearrange("p (a b) -> p a b", a=2))

        def s_a1(s):
            with s.Fori(0, NT // U5) as i:
                for u in range(U5):
                    s.wait_ge(S("a1_zr"), done(i, u))
                    s.dma_start(tiles(tab1)[:, ds(i * U5 + u, 1), :].rearrange("p a d -> p (a d)"), zrow[:, u, :]
                                ).then_inc(S(f"a_out{u}"), 16)
            for u in range(U5):
                s.wait_ge(S(f"a_out{u}"), landed(2 * (NT // U5)))

        def p_a1(p):
            seed(p, "a1_xkeep")
            seed(p, "a1_keep", n=1)
            with p.Fori(0, NT // U5) as i:
                p.wait_ge(S("x_xs"), (BEFORE["a1"] + i) * U5 + U5)
                p.sem_inc(S("holds_waits"), 1)
                p.tensor_copy(XN[:, ds(i * U5, U5), :], xs[:, :, :]).then_inc(S("a1_keep"), 1)
                for h in range(2):
                    p_scatter(p, h, SC + SCB + SCM + i, (SCB + SCM + i) * 2 + h, slot1)
                for u in range(U5):
                    p.wait_ge(S("x_xT"), done(BEFORE["a1"] + i, u))
                    p.wait_ge(consts, 1)
                    p.tensor_copy(xnT[:, :, ds((i * U5 + u) * R, R)], xT[:, u, :, :]).then_inc(S("a1_xkeep"), 1)

        GU = EU1 // GT1
        assert GU == EU // GT0
        GS = GT1 * 128
        c = Carver(SCR)
        gs = c(GU, GT1)
        ohg = c(4, GT1, R)
        unb = c(4, GT1 * (R + 1) // 2, dt=BF16)
        gmx = c(GU, rows=R)
        t1 = c(GU, 2, rows=R)
        mnew = c(GU, rows=R)
        bs = c(GU, 4, rows=R)
        rsc = c(GU, rows=R)
        nkey = c(T1)
        g1 = c(EU1, ROW1)
        c = Carver(WD)
        c.at = 2 * ROW1 + 4 * D
        E1 = c(2, GS, rows=R)
        E2 = c(2, GS, rows=R)
        Pm = c(2, GS, rows=R)
        Ps = c(2, GT1, R)

        def scores(w):
            return psum[(0, 1, 6, 7)[w % 4]][0:R, :]

        def v1_scores(v, i, w):
            v.wait_ge(S(f"e_g{w}"), gathered(i + 1, GT1) + gathered(T0 // EU, GT0))
            v.tensor_tensor(gs[:, w, :], g1[:, GT1 * w:GT1 * (w + 1), D],
                            slots_[:, ds((i * GU + w) * GT1, GT1), 2], ALU.add)

        def v1_onehot(v, i, w):
            v.wait_ge(S("e1_dt"), freed(i, w, 4, GU))
            for k in range(GT1):
                j = v.tensor_scalar(ohg[:, w % 4, k, :], iota[:, 1:R + 1], slots_[:, ds((i * GU + w) * GT1 + k, 1), 0],
                                    gs[:, w, k:k + 1], ALU.is_equal, ALU.mult)
            j.then_inc(S("e1_sel"), 1)

        def v1_settled(v, i, w):
            v.drain()

        def a1_far(a, i, w):
            a.wait_ge(S("e1_dt"), freed(i, w, 4, GU))
            a.wait_ge(consts, 1)
            for k in range(GT1):
                j = a.activation(unb[:, w % 4, k * (R + 1):k * (R + 1) + R], iota[:, 1:R + 1], ACT.Abs,
                                 bias=nkey[:, ds((i * GU + w) * GT1 + k, 1)], scale=BIG)
            j.then_inc(S("e1_far"), 1)

        def t1_mask(t, i, w):
            t.wait_ge(S("e1_sel"), i * GU + (w + 1))
            t.wait_ge(S("e1_far"), i * GU + (w + 1))
            t.wait_ge(S("e1_exp"), freed(i, w, 4, GU))
            for k in range(GT1):
                o = scores(w)[:, k * 128:(k + 1) * 128]
                t.matmul(o, ohg[:, w % 4, k, :], ident[:, :], start=True, stop=False)
                j = t.matmul(o, unb[:, w % 4, k * (R + 1):k * (R + 1) + R], nident[:, :], start=False, stop=True)
            j.then_inc(S("e1_dt"), 1)

        FIRST1, LAST1 = 0, G1 // GU - 1
        late = []
        blocks = []

        def dmax(w):
            return turn(dm[:, ds(blocks[w], 1), :])

        def v1_max(v, i, w):
            if w == 0:
                if i is not FIRST1:
                    late[:] = load_blocks(gblk1, i * GU - 3, 3)
                blocks[:] = load_blocks(gblk1, i * GU, GU)
            v.wait_ge(S("e1_dt"), done(i, w, GU))
            v.tensor_reduce(gmx[:, w:w + 1], scores(w)[:, :], AX_X, ALU.max)

        def v1_leaky(v, i, w):
            d_, m_ = dmax(w)[:, 0:1], dmax(w)[:, 2:3]
            v.tensor_scalar(t1[:, w, 0:1], gmx[:, w:w + 1], d_, m_, ALU.add, ALU.max)
            v.tensor_scalar(t1[:, w, 1:2], gmx[:, w:w + 1], d_, 0.01, ALU.add, ALU.mult)

        def v1_new(v, i, w):
            v.tensor_tensor(mnew[:, w:w + 1], t1[:, w, 0:1], t1[:, w, 1:2], ALU.max)

        def v1_shift(v, i, w):
            v.tensor_scalar(bs[:, w, 0:3], dmax(w), mnew[:, w:w + 1], None, ALU.subtract).then_inc(S("e1_max"), 1)

        def v1_keep(v, i, w):
            v.tensor_scalar(dmax(w)[:, 2:3], mnew[:, w:w + 1], 1.0, None, ALU.mult)

        def a1_exp(a, i, w):
            a.wait_ge(S("e1_max"), i * GU + (w + 1))
            a.wait_ge(S("e1_p"), freed(i, w, 2, GU))
            a.activation(E1[:, w % 2, :], scores(w)[:, :], ACT.Exp, bias=bs[:, w, 0:1])
            a.activation(E2[:, w % 2, :], scores(w)[:, :], ACT.Exp, bias=bs[:, w, 1:2], scale=0.01)
            a.activation(rsc[:, w:w + 1], bs[:, w, 2:3], ACT.Exp).then_inc(S("e1_exp"), 1)

        def v1_prob(v, i, w):
            v.wait_ge(S("e1_exp"), done(i, w, GU))
            v.wait_ge(S("e1_pt"), freed(i, w, 2, GU))
            v.scalar_tensor_tensor(Pm[:, w % 2, :], E1[:, w % 2, :], 1.0, E2[:, w % 2, :], ALU.mult, ALU.max,
                                   accum_out=bs[:, w, 3:4]).then_inc(S("e1_p"), 1)

        def t1_turn(t, i, w):
            t.wait_ge(S("e1_p"), done(i, w, GU))
            t.wait_ge(S("e1_ps"), freed(i, w, 2, GU))
            for k in range(GT1):
                j = t.transpose(psum[2 + w % 2][:, k * 128:k * 128 + R], Pm[:, w % 2, k * 128:(k + 1) * 128],
                                ident[0:R, 0:R])
            j.then_inc(S("e1_pt"), 1)

        def a1_turned(a, i, w):
            a.wait_ge(S("e1_pt"), done(i, w, GU))
            a.wait_ge(S("e1_sum"), freed(i, w, 2, GU) * GT1)
            a.copy(Ps[:, w % 2, :, :], psum[2 + w % 2][:, :].rearrange("p (k r) -> p k r", k=GT1)[:, :, 0:R]
                   ).then_inc(S("e1_ps"), 1)

        def a1_rows(a, i, w):
            if i is not LAST1:
                a_rows(a, "e1", i + 1, w)

        def t1_sum(t, i, w):
            t.wait_ge(S("e1_ps"), done(i, w, GU))
            t.wait_ge(S("e1_acc"), freed(i, w, 2, GU))
            for k in range(GT1):
                t.matmul(psum[4 + w % 2][0:R, 0:D], Ps[:, w % 2, k, :], g1[:, GT1 * w + k, 0:D],
                         start=(k == 0), stop=(k == GT1 - 1)).then_inc(S("e1_sum"), 1)

        def v1_acc(v, i, w):
            blk = blocks[w] if w < GU - 3 or i is LAST1 else late[w - (GU - 3)]
            a, n_ = turn(AGG[:, ds(blk, 1), :]), den[:, ds(blk, 1)]
            v.wait_ge(S("e1_sum"), done(i, w, GU) * GT1)
            v.scalar_tensor_tensor(a, a, rsc[:, w:w + 1], psum[4 + w % 2][0:R, 0:D], ALU.mult, ALU.add
                                   ).then_inc(S("e1_acc"), 1)
            v.scalar_tensor_tensor(n_, n_, rsc[:, w:w + 1], bs[:, w, 3:4], ALU.mult, ALU.add)

        EVERY = -100

        def skewed(eng, *stages):
            first, last = min(l for l, _ in stages if l > EVERY), max(l for l, _ in stages)
            for k in range(first, GU):
                for lag, stage in stages:
                    if lag == EVERY:
                        stage(eng, 0, 0)
                    elif k >= lag:
                        stage(eng, 0 if k - lag < GU else 1, (k - lag) % GU)
            with eng.Fori(1, G1 // GU - 1) as i:
                for k in range(GU):
                    for lag, stage in stages:
                        if lag == EVERY:
                            stage(eng, 0, 0)
                        else:
                            stage(eng, i + (k - lag) // GU, (k - lag) % GU)
            for k in range(G1 - GU, G1 + last):
                for lag, stage in stages:
                    if lag == EVERY:
                        stage(eng, 0, 0)
                    elif k - lag < G1:
                        stage(eng, LAST1 if k - lag >= G1 - GU else LAST1 - 1, (k - lag) % GU)

        def v_e1(v):
            seed(v, "e1_p", "e1_acc", n=GU)
            v.tensor_scalar(nkey[:, :], slots_[:, :, 0], -BIG, None, ALU.mult)
            v.drain().then_inc(S("e1_nkey"), 1)
            settled = (EVERY, v1_settled)
            skewed(v, (-2, v1_scores), (0, v1_max), settled, (0, v1_leaky), (-2, v1_onehot), settled,
                   (0, v1_new), (1, v1_prob), settled, (0, v1_shift), (3, v1_acc), settled, (0, v1_keep))

        def a_e1(a):
            seed(a, "e1_exp", "e1_ps", n=GU)
            for w in range(GU):
                a_rows(a, "e1", 0, w)
            a.wait_ge(S("e1_nkey"), 1)
            skewed(a, (-2, a1_far), (0, a1_exp), (1, a1_turned), (2, a1_rows))

        def t_e1(t):
            seed(t, "e1_dt", "e1_pt", n=GU)
            t.sem_inc(S("e1_sum"), GT1 * GU)
            skewed(t, (-1, t1_mask), (2, t1_sum), (1, t1_turn))

        c = Carver(SCR)
        c(U5, D)
        xT1 = c(U5, 2, R)
        hn = c(U5, D, rows=R)
        rden = c(NT, rows=R)
        hasn = c(NT, rows=R)

        def p_c1(p):
            seed(p, "c1_x")
            with p.Fori(0, NT // U5) as i:
                for u in range(U5):
                    p.wait_ge(S("c1_p"), freed(i, u, U5))
                    p.sem_inc(S("holds_waits"), 1)
                    p.tensor_copy(xT1[:, u, :, :], xnT[:, :, ds((i * U5 + u) * R, R)]).then_inc(S("c1_x"), 1)

        def t_c1(t):
            seed(t, "c1_p")
            with t.Fori(0, NT // U5) as i:
                for u in range(U5):
                    t.wait_ge(S("c1_x"), done(i, u))
                    t.wait_ge(S("c1_d"), freed(i, u, U5))
                    for h in range(2):
                        k = t.matmul(psum[2 + u][0:R, :], xT1[:, u, h, :], wsm[:, h, :],
                                     start=(h == 0), stop=(h == 1))
                    k.then_inc(S("c1_p"), 1)

        def v_c1(v):
            seed(v, "c1_d")
            v.tensor_scalar(has[:, :], den[:, :], 0.0, None, ALU.is_gt)
            v.tensor_scalar(rden[:, :], den[:, :], 1e-30, None, ALU.max)
            v.drain()
            v.reciprocal(rden[:, :], rden[:, :])
            v.tensor_scalar(hasn[:, :], has[:, :], -1.0, 1.0, ALU.mult, ALU.add)
            v.drain()
            with v.Fori(0, NT // U5) as i:
                tiles5 = ds(i * U5, U5)
                x5, xn5, agg5 = X[:, tiles5, :], XN[:, tiles5, :], AGG[:, tiles5, :]
                for u in range(U5):
                    n = ds(i * U5 + u, 1)
                    ps = psum[2 + u]
                    v.wait_ge(S("c1_p"), done(i, u))
                    v.scalar_tensor_tensor(hn[:, u, :], turn(AGG[:, n, :]), rden[:, n], ps[0:R, 0:D], ALU.mult, ALU.add)
                    xr = turn(X[:, n, :])
                    v.tensor_tensor(xr, xr, ps[0:R, D:2 * D], ALU.add).then_inc(S("c1_d"), 1)
                v.drain()
                v.tensor_tensor(hn[:, :, :], hn[:, :, :], has[:, tiles5].unsqueeze(2).broadcast_to([R, U5, D]), ALU.mult)
                v.tensor_tensor(agg5, xn5, hasn[:, tiles5].unsqueeze(2).broadcast_to([R, U5, D]), ALU.mult)
                v.drain()
                v.tensor_tensor(hn[:, :, :], hn[:, :, :], agg5, ALU.add)
                v.drain()
                v.scalar_tensor_tensor(hn[:, :, :], hn[:, :, :], 0.0, xn5, ALU.max, ALU.add)
                v.drain()
                v.tensor_tensor(x5, x5, hn[:, :, :], ALU.add)
                v.drain()

        g2b, b2b, gammab, betab = vec["g2b"], vec["b2b"], vec["gammab"], vec["betab"]
        boutb, gamma1b, beta1b, attb = g2b, b2b, gammab, vec["attb"]
        gb0, gb1 = vec["gb0"], vec["gb1"]

        def halves(w):
            return w.rearrange("(h p) n -> p h n", p=128)

        def row(w):
            return w.rearrange("(a n) -> a n", a=1)

        hamilton = (("r", "i", "j", "k"), ("-i", "r", "k", "-j"), ("-j", "-k", "r", "i"), ("-k", "j", "-i", "r"))
        L0_DENSE = [(wkv[:, :, 0:D], halves(A["L0_mix_Wk"])), (wkv[:, :, D:2 * D], halves(A["L0_mix_Wv"])),
                    (wq, halves(A["L0_mix_Wq"])), (wm, halves(A["L0_mix_Wm"])), (w1, halves(A["L0_mix_W1"])),
                    (w2, halves(A["L0_mix_W2"]))]
        for a_ in range(4):
            for b_ in range(4):
                q_ = "rijk".index(hamilton[a_][b_][-1])
                L0_DENSE.append((ham[(a_ % 2) * 64:(a_ % 2) * 64 + 64, a_ // 2, b_ * 64:(b_ + 1) * 64],
                                 A["L0_gnn_weight"][:, q_ * 64:(q_ + 1) * 64]))
        W0 = len(L0_DENSE)
        L1_DENSE = [(wfx[:, :, 0:D], halves(A["L1_gnn_W_func_T"])), (wsm[:, :, 0:D], halves(A["L1_gnn_W_self_T"])),
                    (wkv1, halves(A["L1_mix_Wqkv_T"])[:, :, HID:3 * HID]), (wout, halves(A["L1_mix_Wout_T"])),
                    (wqo, halves(A["L1_mix_Wqkv"][0:HID, :]))]
        VECTORS = [(g2b, "L0_mix_g2"), (b2b, "L0_mix_b2"), (gammab, "L0_gnn_gamma"), (betab, "L0_gnn_beta"),
                   (gb0, "L0_ffn_gate_b"), (gb1, "L1_ffn_gate_b")]
        VECTORS1 = [(boutb, "L1_mix_bout"), (gamma1b, "L1_ffn_gamma"), (beta1b, "L1_ffn_beta")]
        NVEC = len(VECTORS) + 7
        ew = XN[:, 0:2, :].rearrange("p a b -> p (a b)")[:, 0:EC]
        SCA, SCM = NT // U5, 3 * m0.turns
        SCB = SC - SCA - SCM
        SC0 = 6
        CLEARS = sum(-(-T * 3 // 512) for T in (T0, T1))

        @block.sync
        def _(s):
            for dst, name in ((srcI[:, :], "src"), (dstI[:, :], "dst"), (ew, "edge_weight")):
                s.dma_start(dst, A[name].rearrange("(p c) -> p c", p=R)).then_inc(edges_in, 16)
            s.dma_start(X[:, :, :], tiles(A["x"])).then_inc(x_in, 16)
            for dst, src_ap in L0_DENSE:
                s.dma_start(dst, src_ap).then_inc(w0_raw, 16)
            s.wait_ge(consts, 1)
            for table, T in ((slot0, T0), (slot1, T1)):
                flat = table.rearrange("(p t) r -> p (t r)", p=128)
                for k in range(0, T * 3, 512):
                    w = min(512, T * 3 - k)
                    s.dma_start(flat[:, k:k + w], zeros[:, 0:w]).then_inc(S("slots_clear"), 16)
            for dst, name in VECTORS:
                s.dma_start(dst[:, :], row(A[name]).broadcast_to([128, dst.shape[1]])).then_inc(vec_in, 16)
            s.dma_start(attb[:, :], A["L1_gnn_W_att"].broadcast_to([128, 2 * D + EDIM])).then_inc(vec_in, 16)
            for dst, name in ((g1c, "L0_mix_g1"), (b1c, "L0_mix_b1")):
                for h in range(2):
                    s.dma_start(dst[:, h:h + 1], A[name][h * 128:(h + 1) * 128].rearrange("(p a) -> p a", a=1)
                                ).then_inc(vec_in, 16)
            s.dma_start(gw0[:, :, :], halves(A["L0_ffn_gate_w"])).then_inc(vec_in, 16)
            s.dma_start(gw1[:, :, :], halves(A["L1_ffn_gate_w"])).then_inc(vec_in, 16)
            s_a0(s)
            barrier(s, "sp")
            s_slots(s, (SC, SC), slot0, T0, 1)
            barrier(s, "sp")
            for dst, src_ap in L1_DENSE:
                s.dma_start(dst, src_ap).then_inc(S("w1_in"), 16)
            s_te(s)
            barrier(s, "sp")
            barrier(s, "sp")
            for dst, name in VECTORS1:
                s.dma_start(dst[:, :], row(A[name]).broadcast_to([128, dst.shape[1]])).then_inc(S("L1_vectors_in"), 16)
            s_gate(s, "g0", hrow0)
            barrier(s, "sp")
            s_expert(s, m0, A["L0_ffn_w1"], A["L0_ffn_b1"], A["L0_ffn_w2"], A["L0_ffn_b2"])
            barrier(s, "sp")
            barrier(s, "sp")
            s_a1(s)
            s_slots(s, (2 * SC, 2 * SC), slot1, T1, 2)
            barrier(s, "sp")
            barrier(s, "sp")
            barrier(s, "sp")
            s_gate(s, "g1", hrow1)
            barrier(s, "sp")
            s_expert(s, m1, A["L1_ffn_w1"], A["L1_ffn_b1"], A["L1_ffn_w2"], A["L1_ffn_b2"])
            barrier(s, "sp")
            s_final(s)

        @block.gpsimd
        def _(p):
            p.iota(iotaI[:, :], [[1, MAXG]], base=0, channel_multiplier=0)
            p.iota(nodeI[:, :], [[1, NT]], base=0, channel_multiplier=NT)
            p.memset(ident[:, :], 0.0)
            p.memset(ones[:, :], 1.0)
            p.memset(tri[:, :], 1.0)
            p.memset(zeros[:, :], 0.0)
            p.memset(hm32[:, :], 0.0)
            p.memset(hm64[:, :], 0.0)
            p.memset(eps_t[:, :], EPS)
            p.memset(AGG[:, :, :], 0.0)
            p.drain()
            p.affine_select(out=ident[:, :], in_=ident[:, :], compare_op=ALU.not_equal, fill=1.0, base=0,
                            pattern=[[-1, 128]], channel_multiplier=1)
            p.affine_select(out=tri[:, :], in_=tri[:, :], compare_op=ALU.is_gt, fill=0.0, base=0,
                            pattern=[[1, 128]], channel_multiplier=-1)
            p.drain().then_inc(consts, 1)
            p.wait_ge(S("placed"), 1)
            p.wait_ge(S("slots_clear"), 16 * CLEARS)
            for h in range(2):
                p_scatter(p, h, 0, h, slot0, first=True)
            with p.Fori(1, SC0) as i:
                for h in range(2):
                    p_scatter(p, h, i, i * 2 + h, slot0)
            barrier(p, "pool")
            with p.Fori(SC0, SC) as i:
                for h in range(2):
                    p_scatter(p, h, i, i * 2 + h, slot0)
            barrier(p, "pool")
            with p.Fori(0, T0 // EU) as i:
                p_gather(p, 0, i, GT0, EU, tab0, g0)
            barrier(p, "pool")
            for first, end in ((0, 3), (3, SCB)):
                with p.Fori(first, end) as i:
                    for h in range(2):
                        p_scatter(p, h, SC + i, i * 2 + h, slot1)
                barrier(p, "pool")
            def scatter_three(i):
                for n in range(3):
                    for h in range(2):
                        p_scatter(p, h, SC + SCB + i * 3 + n, (SCB + i * 3 + n) * 2 + h, slot1)

            p_expert(p, m0, hrow0, also=scatter_three)
            barrier(p, "pool")
            p_back(p, "m0", 1, ys0)
            barrier(p, "pool")
            p_a1(p)
            barrier(p, "pool")
            with p.Fori(0, T1 // EU1) as i:
                p_gather(p, G0, i, GT1, EU1, tab1, g1)
            p.tensor_tensor(X[:, :, :], X[:, :, :], bc(boutb[0:R, :]), ALU.add)
            barrier(p, "pool")
            p_c1(p)
            barrier(p, "pool")
            p_keep(p, "g1")
            barrier(p, "pool")
            p_expert(p, m1, hrow1)
            barrier(p, "pool")
            p_back(p, "m1", 2, ys1)

        @block.vector
        def _(v):
            v.wait_ge(consts, 1)
            v.tensor_copy(iota[:, :], iotaI[:, :])
            v.tensor_copy(node[:, :], nodeI[:, :])
            v.tensor_scalar(nident[:, :], ident[:, :], -1.0, None, ALU.mult)
            for k in range(4):
                v.memset(hm32[k * 32:(k + 1) * 32, k * 32:(k + 1) * 32], 1.0)
            for k in range(2):
                v.memset(hm64[k * 64:(k + 1) * 64, k * 64:(k + 1) * 64], 1.0)
            v.drain()
            v.wait_ge(edges_in, 48)
            v_sort_start(v)
            v_keys(v, srcI, dstI)
            v.tensor_copy(rec[:, :, 2], ew)
            with v.Fori(0, NT // 2) as b:
                v_count(v, EC, b * 2, b * 2 + 1)
            v_count(v, EC, NT - 1)
            v_totals(v, "s0", NT, GT0)
            with v.Fori(0, NT // 2) as b:
                v_place(v, EC, G0, b * 2, b * 2 + 1)
            v_place(v, EC, G0, NT - 1)
            v_edges_placed(v, G0, T0, gblk0)
            v.drain().then_inc(S("placed"), 1)
            v.wait_ge(w0_raw, 16 * W0)
            for a_ in range(4):
                for b_ in range(4):
                    if hamilton[a_][b_][0] == "-":
                        h_ = ham[(a_ % 2) * 64:(a_ % 2) * 64 + 64, a_ // 2, b_ * 64:(b_ + 1) * 64]
                        v.tensor_scalar(h_, h_, -1.0, None, ALU.mult)
            v.drain().then_inc(consts, 2)
            v.wait_ge(x_in, 16)
            v_a0(v)
            barrier(v, "dve")
            v.wait_ge(vec_in, 16 * NVEC)
            v_kv(v)
            v.drain().then_inc(S("b0_kvbd"), 1)
            v_b0(v)
            barrier(v, "dve")
            seed(v, "e0_acc", n=GU0)
            seed(v, "te_read", n=2)

            def e0_turn(i):
                blks = load_blocks(gblk0, i * GU0, GU0)
                for w in range(GU0 + 2):
                    if w < GU0:
                        for k in range(GT0):
                            v_sel0(v, i, w * GT0 + k)
                    if w >= 2:
                        v_acc0(v, i, w - 2, blks[w - 2])

            HT = NT // 2
            assert T0 // EU >= 2 * HT + 2 and 2 * TC * (2 * HT + 1) == EC
            v_sort_start(v)
            v_keys(v, dstI, srcI)
            with v.Fori(0, HT) as i:
                e0_turn(i)
                v_te(v, i)
                v_count(v, EC, i * 2, i * 2 + 1)
            e0_turn(HT)
            v_te(v, HT)
            v_count(v, EC, NT - 1)
            v_totals(v, "s1", NT, GT1)
            with v.Fori(0, HT) as i:
                e0_turn(i + (HT + 1))
                v_te(v, i + (HT + 1))
                v_place(v, EC, G1, i * 2, i * 2 + 1)
            e0_turn(2 * HT + 1)
            v_place(v, EC, G1, NT - 1)
            v_edges_placed(v, G1, T1, gblk1)
            with v.Fori(2 * HT + 2, T0 // EU) as i:
                e0_turn(i)
            v.drain()
            barrier(v, "dve")
            v_bn(v)
            barrier(v, "dve")
            v_gate(v, "g0", gb0, X0, False)
            v.drain()
            v_choose(v, "g0", X0, K0)
            v_route(v, "r0", K0, X0, M0)
            barrier(v, "dve")
            v.wait_ge(S("w1_in"), 16 * len(L1_DENSE))
            v.wait_ge(S("L1_vectors_in"), 16 * len(VECTORS1))
            v_w1(v)
            v_expert(v, m0)
            barrier(v, "dve")
            v_back0(v)
            barrier(v, "dve")
            v_a1(v)
            barrier(v, "dve")
            v_e1(v)
            barrier(v, "dve")
            v_c1(v)
            barrier(v, "dve")
            v_gate(v, "g1", gb1, X1, True)
            v.drain()
            v_choose(v, "g1", X1, K1)
            v_route(v, "r1", K1, X1, M1)
            barrier(v, "dve")
            v_expert(v, m1)
            barrier(v, "dve")
            v_back1(v)

        @block.scalar
        def _(a):
            a.wait_ge(consts, 3)
            a_a0(a)
            barrier(a, "act")
            a_b0(a)
            barrier(a, "act")
            with a.Fori(0, T0 // EU) as i:
                for w in range(GU0):
                    a_rows(a, "e0", i, w)
            barrier(a, "act")
            a_bn(a)
            barrier(a, "act")
            a_gate(a, "g0")
            a_choose(a, "g0", X0, K0)
            barrier(a, "act")
            a_expert(a, m0, ys0)
            barrier(a, "act")
            barrier(a, "act")
            a_a1(a)
            barrier(a, "act")
            a_e1(a)
            barrier(a, "act")
            barrier(a, "act")
            a_gate(a, "g1")
            a_choose(a, "g1", X1, K1)
            barrier(a, "act")
            a_expert(a, m1, ys1)
            barrier(a, "act")
            with a.Fori(0, NT // U5) as i:
                a_sqrt(a, BEFORE["fin"], i)

        @block.tensor
        def _(t):
            t.wait_ge(consts, 1)
            t_count(t, "s0", NT)
            t_a0(t)
            barrier(t, "pe")
            t.wait_ge(S("b0_kvbd"), 1)
            t_b0(t)
            barrier(t, "pe")
            seed(t, "e0_sum", n=EU)
            with t.Fori(0, NT // 2 + 1) as i:
                for w in range(GU0):
                    t_e0(t, i, w)
            t_count(t, "s1", NT)
            with t.Fori(NT // 2 + 1, T0 // EU) as i:
                for w in range(GU0):
                    t_e0(t, i, w)
            barrier(t, "pe")
            t_bn(t, AGG, 0, "bn_agg", "bn_sum")
            t_bn(t, bnm, 1, "bn_sq", "bn_ssq")
            barrier(t, "pe")
            seed(t, "s_used")
            t_gate(t, "g0", gw0, X0)
            t_route(t, "r0", K0, X0, M0)
            barrier(t, "pe")
            t_expert(t, m0)
            barrier(t, "pe")
            barrier(t, "pe")
            t_a1(t)
            barrier(t, "pe")
            t_e1(t)
            barrier(t, "pe")
            t_c1(t)
            barrier(t, "pe")
            t_gate(t, "g1", gw1, X1)
            t_route(t, "r1", K1, X1, M1)
            barrier(t, "pe")
            t_expert(t, m1)
            barrier(t, "pe")


_INS = ("x", "src", "dst", "edge_attr_64", "edge_weight", "L0_gnn_weight", "L0_gnn_gamma", "L0_gnn_beta",
        "L0_mix_Wq", "L0_mix_Wk", "L0_mix_Wv", "L0_mix_Wm", "L0_mix_W1", "L0_mix_W2", "L0_mix_g1", "L0_mix_b1",
        "L0_mix_g2", "L0_mix_b2", "L0_ffn_gate_w", "L0_ffn_gate_b", "L0_ffn_w1", "L0_ffn_b1", "L0_ffn_w2",
        "L0_ffn_b2", "L1_gnn_W_self", "L1_gnn_W_func", "L1_gnn_W_att", "L1_mix_Wqkv", "L1_mix_Wout",
        "L1_mix_bout", "L1_ffn_gate_w", "L1_ffn_gate_b", "L1_ffn_w1", "L1_ffn_b1", "L1_ffn_w2", "L1_ffn_b2",
        "L1_ffn_gamma", "L1_ffn_beta")
_TURNED = ("L1_gnn_W_func", "L1_gnn_W_self", "L1_mix_Wqkv", "L1_mix_Wout")


def kernel(**inputs):
    import numpy as _np
    import concourse.bacc as _bacc
    from concourse import mybir as _mybir
    from concourse.bass_utils import run_bass_kernel_spmd as _run

    laid = {n: _np.ascontiguousarray(inputs[n]) for n in _INS}
    for n in _TURNED:
        laid[n + "_T"] = _np.ascontiguousarray(_np.transpose(laid[n]))
    for n in ("L1_gnn_W_func", "L1_gnn_W_self", "L1_mix_Wout"):
        del laid[n]
    nc = _bacc.Bacc("TRN2", target_bir_lowering=False, num_devices=1)
    arrays, A = {}, {}
    for n, a in laid.items():
        arrays["in_" + n] = a
        A[n] = nc.dram_tensor("in_" + n, a.shape, _mybir.dt.from_np(a.dtype), kind="ExternalInput").ap()
    out = nc.dram_tensor("out", (N, D), F32, kind="ExternalOutput").ap()
    gps_kernel(nc, A, out)
    r = _run(nc, [arrays], core_ids=[0])
    return r.results[0]["out"]
```
